# Optimizing a Trainium2 kernel written in Bass

```python
import numpy as np
import jax
import jax.numpy as jnp

def _softmax(x, axis=-1):
    return jax.nn.softmax(x, axis=axis)

def _gelu(x):
    return jax.nn.gelu(x, approximate=True)

def _silu(x):
    return jax.nn.silu(x)

def _sigmoid(x):
    return jax.nn.sigmoid(x)

def _layernorm(x, axis=-1, eps=1e-05):
    m = jnp.mean(x, axis=axis, keepdims=True)
    v = jnp.var(x, axis=axis, keepdims=True)
    return (x - m) / jnp.sqrt(v + eps)

def _scatter_add(tgt, idx, src, axis=0):
    return tgt.at[idx].add(src)

def _segment_sum(src, seg, n):
    return jax.ops.segment_sum(src, seg, n)
kernel_name = 'mk_perceiver_d4_seqx_r4_d57b8e'

def setup_inputs(seed: int=0):
    np.random.seed(seed)
    _w = jnp.asarray

    def _rec_inputs():
        import jax
        import jax.numpy as jnp
        _rk = jax.random.key(seed)
        x = 7.22e-05 + 1 * jax.random.normal(jax.random.fold_in(_rk, 1), (1, 128, 256), jnp.float32)
        _lenS = 128 - jax.random.randint(jax.random.fold_in(_rk, 7), (1,), 0, max(1, 128 // 4) + 1, jnp.int32)
        _lenS2 = 12544 - jax.random.randint(jax.random.fold_in(_rk, 8), (1,), 0, max(1, 12544 // 4) + 1, jnp.int32)
        _ctx_1024P = jax.random.normal(jax.random.fold_in(_rk, 11), (1, 16, 256), jnp.float32)
        _ctx_1024c = jax.random.dirichlet(jax.random.fold_in(_rk, 511), 0.3 * jnp.ones((16,), jnp.float32), (1, 12544))
        _ctx_1024t = jnp.einsum('bsk,bkd->bsd', _ctx_1024c, _ctx_1024P)
        _ctx_1024t = _ctx_1024t * jax.lax.rsqrt(jnp.mean(jnp.square(_ctx_1024t)) + 1e-12) * 0.953939
        ctx_1024 = 4.13588e-05 + 0.999923 * (_ctx_1024t + 0.3 * jax.random.normal(jax.random.fold_in(_rk, 611), (1, 12544, 256), jnp.float32))
        fside_SxS2_0 = 0.000675642 + 1.00031 * jax.random.normal(jax.random.fold_in(_rk, 13), (128, 12544), jnp.float32)
        fside_BxS2_0 = -0.00205293 + 0.99739 * jax.random.normal(jax.random.fold_in(_rk, 14), (1, 12544), jnp.float32)
        _validS = jnp.arange(128)[None, :] < _lenS[:, None]
        _validS2 = jnp.arange(12544)[None, :] < _lenS2[:, None]
        _causal = jnp.tril(jnp.ones((128, 128), dtype=bool))
        mask_BxS2_ik0 = jnp.where(jnp.broadcast_to(_validS2[:, :], (1, 12544)), 0, 1).astype(jnp.int32)
        mask_Bx1x1xS2_fk0 = jnp.where(jnp.broadcast_to(_validS2[:, None, None, :], (1, 1, 1, 12544)), 0.0, 1.0).astype(jnp.float32)
        return (x, ctx_1024, fside_SxS2_0, fside_BxS2_0, mask_BxS2_ik0, mask_Bx1x1xS2_fk0)
    x, ctx_1024, fside_SxS2_0, fside_BxS2_0, mask_BxS2_ik0, mask_Bx1x1xS2_fk0 = _rec_inputs()

    def _L0_xattn_setup():
        import jax, jax.numpy as jnp
        import numpy as np
        B, LQ, LK, D = (4, 512, 512, 256)
        H = 16
        HD = D // H

        def _split_heads(x):
            b, l, _ = x.shape
            return x.reshape(b, l, H, HD).transpose(0, 2, 1, 3)
        key = jax.random.key(seed)
        ks = jax.random.split(key, 10)
        s = 0.02
        return {'hidden_states': jax.random.normal(ks[0], (B, LQ, D), jnp.float32), 'context': jax.random.normal(ks[1], (B, LK, D), jnp.float32), 'attention_mask': jax.random.randint(ks[2], (B, LK), 0, 2, jnp.int32), 'q_w': jax.random.normal(ks[3], (D, D), jnp.float32) * s, 'q_b': jnp.zeros((D,), jnp.float32), 'k_w': jax.random.normal(ks[4], (D, D), jnp.float32) * s, 'k_b': jnp.zeros((D,), jnp.float32), 'v_w': jax.random.normal(ks[5], (D, D), jnp.float32) * s, 'v_b': jnp.zeros((D,), jnp.float32)}
    _L0_xattn_all = _L0_xattn_setup()
    _L0_xattn_in = {k: v for k, v in _L0_xattn_all.items() if k in ('q_w', 'q_b', 'k_w', 'k_b', 'v_w', 'v_b')}
    del _L0_xattn_all

    def _L0_attn_setup():
        import jax, jax.numpy as jnp
        import numpy as np
        import math
        E = 256
        B, T = (8, 512)
        key = jax.random.key(seed)
        ks = jax.random.split(key, 7)
        s = 1.0 / math.sqrt(E)
        return {'X': jax.random.normal(ks[0], (B, T, E), dtype=jnp.float32), 'Wq': jax.random.uniform(ks[1], (E, E), jnp.float32, -s, s), 'bq': jax.random.uniform(ks[2], (E,), jnp.float32, -s, s), 'Wk': jax.random.uniform(ks[3], (E, E), jnp.float32, -s, s), 'bk': jax.random.uniform(ks[4], (E,), jnp.float32, -s, s), 'Wv': jax.random.uniform(ks[5], (E, E), jnp.float32, -s, s), 'bv': jax.random.uniform(ks[6], (E,), jnp.float32, -s, s)}
    _L0_attn_all = _L0_attn_setup()
    _L0_attn_in = {k: v for k, v in _L0_attn_all.items() if k in ('Wq', 'bq', 'Wk', 'bk', 'Wv', 'bv')}
    del _L0_attn_all

    def _L0_ffn_setup():
        import jax, jax.numpy as jnp
        import numpy as np
        K = 64
        key = jax.random.key(seed)
        ks = jax.random.split(key, 9)
        B, S, D, O, E = (8, 512, 256, 256, 16)

        def xavier(k_, shape):
            fan_in, fan_out = (shape[-2], shape[-1])
            lim = (6.0 / (fan_in + fan_out)) ** 0.5
            return jax.random.uniform(k_, shape, jnp.float32, -lim, lim)
        return {'x': jax.random.normal(ks[0], (B, S, D), jnp.float32), 'Wg': xavier(ks[1], (D, E)), 'bg': jnp.zeros((E,), jnp.float32), 'w1': xavier(ks[2], (E, D, O)), 'b1': xavier(ks[3], (E, 1)), 'w2': xavier(ks[4], (E, O, O)), 'b2': xavier(ks[5], (E, 1)), 'w3': xavier(ks[6], (E, O, O)), 'b3': xavier(ks[7], (E, 1))}
    _L0_ffn_all = _L0_ffn_setup()
    _L0_ffn_in = {k: v for k, v in _L0_ffn_all.items() if k in ('Wg', 'bg', 'w1', 'b1', 'w2', 'b2', 'w3', 'b3')}
    del _L0_ffn_all

    def _L1_xattn_setup():
        import jax, jax.numpy as jnp
        import numpy as np
        D = 256
        NH = 16
        DK = D // NH
        B, L, LP = (2, 512, 512)
        key = jax.random.key(seed)
        ks = jax.random.split(key, 14)
        s = 1.0 / np.sqrt(D)
        return {'K_in': jax.random.normal(ks[0], (B, L, D), jnp.float32), 'V_in': jax.random.normal(ks[1], (B, L, D), jnp.float32), 'Q_in': jax.random.normal(ks[2], (B, LP, D), jnp.float32), 'mask_attn': jax.random.normal(ks[3], (LP, L), jnp.float32), 'mask_pad': jax.random.normal(ks[4], (B, L), jnp.float32), 'Wk': jax.random.normal(ks[5], (D, NH * DK), jnp.float32) * s, 'bk': jax.random.normal(ks[6], (NH * DK,), jnp.float32) * s, 'Wv': jax.random.normal(ks[7], (D, NH * DK), jnp.float32) * s, 'bv': jax.random.normal(ks[8], (NH * DK,), jnp.float32) * s, 'Wq': jax.random.normal(ks[9], (D, NH * DK), jnp.float32) * s, 'bq': jax.random.normal(ks[10], (NH * DK,), jnp.float32) * s, 'Wo': jax.random.normal(ks[11], (NH * DK, D), jnp.float32) * s, 'bo': jax.random.normal(ks[12], (D,), jnp.float32) * s}
    _L1_xattn_all = _L1_xattn_setup()
    _L1_xattn_in = {k: v for k, v in _L1_xattn_all.items() if k in ('Wk', 'bk', 'Wv', 'bv', 'Wq', 'bq', 'Wo', 'bo')}
    del _L1_xattn_all

    def _L1_attn_setup():
        import jax, jax.numpy as jnp
        import numpy as np
        CHUNK = 32
        H = 4

        def silu(x):
            return x * jax.nn.sigmoid(x)

        def l2norm(x):
            return x * jax.lax.rsqrt(jnp.sum(x * x, -1, keepdims=True) + 1e-06)

        def dwconv_causal(x_cl, w):
            k = w.shape[1]
            xp = jnp.pad(x_cl, ((0, 0), (0, 0), (k - 1, 0)))
            return jax.lax.conv_general_dilated(xp, w[:, None, :], (1,), 'VALID', dimension_numbers=('NCH', 'OIH', 'NCH'), feature_group_count=x_cl.shape[1])

        def short_conv_silu(x_bld, w):
            y = dwconv_causal(jnp.swapaxes(x_bld, 1, 2), w)
            return silu(jnp.swapaxes(y, 1, 2))

        def delta_rule_chunkwise(q, k, v, beta, chunk=CHUNK):
            b, h, L, dk = q.shape
            dv = v.shape[-1]
            pad = -L % chunk
            if pad:
                q, k, v = (jnp.pad(t, ((0, 0), (0, 0), (0, pad), (0, 0))) for t in (q, k, v))
                beta = jnp.pad(beta, ((0, 0), (0, 0), (0, pad)))
            n = (L + pad) // chunk
            q = l2norm(q)
            k = l2norm(k)
            v = v * beta[..., None]
            kb = k * beta[..., None]
            ch = lambda x: x.reshape(b, h, n, chunk, x.shape[-1])
            qc, kc, vc, kbc = map(ch, (q, k, v, kb))
            idx = jnp.arange(chunk)
            strict_lower = (idx[:, None] > idx[None, :]).astype(q.dtype)
            incl_lower = (idx[:, None] >= idx[None, :]).astype(q.dtype)
            attn = -jnp.einsum('bhncd,bhned->bhnce', kbc, kc) * strict_lower
            for i in range(1, chunk):
                upd = jnp.einsum('...j,...ji->...i', attn[..., i, :], attn[..., :, :i])
                attn = attn.at[..., i, :i].add(upd)
            attn = attn + jnp.eye(chunk, dtype=q.dtype)
            u = attn @ vc
            w = attn @ kbc
            xs = tuple((jnp.moveaxis(t, 2, 0) for t in (qc, kc, u, w)))
            S0 = jnp.zeros((b, h, dk, dv), q.dtype)

            def step(S, x):
                qi, ki, ui, wi = x
                a_loc = jnp.einsum('bhcd,bhed->bhce', qi, ki) * incl_lower
                ui = ui - wi @ S
                oi = qi @ S + a_loc @ ui
                S = S + jnp.einsum('bhcd,bhcv->bhdv', ki, ui)
                return (S, oi)
            S, o = jax.lax.scan(step, S0, xs)
            o = jnp.moveaxis(o, 0, 2).reshape(b, h, n * chunk, dv)[:, :, :L]
            return (o, S)

        def multiscale_conv(v, ms_w3, ms_w15, ms_w31, kernel_mix_w, channel_mixer_w):
            b, l, h, d = v.shape
            x = jnp.swapaxes(v.reshape(b, l, h * d), 1, 2)
            outs = [dwconv_causal(x, w) for w in (ms_w3, ms_w15, ms_w31)]
            y = jnp.concatenate(outs, axis=1)
            y = y.reshape(b, h, 3 * d, l).transpose(0, 3, 1, 2)
            y = y @ kernel_mix_w
            y = (y.reshape(b, l, h * d) @ channel_mixer_w).reshape(b, l, h, d)
            return y

        def _forward(hidden_states, Wq, Wk, Wv, Wb, conv_q_w, conv_k_w, conv_v_w, ms_w3, ms_w15, ms_w31, kernel_mix_w, channel_mixer_w, fusion_w1, fusion_b1, fusion_w2, fusion_b2, o_norm_w, Wo):
            b, L, D = hidden_states.shape
            h = H
            dk = Wq.shape[1] // h
            dv = Wv.shape[1] // h
            q = short_conv_silu(hidden_states @ Wq, conv_q_w).reshape(b, L, h, dk)
            k = short_conv_silu(hidden_states @ Wk, conv_k_w).reshape(b, L, h, dk)
            v = short_conv_silu(hidden_states @ Wv, conv_v_w).reshape(b, L, h, dv)
            v_direct = v
            beta = jax.nn.sigmoid(hidden_states @ Wb)
            tr = lambda x: jnp.swapaxes(x, 1, 2)
            delta_out, _S = delta_rule_chunkwise(tr(q), tr(k), tr(v), tr(beta))
            delta_out = jnp.swapaxes(delta_out, 1, 2)
            ms_out = multiscale_conv(v_direct, ms_w3, ms_w15, ms_w31, kernel_mix_w, channel_mixer_w)
            bn = lambda x: jnp.mean(jnp.abs(x), -1)
            gate_features = jnp.concatenate([hidden_states, bn(ms_out), bn(delta_out), bn(v_direct)], -1)
            hdn = jax.nn.gelu(gate_features @ fusion_w1 + fusion_b1, approximate=False)
            logits = (hdn @ fusion_w2 + fusion_b2).reshape(b, L, h, 3)
            wts = jax.nn.softmax(logits, -1)
            o = wts[..., 0:1] * ms_out + wts[..., 1:2] * delta_out + wts[..., 2:3] * v_direct
            o = o * jax.lax.rsqrt(jnp.mean(o * o, -1, keepdims=True) + 1e-05) * o_norm_w
            return o.reshape(b, L, h * dv) @ Wo
        B, L, D = (4, 512, 256)
        h, d = (H, D // H)
        key = jax.random.key(seed)
        ks = jax.random.split(key, 20)
        nrm = lambda k, shp, s: jax.random.normal(k, shp, dtype=jnp.float32) * s
        inp = {'hidden_states': nrm(ks[0], (B, L, D), 1.0), 'Wq': nrm(ks[1], (D, D), D ** (-0.5)), 'Wk': nrm(ks[2], (D, D), D ** (-0.5)), 'Wv': nrm(ks[3], (D, D), D ** (-0.5)), 'Wb': nrm(ks[4], (D, h), D ** (-0.5)), 'conv_q_w': nrm(ks[5], (D, 4), 0.3), 'conv_k_w': nrm(ks[6], (D, 4), 0.3), 'conv_v_w': nrm(ks[7], (D, 4), 0.3), 'ms_w3': nrm(ks[8], (D, 3), 0.02), 'ms_w15': nrm(ks[9], (D, 15), 0.02), 'ms_w31': nrm(ks[10], (D, 31), 0.02), 'kernel_mix_w': nrm(ks[11], (3 * d, d), (3 * d) ** (-0.5)), 'channel_mixer_w': nrm(ks[12], (D, D), D ** (-0.5)), 'fusion_w1': nrm(ks[13], (D + 3 * h, 2 * D), (D + 3 * h) ** (-0.5)), 'fusion_b1': jnp.zeros((2 * D,), jnp.float32), 'fusion_w2': nrm(ks[14], (2 * D, 3 * h), (2 * D) ** (-0.5)), 'fusion_b2': jnp.concatenate([jnp.zeros((2 * h,), jnp.float32), jnp.ones((h,), jnp.float32)]), 'o_norm_w': jnp.ones((d,), jnp.float32), 'Wo': nrm(ks[15], (D, D), D ** (-0.5))}
        return inp
    _L1_attn_all = _L1_attn_setup()
    _L1_attn_in = {k: v for k, v in _L1_attn_all.items() if k in ('Wq', 'Wk', 'Wv', 'Wb', 'conv_q_w', 'conv_k_w', 'conv_v_w', 'ms_w3', 'ms_w15', 'ms_w31', 'kernel_mix_w', 'channel_mixer_w', 'fusion_w1', 'fusion_b1', 'fusion_w2', 'fusion_b2', 'o_norm_w', 'Wo')}
    del _L1_attn_all

    def _L1_ffn_setup():
        import jax, jax.numpy as jnp
        import numpy as np
        DIM = 256
        E = 8
        K = 2
        EPS = 1e-05

        def _ln(x, g, b):
            mu = jnp.mean(x, axis=-1, keepdims=True)
            var = jnp.mean(jnp.square(x - mu), axis=-1, keepdims=True)
            return (x - mu) * jax.lax.rsqrt(var + EPS) * g + b
        key = jax.random.key(seed)
        ks = jax.random.split(key, 8)
        H = 2 * DIM
        s_in = 1.0 / np.sqrt(DIM)
        s_h = 1.0 / np.sqrt(H)
        return {'x': jax.random.normal(ks[0], (2, 512, DIM), dtype=jnp.float32), 'gate_w': jax.random.uniform(ks[1], (DIM, E), minval=-s_in, maxval=s_in, dtype=jnp.float32), 'w1': jax.random.uniform(ks[2], (E, DIM, H), minval=-s_in, maxval=s_in, dtype=jnp.float32), 'b1': jax.random.uniform(ks[3], (E, H), minval=-s_in, maxval=s_in, dtype=jnp.float32), 'ln1_g': jnp.ones((E, H), dtype=jnp.float32), 'ln1_b': jnp.zeros((E, H), dtype=jnp.float32), 'w2': jax.random.uniform(ks[4], (E, H, DIM), minval=-s_h, maxval=s_h, dtype=jnp.float32), 'b2': jax.random.uniform(ks[5], (E, DIM), minval=-s_h, maxval=s_h, dtype=jnp.float32), 'ln_g': jnp.ones((DIM,), dtype=jnp.float32), 'ln_b': jnp.zeros((DIM,), dtype=jnp.float32)}
    _L1_ffn_all = _L1_ffn_setup()
    _L1_ffn_in = {k: v for k, v in _L1_ffn_all.items() if k in ('gate_w', 'w1', 'b1', 'ln1_g', 'ln1_b', 'w2', 'b2', 'ln_g', 'ln_b')}
    del _L1_ffn_all

    def _L2_xattn_setup():
        import jax, jax.numpy as jnp
        import numpy as np
        EMBED_DIM = 256
        NUM_HEADS = 16
        HEAD_DIM = EMBED_DIM // NUM_HEADS

        def _split_heads(x):
            B, S, _ = x.shape
            return x.reshape(B, S, NUM_HEADS, HEAD_DIM).transpose(0, 2, 1, 3)
        key = jax.random.key(seed)
        ks = jax.random.split(key, 11)
        B, S, D = (2, 512, EMBED_DIM)
        scale = 1.0 / np.sqrt(D)
        return {'x_q': jax.random.normal(ks[0], (B, S, D), jnp.float32), 'x_k': jax.random.normal(ks[1], (B, S, D), jnp.float32), 'x_v': jax.random.normal(ks[2], (B, S, D), jnp.float32), 'wq': jax.random.normal(ks[3], (D, D), jnp.float32) * scale, 'bq': jnp.zeros((D,), jnp.float32), 'wk': jax.random.normal(ks[4], (D, D), jnp.float32) * scale, 'bk': jnp.zeros((D,), jnp.float32), 'wv': jax.random.normal(ks[5], (D, D), jnp.float32) * scale, 'bv': jnp.zeros((D,), jnp.float32), 'wo': jax.random.normal(ks[6], (D, D), jnp.float32) * scale, 'bo': jnp.zeros((D,), jnp.float32)}
    _L2_xattn_all = _L2_xattn_setup()
    _L2_xattn_in = {k: v for k, v in _L2_xattn_all.items() if k in ('wq', 'bq', 'wk', 'bk', 'wv', 'bv', 'wo', 'bo')}
    del _L2_xattn_all

    def _L2_attn_setup():
        import jax, jax.numpy as jnp
        import numpy as np
        B, S, D_MODEL, D_K = (4, 512, 256, 1)
        D_QKV = D_MODEL * D_K
        MASK_NEG = -9000000000000000.0

        def _scaled_dot_product_attention(q, k, v):
            d_k = k.shape[-1]
            scores = jnp.einsum('bqd,bkd->bqk', q, k) / jnp.sqrt(jnp.float32(d_k))
            scores = jnp.triu(scores, k=0)
            scores = jnp.where(scores == 0, MASK_NEG, scores)
            attn = jax.nn.softmax(scores, axis=-1)
            return jnp.einsum('bqk,bkd->bqd', attn, v)
        key = jax.random.key(seed)
        kx, kw = jax.random.split(key)
        x = jax.random.normal(kx, (B, S, D_MODEL), dtype=jnp.float32)
        W = jax.random.normal(kw, (D_MODEL, 3 * D_QKV), dtype=jnp.float32) * (1.0 / np.sqrt(D_MODEL))
        return {'x': x, 'W': W}
    _L2_attn_all = _L2_attn_setup()
    _L2_attn_in = {k: v for k, v in _L2_attn_all.items() if k in ('W',)}
    del _L2_attn_all

    def _L2_ffn_setup():
        import jax, jax.numpy as jnp
        import numpy as np
        MANT_BITS = 8
        _PWL_X = jnp.linspace(-4.0, 4.0, 33, dtype=jnp.float32)
        _PWL_Y = 0.5 * _PWL_X * (1.0 + jax.lax.erf(_PWL_X / jnp.sqrt(jnp.float32(2.0))))

        def float2fix(x, mantissa_bits):
            s = jnp.float32(2.0 ** mantissa_bits)
            q = jnp.round(x * s) / s
            return x + jax.lax.stop_gradient(q - x)

        def pwlin_gelu_basic(x, mantissa_bits_in, mantissa_bits_out):
            xq = float2fix(x, mantissa_bits_in)
            y = jnp.interp(xq, _PWL_X, _PWL_Y)
            y = jnp.where(xq > 4.0, xq, jnp.where(xq < -4.0, jnp.float32(0.0), y))
            return float2fix(y, mantissa_bits_out)
        key = jax.random.key(seed)
        k_x, k_w1, k_b1, k_w2, k_b2 = jax.random.split(key, 5)
        dim, ff_dim = (256, 1024)
        B, S = (32, 128)
        sc1 = 1.0 / np.sqrt(dim)
        sc2 = 1.0 / np.sqrt(ff_dim)
        return {'x': jax.random.normal(k_x, (B, S, dim), dtype=jnp.float32), 'w1': jax.random.uniform(k_w1, (dim, ff_dim), jnp.float32, -sc1, sc1), 'b1': jax.random.uniform(k_b1, (ff_dim,), jnp.float32, -sc1, sc1), 'w2': jax.random.uniform(k_w2, (ff_dim, dim), jnp.float32, -sc2, sc2), 'b2': jax.random.uniform(k_b2, (dim,), jnp.float32, -sc2, sc2)}
    _L2_ffn_all = _L2_ffn_setup()
    _L2_ffn_in = {k: v for k, v in _L2_ffn_all.items() if k in ('w1', 'b1', 'w2', 'b2')}
    del _L2_ffn_all

    def _L3_xattn_setup():
        import jax, jax.numpy as jnp
        import numpy as np
        B, S, D, H = (2, 512, 256, 16)
        DH = D // H

        def _split_heads(x):
            b, s, _ = x.shape
            return x.reshape(b, s, H, DH).transpose(0, 2, 1, 3)
        key = jax.random.key(seed)
        ks = jax.random.split(key, 8)
        scale = 0.02
        return {'query': jax.random.normal(ks[0], (B, S, D), jnp.float32), 'key': jax.random.normal(ks[1], (B, S, D), jnp.float32), 'value': jax.random.normal(ks[2], (B, S, D), jnp.float32), 'mask': jax.random.randint(ks[3], (B, 1, 1, S), 0, 2).astype(jnp.float32), 'Wq': jax.random.normal(ks[4], (D, D), jnp.float32) * scale, 'bq': jnp.zeros((D,), jnp.float32), 'Wk': jax.random.normal(ks[5], (D, D), jnp.float32) * scale, 'bk': jnp.zeros((D,), jnp.float32), 'Wv': jax.random.normal(ks[6], (D, D), jnp.float32) * scale, 'bv': jnp.zeros((D,), jnp.float32), 'Wo': jax.random.normal(ks[7], (D, D), jnp.float32) * scale, 'bo': jnp.zeros((D,), jnp.float32)}
    _L3_xattn_all = _L3_xattn_setup()
    _L3_xattn_in = {k: v for k, v in _L3_xattn_all.items() if k in ('Wq', 'bq', 'Wk', 'bk', 'Wv', 'bv', 'Wo', 'bo')}
    del _L3_xattn_all

    def _L3_attn_setup():
        import jax, jax.numpy as jnp
        import numpy as np
        DIM = 256
        DIM_HEAD = 64
        HEADS = DIM // DIM_HEAD
        WINDOW = 32
        EPS = 1e-05

        def _rotate_half(x):
            x1, x2 = jnp.split(x, 2, axis=-1)
            return jnp.concatenate((-x2, x1), axis=-1)
        key = jax.random.key(seed)
        k0, k1, k2 = jax.random.split(key, 3)
        B, T = (2, 512)
        x = jax.random.normal(k0, (B, T, DIM), dtype=jnp.float32)
        ln_w = jnp.ones((DIM,), dtype=jnp.float32)
        ln_b = jnp.zeros((DIM,), dtype=jnp.float32)
        w_qkv = jax.random.normal(k1, (3 * DIM, DIM), dtype=jnp.float32) * (1.0 / np.sqrt(DIM))
        w_out = jax.random.normal(k2, (DIM, DIM), dtype=jnp.float32) * (1.0 / np.sqrt(DIM))
        return {'x': x, 'ln_w': ln_w, 'ln_b': ln_b, 'w_qkv': w_qkv, 'w_out': w_out}
    _L3_attn_all = _L3_attn_setup()
    _L3_attn_in = {k: v for k, v in _L3_attn_all.items() if k in ('ln_w', 'ln_b', 'w_qkv', 'w_out')}
    del _L3_attn_all

    def _L3_ffn_setup():
        import jax, jax.numpy as jnp
        import numpy as np
        E, D, F = (8, 256, 1024)
        LN_EPS = 1e-05
        key = jax.random.key(seed)
        k = jax.random.split(key, 8)
        x = jax.random.normal(k[0], (4, 512, D), jnp.float32)
        centroids = jax.random.normal(k[1], (E, D), jnp.float32) * 0.1
        ln_g = jnp.ones((E, D), jnp.float32)
        ln_b = jnp.zeros((E, D), jnp.float32)
        w1 = jax.random.normal(k[2], (E, F, D), jnp.float32) * (1.0 / np.sqrt(D))
        b1 = jnp.zeros((E, F), jnp.float32)
        w2 = jax.random.normal(k[3], (E, D, F), jnp.float32) * (1.0 / np.sqrt(F))
        b2 = jnp.zeros((E, D), jnp.float32)
        return {'input_features': x, 'centroids': centroids, 'ln_g': ln_g, 'ln_b': ln_b, 'w1': w1, 'b1': b1, 'w2': w2, 'b2': b2}
    _L3_ffn_all = _L3_ffn_setup()
    _L3_ffn_in = {k: v for k, v in _L3_ffn_all.items() if k in ('centroids', 'ln_g', 'ln_b', 'w1', 'b1', 'w2', 'b2')}
    del _L3_ffn_all
    return {'x': x, 'ctx_1024': ctx_1024, 'fside_SxS2_0': fside_SxS2_0, 'fside_BxS2_0': fside_BxS2_0, 'mask_BxS2_ik0': mask_BxS2_ik0, 'mask_Bx1x1xS2_fk0': mask_Bx1x1xS2_fk0, 'L0_xattn_q_w': _L0_xattn_in['q_w'], 'L0_xattn_q_b': _L0_xattn_in['q_b'], 'L0_xattn_k_w': _L0_xattn_in['k_w'], 'L0_xattn_k_b': _L0_xattn_in['k_b'], 'L0_xattn_v_w': _L0_xattn_in['v_w'], 'L0_xattn_v_b': _L0_xattn_in['v_b'], 'L0_attn_Wq': _L0_attn_in['Wq'], 'L0_attn_bq': _L0_attn_in['bq'], 'L0_attn_Wk': _L0_attn_in['Wk'], 'L0_attn_bk': _L0_attn_in['bk'], 'L0_attn_Wv': _L0_attn_in['Wv'], 'L0_attn_bv': _L0_attn_in['bv'], 'L0_ffn_Wg': _L0_ffn_in['Wg'], 'L0_ffn_bg': _L0_ffn_in['bg'], 'L0_ffn_w1': _L0_ffn_in['w1'], 'L0_ffn_b1': _L0_ffn_in['b1'], 'L0_ffn_w2': _L0_ffn_in['w2'], 'L0_ffn_b2': _L0_ffn_in['b2'], 'L0_ffn_w3': _L0_ffn_in['w3'], 'L0_ffn_b3': _L0_ffn_in['b3'], 'L1_xattn_Wk': _L1_xattn_in['Wk'], 'L1_xattn_bk': _L1_xattn_in['bk'], 'L1_xattn_Wv': _L1_xattn_in['Wv'], 'L1_xattn_bv': _L1_xattn_in['bv'], 'L1_xattn_Wq': _L1_xattn_in['Wq'], 'L1_xattn_bq': _L1_xattn_in['bq'], 'L1_xattn_Wo': _L1_xattn_in['Wo'], 'L1_xattn_bo': _L1_xattn_in['bo'], 'L1_attn_Wq': _L1_attn_in['Wq'], 'L1_attn_Wk': _L1_attn_in['Wk'], 'L1_attn_Wv': _L1_attn_in['Wv'], 'L1_attn_Wb': _L1_attn_in['Wb'], 'L1_attn_conv_q_w': _L1_attn_in['conv_q_w'], 'L1_attn_conv_k_w': _L1_attn_in['conv_k_w'], 'L1_attn_conv_v_w': _L1_attn_in['conv_v_w'], 'L1_attn_ms_w3': _L1_attn_in['ms_w3'], 'L1_attn_ms_w15': _L1_attn_in['ms_w15'], 'L1_attn_ms_w31': _L1_attn_in['ms_w31'], 'L1_attn_kernel_mix_w': _L1_attn_in['kernel_mix_w'], 'L1_attn_channel_mixer_w': _L1_attn_in['channel_mixer_w'], 'L1_attn_fusion_w1': _L1_attn_in['fusion_w1'], 'L1_attn_fusion_b1': _L1_attn_in['fusion_b1'], 'L1_attn_fusion_w2': _L1_attn_in['fusion_w2'], 'L1_attn_fusion_b2': _L1_attn_in['fusion_b2'], 'L1_attn_o_norm_w': _L1_attn_in['o_norm_w'], 'L1_attn_Wo': _L1_attn_in['Wo'], 'L1_ffn_gate_w': _L1_ffn_in['gate_w'], 'L1_ffn_w1': _L1_ffn_in['w1'], 'L1_ffn_b1': _L1_ffn_in['b1'], 'L1_ffn_ln1_g': _L1_ffn_in['ln1_g'], 'L1_ffn_ln1_b': _L1_ffn_in['ln1_b'], 'L1_ffn_w2': _L1_ffn_in['w2'], 'L1_ffn_b2': _L1_ffn_in['b2'], 'L1_ffn_ln_g': _L1_ffn_in['ln_g'], 'L1_ffn_ln_b': _L1_ffn_in['ln_b'], 'L2_xattn_wq': _L2_xattn_in['wq'], 'L2_xattn_bq': _L2_xattn_in['bq'], 'L2_xattn_wk': _L2_xattn_in['wk'], 'L2_xattn_bk': _L2_xattn_in['bk'], 'L2_xattn_wv': _L2_xattn_in['wv'], 'L2_xattn_bv': _L2_xattn_in['bv'], 'L2_xattn_wo': _L2_xattn_in['wo'], 'L2_xattn_bo': _L2_xattn_in['bo'], 'L2_attn_W': _L2_attn_in['W'], 'L2_ffn_w1': _L2_ffn_in['w1'], 'L2_ffn_b1': _L2_ffn_in['b1'], 'L2_ffn_w2': _L2_ffn_in['w2'], 'L2_ffn_b2': _L2_ffn_in['b2'], 'L3_xattn_Wq': _L3_xattn_in['Wq'], 'L3_xattn_bq': _L3_xattn_in['bq'], 'L3_xattn_Wk': _L3_xattn_in['Wk'], 'L3_xattn_bk': _L3_xattn_in['bk'], 'L3_xattn_Wv': _L3_xattn_in['Wv'], 'L3_xattn_bv': _L3_xattn_in['bv'], 'L3_xattn_Wo': _L3_xattn_in['Wo'], 'L3_xattn_bo': _L3_xattn_in['bo'], 'L3_attn_ln_w': _L3_attn_in['ln_w'], 'L3_attn_ln_b': _L3_attn_in['ln_b'], 'L3_attn_w_qkv': _L3_attn_in['w_qkv'], 'L3_attn_w_out': _L3_attn_in['w_out'], 'L3_ffn_centroids': _L3_ffn_in['centroids'], 'L3_ffn_ln_g': _L3_ffn_in['ln_g'], 'L3_ffn_ln_b': _L3_ffn_in['ln_b'], 'L3_ffn_w1': _L3_ffn_in['w1'], 'L3_ffn_b1': _L3_ffn_in['b1'], 'L3_ffn_w2': _L3_ffn_in['w2'], 'L3_ffn_b2': _L3_ffn_in['b2']}

def reference(x, ctx_1024, fside_SxS2_0, fside_BxS2_0, mask_BxS2_ik0, mask_Bx1x1xS2_fk0, L0_xattn_q_w, L0_xattn_q_b, L0_xattn_k_w, L0_xattn_k_b, L0_xattn_v_w, L0_xattn_v_b, L0_attn_Wq, L0_attn_bq, L0_attn_Wk, L0_attn_bk, L0_attn_Wv, L0_attn_bv, L0_ffn_Wg, L0_ffn_bg, L0_ffn_w1, L0_ffn_b1, L0_ffn_w2, L0_ffn_b2, L0_ffn_w3, L0_ffn_b3, L1_xattn_Wk, L1_xattn_bk, L1_xattn_Wv, L1_xattn_bv, L1_xattn_Wq, L1_xattn_bq, L1_xattn_Wo, L1_xattn_bo, L1_attn_Wq, L1_attn_Wk, L1_attn_Wv, L1_attn_Wb, L1_attn_conv_q_w, L1_attn_conv_k_w, L1_attn_conv_v_w, L1_attn_ms_w3, L1_attn_ms_w15, L1_attn_ms_w31, L1_attn_kernel_mix_w, L1_attn_channel_mixer_w, L1_attn_fusion_w1, L1_attn_fusion_b1, L1_attn_fusion_w2, L1_attn_fusion_b2, L1_attn_o_norm_w, L1_attn_Wo, L1_ffn_gate_w, L1_ffn_w1, L1_ffn_b1, L1_ffn_ln1_g, L1_ffn_ln1_b, L1_ffn_w2, L1_ffn_b2, L1_ffn_ln_g, L1_ffn_ln_b, L2_xattn_wq, L2_xattn_bq, L2_xattn_wk, L2_xattn_bk, L2_xattn_wv, L2_xattn_bv, L2_xattn_wo, L2_xattn_bo, L2_attn_W, L2_ffn_w1, L2_ffn_b1, L2_ffn_w2, L2_ffn_b2, L3_xattn_Wq, L3_xattn_bq, L3_xattn_Wk, L3_xattn_bk, L3_xattn_Wv, L3_xattn_bv, L3_xattn_Wo, L3_xattn_bo, L3_attn_ln_w, L3_attn_ln_b, L3_attn_w_qkv, L3_attn_w_out, L3_ffn_centroids, L3_ffn_ln_g, L3_ffn_ln_b, L3_ffn_w1, L3_ffn_b1, L3_ffn_w2, L3_ffn_b2):
    import jax
    import jax.numpy as jnp

    def _L0_xattn_ref(hidden_states, context, attention_mask, q_w, q_b, k_w, k_b, v_w, v_b):
        import jax, jax.numpy as jnp
        import numpy as np
        B, LQ, LK, D = (4, 512, 512, 256)
        H = 16
        HD = D // H

        def _split_heads(x):
            b, l, _ = x.shape
            return x.reshape(b, l, H, HD).transpose(0, 2, 1, 3)
        q = _split_heads(hidden_states @ q_w.T + q_b)
        k = _split_heads(context @ k_w.T + k_b)
        v = _split_heads(context @ v_w.T + v_b)
        scores = jnp.einsum('bhqd,bhkd->bhqk', q, k) / jnp.sqrt(jnp.float32(HD))
        mask = (attention_mask > 0)[:, None, None, :]
        scores = jnp.where(mask, -jnp.inf, scores)
        probs = jax.nn.softmax(scores, axis=-1)
        ctx = jnp.einsum('bhqk,bhkd->bhqd', probs, v)
        ctx = ctx.transpose(0, 2, 1, 3).reshape(ctx.shape[0], ctx.shape[2], H * HD)
        return ctx

    def _L0_attn_ref(X, Wq, bq, Wk, bk, Wv, bv):
        import jax, jax.numpy as jnp
        import numpy as np
        import math
        E = 256
        B, T = (8, 512)
        q = jnp.einsum('bte,fe->btf', X, Wq) + bq
        k = jnp.einsum('bte,fe->btf', X, Wk) + bk
        v = jnp.einsum('bte,fe->btf', X, Wv) + bv
        scores = jnp.einsum('bie,bje->bij', q, k) / math.sqrt(E)
        i = jnp.arange(scores.shape[-2])[:, None]
        j = jnp.arange(scores.shape[-1])[None, :]
        scores = jnp.where(j > i, -jnp.inf, scores)
        attn = jax.nn.softmax(scores, axis=-2)
        return jnp.einsum('bij,bje->bie', attn, v)

    def _L0_ffn_ref(x, Wg, bg, w1, b1, w2, b2, w3, b3):
        import jax, jax.numpy as jnp
        import numpy as np
        K = 64
        B, S, D = x.shape
        E, _, O = w1.shape
        logits = jnp.einsum('bsd,de->bse', x, Wg) + bg
        probs = jax.nn.softmax(logits, axis=-2)
        pv = jnp.transpose(probs, (0, 2, 1))
        vals, idx = jax.lax.top_k(pv, K)
        bidx = jnp.arange(B)[:, None, None]
        tok = x[bidx, idx]
        b1b = b1[None, :, None, :]
        b2b = b2[None, :, None, :]
        b3b = b3[None, :, None, :]
        h = jax.nn.relu(jnp.einsum('bekd,edo->beko', tok, w1) + b1b)
        h = jax.nn.relu(jnp.einsum('bekd,edo->beko', h, w2) + b2b)
        h = jnp.einsum('bekd,edo->beko', h, w3) + b3b
        out = h * vals[..., None]
        outputs = jnp.zeros((B, S, O), x.dtype).at[bidx, idx].add(out)
        return outputs

    def _L1_xattn_ref(K_in, V_in, Q_in, mask_attn, mask_pad, Wk, bk, Wv, bv, Wq, bq, Wo, bo):
        import jax, jax.numpy as jnp
        import numpy as np
        D = 256
        NH = 16
        DK = D // NH
        B, L, LP = (2, 512, 512)
        b, l = (K_in.shape[0], K_in.shape[1])
        lp = Q_in.shape[1]
        K = (K_in @ Wk + bk).reshape(b, l, NH, DK).transpose(0, 2, 1, 3)
        V = (V_in @ Wv + bv).reshape(b, l, NH, DK).transpose(0, 2, 1, 3)
        Q = (Q_in @ Wq + bq).reshape(b, lp, NH, DK).transpose(0, 2, 1, 3)
        KQ = jnp.einsum('bhld,bhpd->bhlp', K, Q) / np.float32(np.sqrt(DK))
        KQ = KQ + mask_pad.reshape(b, 1, l, 1)
        KQ = KQ + mask_attn.T.reshape(1, 1, l, lp)
        alpha = jax.nn.softmax(KQ, axis=2)
        O = jnp.einsum('bhlp,bhld->bhpd', alpha, V)
        O = O.transpose(0, 2, 1, 3).reshape(b, lp, NH * DK)
        return O @ Wo + bo

    def _L1_attn_ref(hidden_states, Wq, Wk, Wv, Wb, conv_q_w, conv_k_w, conv_v_w, ms_w3, ms_w15, ms_w31, kernel_mix_w, channel_mixer_w, fusion_w1, fusion_b1, fusion_w2, fusion_b2, o_norm_w, Wo):
        import jax, jax.numpy as jnp
        import numpy as np
        CHUNK = 32
        H = 4

        def silu(x):
            return x * jax.nn.sigmoid(x)

        def l2norm(x):
            return x * jax.lax.rsqrt(jnp.sum(x * x, -1, keepdims=True) + 1e-06)

        def dwconv_causal(x_cl, w):
            k = w.shape[1]
            xp = jnp.pad(x_cl, ((0, 0), (0, 0), (k - 1, 0)))
            return jax.lax.conv_general_dilated(xp, w[:, None, :], (1,), 'VALID', dimension_numbers=('NCH', 'OIH', 'NCH'), feature_group_count=x_cl.shape[1])

        def short_conv_silu(x_bld, w):
            y = dwconv_causal(jnp.swapaxes(x_bld, 1, 2), w)
            return silu(jnp.swapaxes(y, 1, 2))

        def delta_rule_chunkwise(q, k, v, beta, chunk=CHUNK):
            b, h, L, dk = q.shape
            dv = v.shape[-1]
            pad = -L % chunk
            if pad:
                q, k, v = (jnp.pad(t, ((0, 0), (0, 0), (0, pad), (0, 0))) for t in (q, k, v))
                beta = jnp.pad(beta, ((0, 0), (0, 0), (0, pad)))
            n = (L + pad) // chunk
            q = l2norm(q)
            k = l2norm(k)
            v = v * beta[..., None]
            kb = k * beta[..., None]
            ch = lambda x: x.reshape(b, h, n, chunk, x.shape[-1])
            qc, kc, vc, kbc = map(ch, (q, k, v, kb))
            idx = jnp.arange(chunk)
            strict_lower = (idx[:, None] > idx[None, :]).astype(q.dtype)
            incl_lower = (idx[:, None] >= idx[None, :]).astype(q.dtype)
            attn = -jnp.einsum('bhncd,bhned->bhnce', kbc, kc) * strict_lower
            for i in range(1, chunk):
                upd = jnp.einsum('...j,...ji->...i', attn[..., i, :], attn[..., :, :i])
                attn = attn.at[..., i, :i].add(upd)
            attn = attn + jnp.eye(chunk, dtype=q.dtype)
            u = attn @ vc
            w = attn @ kbc
            xs = tuple((jnp.moveaxis(t, 2, 0) for t in (qc, kc, u, w)))
            S0 = jnp.zeros((b, h, dk, dv), q.dtype)

            def step(S, x):
                qi, ki, ui, wi = x
                a_loc = jnp.einsum('bhcd,bhed->bhce', qi, ki) * incl_lower
                ui = ui - wi @ S
                oi = qi @ S + a_loc @ ui
                S = S + jnp.einsum('bhcd,bhcv->bhdv', ki, ui)
                return (S, oi)
            S, o = jax.lax.scan(step, S0, xs)
            o = jnp.moveaxis(o, 0, 2).reshape(b, h, n * chunk, dv)[:, :, :L]
            return (o, S)

        def multiscale_conv(v, ms_w3, ms_w15, ms_w31, kernel_mix_w, channel_mixer_w):
            b, l, h, d = v.shape
            x = jnp.swapaxes(v.reshape(b, l, h * d), 1, 2)
            outs = [dwconv_causal(x, w) for w in (ms_w3, ms_w15, ms_w31)]
            y = jnp.concatenate(outs, axis=1)
            y = y.reshape(b, h, 3 * d, l).transpose(0, 3, 1, 2)
            y = y @ kernel_mix_w
            y = (y.reshape(b, l, h * d) @ channel_mixer_w).reshape(b, l, h, d)
            return y

        def _forward(hidden_states, Wq, Wk, Wv, Wb, conv_q_w, conv_k_w, conv_v_w, ms_w3, ms_w15, ms_w31, kernel_mix_w, channel_mixer_w, fusion_w1, fusion_b1, fusion_w2, fusion_b2, o_norm_w, Wo):
            b, L, D = hidden_states.shape
            h = H
            dk = Wq.shape[1] // h
            dv = Wv.shape[1] // h
            q = short_conv_silu(hidden_states @ Wq, conv_q_w).reshape(b, L, h, dk)
            k = short_conv_silu(hidden_states @ Wk, conv_k_w).reshape(b, L, h, dk)
            v = short_conv_silu(hidden_states @ Wv, conv_v_w).reshape(b, L, h, dv)
            v_direct = v
            beta = jax.nn.sigmoid(hidden_states @ Wb)
            tr = lambda x: jnp.swapaxes(x, 1, 2)
            delta_out, _S = delta_rule_chunkwise(tr(q), tr(k), tr(v), tr(beta))
            delta_out = jnp.swapaxes(delta_out, 1, 2)
            ms_out = multiscale_conv(v_direct, ms_w3, ms_w15, ms_w31, kernel_mix_w, channel_mixer_w)
            bn = lambda x: jnp.mean(jnp.abs(x), -1)
            gate_features = jnp.concatenate([hidden_states, bn(ms_out), bn(delta_out), bn(v_direct)], -1)
            hdn = jax.nn.gelu(gate_features @ fusion_w1 + fusion_b1, approximate=False)
            logits = (hdn @ fusion_w2 + fusion_b2).reshape(b, L, h, 3)
            wts = jax.nn.softmax(logits, -1)
            o = wts[..., 0:1] * ms_out + wts[..., 1:2] * delta_out + wts[..., 2:3] * v_direct
            o = o * jax.lax.rsqrt(jnp.mean(o * o, -1, keepdims=True) + 1e-05) * o_norm_w
            return o.reshape(b, L, h * dv) @ Wo
        return _forward(hidden_states, Wq, Wk, Wv, Wb, conv_q_w, conv_k_w, conv_v_w, ms_w3, ms_w15, ms_w31, kernel_mix_w, channel_mixer_w, fusion_w1, fusion_b1, fusion_w2, fusion_b2, o_norm_w, Wo)

    def _L1_ffn_ref(x, gate_w, w1, b1, ln1_g, ln1_b, w2, b2, ln_g, ln_b):
        import jax, jax.numpy as jnp
        import numpy as np
        DIM = 256
        E = 8
        K = 2
        EPS = 1e-05

        def _ln(x, g, b):
            mu = jnp.mean(x, axis=-1, keepdims=True)
            var = jnp.mean(jnp.square(x - mu), axis=-1, keepdims=True)
            return (x - mu) * jax.lax.rsqrt(var + EPS) * g + b
        shape = x.shape
        xf = x.reshape(-1, shape[-1])
        gates = jax.nn.softmax(xf @ gate_w, axis=-1)
        topw, topi = jax.lax.top_k(gates, K)
        topw = topw / jnp.sum(topw, axis=-1, keepdims=True)
        combine = jnp.sum(topw[:, :, None] * jax.nn.one_hot(topi, E, dtype=xf.dtype), axis=1)
        h = jnp.einsum('td,edh->teh', xf, w1) + b1
        h = _ln(h, ln1_g, ln1_b)
        h = jax.nn.gelu(h, approximate=False)
        y = jnp.einsum('teh,ehd->ted', h, w2) + b2
        out = jnp.einsum('ted,te->td', y, combine)
        out = _ln(out + xf, ln_g, ln_b)
        return out.reshape(shape)

    def _L2_xattn_ref(x_q, x_k, x_v, wq, bq, wk, bk, wv, bv, wo, bo):
        import jax, jax.numpy as jnp
        import numpy as np
        EMBED_DIM = 256
        NUM_HEADS = 16
        HEAD_DIM = EMBED_DIM // NUM_HEADS

        def _split_heads(x):
            B, S, _ = x.shape
            return x.reshape(B, S, NUM_HEADS, HEAD_DIM).transpose(0, 2, 1, 3)
        q = _split_heads(x_q @ wq + bq)
        k = _split_heads(x_k @ wk + bk)
        v = _split_heads(x_v @ wv + bv)
        scores = jnp.einsum('bhqd,bhkd->bhqk', q, k) / jnp.sqrt(jnp.float32(HEAD_DIM))
        weights = jax.nn.softmax(scores, axis=-1)
        attn = jnp.einsum('bhqk,bhkd->bhqd', weights, v)
        B, H, S, hd = attn.shape
        concat = attn.transpose(0, 2, 1, 3).reshape(B, S, H * hd)
        return concat @ wo + bo

    def _L2_attn_ref(x, W):
        import jax, jax.numpy as jnp
        import numpy as np
        B, S, D_MODEL, D_K = (4, 512, 256, 1)
        D_QKV = D_MODEL * D_K
        MASK_NEG = -9000000000000000.0

        def _scaled_dot_product_attention(q, k, v):
            d_k = k.shape[-1]
            scores = jnp.einsum('bqd,bkd->bqk', q, k) / jnp.sqrt(jnp.float32(d_k))
            scores = jnp.triu(scores, k=0)
            scores = jnp.where(scores == 0, MASK_NEG, scores)
            attn = jax.nn.softmax(scores, axis=-1)
            return jnp.einsum('bqk,bkd->bqd', attn, v)
        qkv = jnp.einsum('bsd,df->bsf', x, W)
        q, k, v = jnp.split(qkv, 3, axis=-1)
        return _scaled_dot_product_attention(q, k, v)

    def _L2_ffn_ref(x, w1, b1, w2, b2):
        import jax, jax.numpy as jnp
        import numpy as np
        MANT_BITS = 8
        _PWL_X = jnp.linspace(-4.0, 4.0, 33, dtype=jnp.float32)
        _PWL_Y = 0.5 * _PWL_X * (1.0 + jax.lax.erf(_PWL_X / jnp.sqrt(jnp.float32(2.0))))

        def float2fix(x, mantissa_bits):
            s = jnp.float32(2.0 ** mantissa_bits)
            q = jnp.round(x * s) / s
            return x + jax.lax.stop_gradient(q - x)

        def pwlin_gelu_basic(x, mantissa_bits_in, mantissa_bits_out):
            xq = float2fix(x, mantissa_bits_in)
            y = jnp.interp(xq, _PWL_X, _PWL_Y)
            y = jnp.where(xq > 4.0, xq, jnp.where(xq < -4.0, jnp.float32(0.0), y))
            return float2fix(y, mantissa_bits_out)
        h = jnp.einsum('bsd,df->bsf', x, w1) + b1
        h = float2fix(h, MANT_BITS)
        h = pwlin_gelu_basic(h, MANT_BITS, MANT_BITS)
        h = float2fix(h, MANT_BITS)
        out = jnp.einsum('bsf,fd->bsd', h, w2) + b2
        return float2fix(out, MANT_BITS)

    def _L3_xattn_ref(query, key, value, mask, Wq, bq, Wk, bk, Wv, bv, Wo, bo):
        import jax, jax.numpy as jnp
        import numpy as np
        B, S, D, H = (2, 512, 256, 16)
        DH = D // H

        def _split_heads(x):
            b, s, _ = x.shape
            return x.reshape(b, s, H, DH).transpose(0, 2, 1, 3)
        q = _split_heads(query @ Wq + bq)
        k = _split_heads(key @ Wk + bk)
        v = _split_heads(value @ Wv + bv)
        logits = jnp.einsum('bhqd,bhkd->bhqk', q, k) / jnp.sqrt(jnp.float32(DH))
        logits = logits + mask * -1000000000.0
        attn = jax.nn.softmax(logits, axis=-1)
        out = jnp.einsum('bhqk,bhkd->bhqd', attn, v)
        out = out.transpose(0, 2, 1, 3).reshape(query.shape[0], -1, D)
        return out @ Wo + bo

    def _L3_attn_ref(x, ln_w, ln_b, w_qkv, w_out):
        import jax, jax.numpy as jnp
        import numpy as np
        DIM = 256
        DIM_HEAD = 64
        HEADS = DIM // DIM_HEAD
        WINDOW = 32
        EPS = 1e-05

        def _rotate_half(x):
            x1, x2 = jnp.split(x, 2, axis=-1)
            return jnp.concatenate((-x2, x1), axis=-1)
        B, T, C = x.shape
        residual = x
        mu = jnp.mean(x, axis=-1, keepdims=True)
        var = jnp.mean(jnp.square(x - mu), axis=-1, keepdims=True)
        xn = (x - mu) * jax.lax.rsqrt(var + EPS) * ln_w + ln_b
        qkv = xn @ w_qkv.T
        q, k, v = jnp.split(qkv, 3, axis=-1)

        def to_heads(t):
            return t.reshape(B, T, HEADS, DIM_HEAD).transpose(0, 2, 1, 3)
        q, k, v = (to_heads(q), to_heads(k), to_heads(v))
        inv_freq = 1.0 / 10000.0 ** (jnp.arange(0, DIM_HEAD, 2, dtype=jnp.float32) / DIM_HEAD)
        t_pos = jnp.arange(T, dtype=jnp.float32)
        freqs = t_pos[:, None] * inv_freq[None, :]
        freqs = jnp.concatenate((freqs, freqs), axis=-1)
        cos, sin = (jnp.cos(freqs), jnp.sin(freqs))
        q = q * cos + _rotate_half(q) * sin
        k = k * cos + _rotate_half(k) * sin
        pos = jnp.arange(T)
        mask = (pos[:, None] >= pos[None, :]) & (pos[:, None] - pos[None, :] < WINDOW)
        scale = 1.0 / np.sqrt(DIM_HEAD)
        scores = jnp.einsum('bhqd,bhkd->bhqk', q, k) * scale
        scores = jnp.where(mask, scores, jnp.float32(-1e+30))
        attn = jax.nn.softmax(scores, axis=-1)
        out = jnp.einsum('bhqk,bhkd->bhqd', attn, v)
        out = out.transpose(0, 2, 1, 3).reshape(B, T, C) @ w_out.T
        return out + residual

    def _L3_ffn_ref(input_features, centroids, ln_g, ln_b, w1, b1, w2, b2):
        import jax, jax.numpy as jnp
        import numpy as np
        E, D, F = (8, 256, 1024)
        LN_EPS = 1e-05
        x = input_features.reshape(-1, D)
        aff = jax.lax.stop_gradient(x) @ centroids.T
        assign = jnp.argmax(aff, axis=1)
        onehot = jax.nn.one_hot(assign, E, dtype=x.dtype)
        mu = jnp.mean(x, axis=-1, keepdims=True)
        var = jnp.mean((x - mu) ** 2, axis=-1, keepdims=True)
        xhat = (x - mu) * jax.lax.rsqrt(var + LN_EPS)
        xn = xhat[None, :, :] * ln_g[:, None, :] + ln_b[:, None, :]
        h = jax.nn.relu(jnp.einsum('etd,efd->etf', xn, w1) + b1[:, None, :])
        y = x[None, :, :] + jnp.einsum('etf,edf->etd', h, w2) + b2[:, None, :]
        alpha = jax.nn.sigmoid(x @ centroids.T)
        a = alpha.T[:, :, None]
        gated = a * y + (1.0 - a) * x[None, :, :]
        out = jnp.einsum('te,etd->td', onehot, gated)
        return out.reshape(input_features.shape)
    x = x + _L0_xattn_ref(_layernorm(x, axis=-1), ctx_1024, mask_BxS2_ik0, L0_xattn_q_w, L0_xattn_q_b, L0_xattn_k_w, L0_xattn_k_b, L0_xattn_v_w, L0_xattn_v_b)
    x = x + _L0_attn_ref(_layernorm(x, axis=-1), L0_attn_Wq, L0_attn_bq, L0_attn_Wk, L0_attn_bk, L0_attn_Wv, L0_attn_bv)
    x = x + _L0_ffn_ref(_layernorm(x, axis=-1), L0_ffn_Wg, L0_ffn_bg, L0_ffn_w1, L0_ffn_b1, L0_ffn_w2, L0_ffn_b2, L0_ffn_w3, L0_ffn_b3)
    x = x + _L1_xattn_ref(ctx_1024, ctx_1024, _layernorm(x, axis=-1), fside_SxS2_0, fside_BxS2_0, L1_xattn_Wk, L1_xattn_bk, L1_xattn_Wv, L1_xattn_bv, L1_xattn_Wq, L1_xattn_bq, L1_xattn_Wo, L1_xattn_bo)
    x = x + _L1_attn_ref(_layernorm(x, axis=-1), L1_attn_Wq, L1_attn_Wk, L1_attn_Wv, L1_attn_Wb, L1_attn_conv_q_w, L1_attn_conv_k_w, L1_attn_conv_v_w, L1_attn_ms_w3, L1_attn_ms_w15, L1_attn_ms_w31, L1_attn_kernel_mix_w, L1_attn_channel_mixer_w, L1_attn_fusion_w1, L1_attn_fusion_b1, L1_attn_fusion_w2, L1_attn_fusion_b2, L1_attn_o_norm_w, L1_attn_Wo)
    x = x + _L1_ffn_ref(_layernorm(x, axis=-1), L1_ffn_gate_w, L1_ffn_w1, L1_ffn_b1, L1_ffn_ln1_g, L1_ffn_ln1_b, L1_ffn_w2, L1_ffn_b2, L1_ffn_ln_g, L1_ffn_ln_b)
    x = x + _L2_xattn_ref(_layernorm(x, axis=-1), ctx_1024, ctx_1024, L2_xattn_wq, L2_xattn_bq, L2_xattn_wk, L2_xattn_bk, L2_xattn_wv, L2_xattn_bv, L2_xattn_wo, L2_xattn_bo)
    x = x + _L2_attn_ref(_layernorm(x, axis=-1), L2_attn_W)
    x = x + _L2_ffn_ref(_layernorm(x, axis=-1), L2_ffn_w1, L2_ffn_b1, L2_ffn_w2, L2_ffn_b2)
    x = x + _L3_xattn_ref(_layernorm(x, axis=-1), ctx_1024, ctx_1024, mask_Bx1x1xS2_fk0, L3_xattn_Wq, L3_xattn_bq, L3_xattn_Wk, L3_xattn_bk, L3_xattn_Wv, L3_xattn_bv, L3_xattn_Wo, L3_xattn_bo)
    x = x + _L3_attn_ref(_layernorm(x, axis=-1), L3_attn_ln_w, L3_attn_ln_b, L3_attn_w_qkv, L3_attn_w_out)
    x = x + _L3_ffn_ref(_layernorm(x, axis=-1), L3_ffn_centroids, L3_ffn_ln_g, L3_ffn_ln_b, L3_ffn_w1, L3_ffn_b1, L3_ffn_w2, L3_ffn_b2)
    return x

_drawn_inputs = setup_inputs


def setup_inputs(seed=0):
    import zlib

    import numpy as np

    out = dict(_drawn_inputs(seed))
    spreads = {'L0_xattn_q_b': (0.0, 0.8),
     'L0_xattn_k_b': (0.0, 2.0),
     'L0_xattn_v_b': (0.0, 0.1),
     'L0_ffn_bg': (0.0, 2.0),
     'L1_attn_fusion_b1': (0.0, 0.336),
     'L1_attn_o_norm_w': (1.0, 0.2),
     'L1_ffn_ln1_g': (1.0, 0.6),
     'L1_ffn_ln1_b': (0.0, 0.795),
     'L1_ffn_ln_g': (1.0, 0.2),
     'L1_ffn_ln_b': (0.0, 0.1),
     'L2_xattn_bq': (0.0, 0.8),
     'L2_xattn_bk': (0.0, 2.0),
     'L2_xattn_bv': (0.0, 0.1),
     'L2_xattn_bo': (0.0, 0.1),
     'L3_xattn_bq': (0.0, 0.8),
     'L3_xattn_bk': (0.0, 2.0),
     'L3_xattn_bv': (0.0, 0.404),
     'L3_xattn_bo': (0.0, 0.1),
     'L3_attn_ln_w': (1.0, 0.2),
     'L3_attn_ln_b': (0.0, 0.308),
     'L3_ffn_ln_g': (1.0, 0.6),
     'L3_ffn_ln_b': (0.0, 0.676),
     'L3_ffn_b1': (0.0, 0.667),
     'L3_ffn_b2': (0.0, 0.488)}
    factors = {'L0_xattn_q_w': 7.292,
     'L0_xattn_k_w': 6.555,
     'L0_attn_bq': 64.0,
     'L0_attn_bk': 7.682,
     'L0_ffn_b2': 3.398,
     'L0_ffn_b3': 8.0,
     'L1_xattn_bk': 64.0,
     'L1_xattn_bq': 3.263,
     'L1_attn_ms_w3': 3.062,
     'L1_ffn_b1': 8.0,
     'L1_ffn_b2': 7.863,
     'L2_ffn_b1': 8.0,
     'L2_ffn_b2': 8.0,
     'L3_xattn_Wq': 8.0,
     'L3_xattn_Wk': 8.0,
     'L3_xattn_Wv': 3.032}
    for name, (base, spread) in spreads.items():
        noise = np.random.default_rng([zlib.crc32(name.encode()), seed]).standard_normal(out[name].shape)
        drawn = base * np.exp(spread * noise) if base else spread * noise
        out[name] = jnp.asarray(drawn.astype(out[name].dtype))
    for name, factor in factors.items():
        out[name] = (out[name] * factor).astype(out[name].dtype)
    return out
```

```python
from contextlib import ExitStack

import numpy as np
import concourse.bass as bass
from concourse import mybir

F32 = mybir.dt.float32
I32 = mybir.dt.int32
ALU = mybir.AluOpType
ACT = mybir.ActivationFunctionType
AX = mybir.AxisListType.X

P = 128
D = 256
DC = D // P
NKEYS = 12544
HX = 16
HD = D // HX
HPC = P // HD
BIG = 1e30


class Module:

    def __init__(self, nc, name):
        self.nc, self.name, self.stack, self.sems = nc, name, ExitStack(), {}

    def sb(self, name, shape, dtype=F32):
        return self.stack.enter_context(self.nc.sbuf_tensor(f"{self.name}_{name}", shape, dtype))

    def ps(self, name, shape=(P, 512), dtype=F32):
        return self.stack.enter_context(self.nc.psum_tensor(f"{self.name}_{name}", list(shape), dtype))

    def sem(self, name):
        if name not in self.sems:
            self.sems[name] = self.nc.alloc_semaphore(f"{self.name}_{name}")
        return self.sems[name]

    def end(self):
        self.nc.clear_and_free_semaphores(list(self.sems.values()))
        self.nc.all_engine_barrier()
        self.stack.close()


KB = 512
NBLK = NKEYS // KB
TAIL = NKEYS - NBLK * KB
S_RING = 4
T_RING = 2
P_RING = 4
PT_RING = 8
VW = 32
DVE_COPIES = (1,)


def cross_attention(nc, st, name, w, mask_kind):
    m = Module(nc, name)
    sb, ps, sem = m.sb, m.ps, m.sem
    x, ident = st["x"], st["ident"]
    has_wo = "wo" in w

    xn = sb("xn", [P, D])
    stats = sb("stats", [P, 6])
    mean_var = sb("mean_var", [P, 2])
    rstd = sb("rstd", [P, 2])
    xnT = sb("xnT", [P, DC, P])
    wq, wk, wv = (sb(n, [P, DC, D]) for n in ("wq", "wk", "wv"))
    wo = sb("wo", [P, DC, D]) if has_wo else None
    bias_q, bias_k = sb("bias_q", [P, DC]), sb("bias_k", [P, DC])
    bias_v = sb("bias_v", [P, D])
    bias_o = sb("bias_o", [P, D]) if has_wo else None
    qT = sb("qT", [P, DC, P])
    q_head = sb("q_head", [P, HX, P])
    ctx = sb("ctx", [P, 2, DC, KB])
    kT = sb("kT", [P, 2, DC, KB])
    v = sb("v", [P, 2, KB // P, HX, VW])
    raw = sb("raw", [P, 2, KB], I32 if mask_kind == "int" else F32) if mask_kind else None
    pad = sb("pad", [P, 2, KB]) if mask_kind == "two" else None
    mask = sb("mask", [P, 2, KB]) if mask_kind else None
    block_max = sb("block_max", [P, HX])
    neg_max = sb("neg_max", [P, 2, HX])
    max_step = sb("max_step", [P, HX])
    alpha = sb("alpha", [P, HX])
    prob = sb("prob", [P, P_RING, KB])
    probT = sb("probT", [P, PT_RING, KB])
    oT = sb("oT", [P, 4, P])
    acc = sb("acc", [P, HX, VW])
    rsum = sb("rsum", [P, HX])
    o = sb("o", [P, D])
    o2T = sb("o2T", [P, DC, P])

    p_s = [ps(f"p_s{i}") for i in range(S_RING)]
    p_t = [ps(f"p_t{i}") for i in range(T_RING)]
    p_proj, p_oT = ps("p_proj"), ps("p_oT")

    LAST = NBLK
    keys = lambda b: TAIL if isinstance(b, int) and b == LAST else KB

    def loads(b, odd):
        return b // 2 + 1 if isinstance(b, int) else (b - odd) // 2 + 1

    def in_register(eng, value):
        return value if isinstance(value, int) else eng.to_reg(value)

    def over_blocks(eng, body):
        body(0, 0)
        body(1, 1)
        with eng.Fori(1, NBLK // 2) as pair:
            body(pair * 2, 0)
            body(pair * 2 + 1, 1)
        body(LAST, LAST % 2)

    def copied(h):
        return "probT_copied_dve" if h % 4 in DVE_COPIES else "probT_copied_act"

    def copies(b, h):
        mine = [i for i in range(HX) if copied(i) == copied(h)]
        return b * len(mine) + len([i for i in mine if i <= h]) if h >= 0 else \
            b * len(mine) - len([i for i in mine if i - HX > h])

    def copy_turned(e, copy, b, odd, h):
        nk = keys(b)
        e.wait_ge(sem("turned"), b * HX + h + 1)
        if not (isinstance(b, int) and b == 0 and h < PT_RING):
            e.wait_ge(sem("valued"), b * 4 + h // 4 - 1)
        copy(probT[:, h % PT_RING, 0:nk], p_t[h % T_RING][:, 0:nk]).then_inc(sem(copied(h)), 1)

    with nc.Block() as block:

        @block.sync
        def _(e):
            e.dma_start(wq[:], w["wq"].rearrange("(c p) n -> p c n", p=P)).then_inc(sem("q_weights"), 16)
            e.dma_start(bias_q[:], w["bq"]).then_inc(sem("q_weights"), 16)
            e.dma_start(wk[:], w["wk"].rearrange("(c p) n -> p c n", p=P)).then_inc(sem("kv_weights"), 16)
            e.dma_start(bias_k[:], w["bk"]).then_inc(sem("kv_weights"), 16)
            e.dma_start(wv[:], w["wv"].rearrange("(c p) n -> p c n", p=P)).then_inc(sem("kv_weights"), 16)
            e.dma_start(bias_v[:], w["bv"]).then_inc(sem("out_weights"), 16)
            if has_wo:
                e.dma_start(wo[:], w["wo"].rearrange("(c p) n -> p c n", p=P)).then_inc(sem("out_weights"), 16)
                e.dma_start(bias_o[:], w["bo"]).then_inc(sem("out_weights"), 16)
            ctx_dram = w["ctxT"].rearrange("(c p) n -> p c n", p=P)

            def load(b, odd):
                nk = keys(b)
                late = not (isinstance(b, int) and b < 2)
                if late:
                    e.wait_ge(sem("projected"), (b - 1) * 4)
                e.dma_start(ctx[:, odd, :, 0:nk], ctx_dram[:, :, bass.ds(b * KB, nk)]).then_inc(sem(f"ctx_loaded_{odd}"), 16)
                if mask_kind:
                    if late:
                        e.wait_ge(sem("mask_made"), b - 1)
                    src = w["mask"]
                    if mask_kind == "two":
                        e.dma_start(raw[:, odd, 0:nk], src[:, bass.ds(b * KB, nk)]).then_inc(sem(f"mask_loaded_{odd}"), 16)
                        e.dma_start(pad[:, odd, 0:nk], w["pad"][:, bass.ds(b * KB, nk)].broadcast_to([P, nk])).then_inc(sem(f"mask_loaded_{odd}"), 16)
                    else:
                        e.dma_start(raw[:, odd, 0:nk], src[:, bass.ds(b * KB, nk)].broadcast_to([P, nk])).then_inc(sem(f"mask_loaded_{odd}"), 16)

            over_blocks(e, load)

        @block.gpsimd
        def _(e):
            e.memset(v[:], 0.0).then_inc(sem("v_zero"), 1)
            e.wait_ge(sem("v_zero"), 1)
            e.memset(v[:, :, :, :, HD:HD + 1], 1.0).then_inc(sem("v_ones"), 1)
            if not mask_kind:
                return

            def make_mask(b, odd):
                nk = keys(b)
                e.wait_ge(sem(f"mask_loaded_{odd}"), loads(b, odd) * (32 if mask_kind == "two" else 16))
                if not (isinstance(b, int) and b < 2):
                    used = in_register(e, (b - 1) * HX)
                    e.wait_ge(sem("v_ones"), 1)
                    e.wait_ge(sem("maxed"), used)
                r, q = raw[:, odd, 0:nk], mask[:, odd, 0:nk]
                if mask_kind == "int":
                    i = e.tensor_scalar(q, r, 0.0, -BIG, ALU.is_gt, ALU.mult)
                elif mask_kind == "float":
                    i = e.tensor_scalar(q, r, -1e9, None, ALU.mult)
                else:
                    i = e.tensor_tensor(q, r, pad[:, odd, 0:nk], ALU.add)
                i.then_inc(sem("mask_made"), 1)

            over_blocks(e, make_mask)

        @block.tensor
        def _(e):
            e.wait_ge(sem("normed"), 1)
            for c in range(DC):
                i = e.transpose(p_t[0][:, c * P:(c + 1) * P], xn[:, c * P:(c + 1) * P], ident[:])
            i.then_inc(sem("xn_turned"), 1)

            def project(b, odd, part):
                nk = keys(b)
                if part == 0:
                    e.wait_ge(sem(f"ctx_loaded_{odd}"), loads(b, odd) * 16)
                if not (isinstance(b, int) and b == 0 and part == 0):
                    e.wait_ge(sem("proj_copied"), b * 4 + part)
                if part == 1 and not (isinstance(b, int) and b < 2):
                    e.wait_ge(sem("added"), b - 1)
                for c in range(DC):
                    if part < 2:
                        i = e.matmul(p_proj[:, 0:nk], wk[:, c, part * P:(part + 1) * P], ctx[:, odd, c, 0:nk],
                                     start=c == 0, stop=c == DC - 1)
                if part >= 2:
                    for t in range(2):
                        k0 = ((part - 2) * 2 + t) * P
                        if k0 < nk:
                            for c in range(DC):
                                i = e.matmul(p_proj[:, t * D:(t + 1) * D], ctx[:, odd, c, k0:k0 + P], wv[:, c, :],
                                             start=c == 0, stop=c == DC - 1)
                i.then_inc(sem("projected"), 1)

            def scores(b, odd, h):
                nk = keys(b)
                if not (isinstance(b, int) and b == 0 and h < S_RING):
                    e.wait_ge(sem("exped"), b * HX + h - S_RING + 1)
                e.matmul(p_s[h % S_RING][:, 0:nk], q_head[:, h, :], kT[:, odd, h // HPC, 0:nk],
                         start=True, stop=True).then_inc(sem("scored"), 1)

            def turn(b, odd, h):
                nk = keys(b)
                e.wait_ge(sem("exped"), b * HX + h + 1)
                if not (isinstance(b, int) and b == 0 and h < T_RING):
                    e.wait_ge(sem(copied(h - T_RING)), copies(b, h - T_RING))
                for t in range(nk // P):
                    i = e.transpose(p_t[h % T_RING][:, t * P:(t + 1) * P], prob[:, h % P_RING, t * P:(t + 1) * P], ident[:])
                i.then_inc(sem("turned"), 1)

            def values(b, odd, g):
                nk = keys(b)
                if g == 0 and not (isinstance(b, int) and b == 0):
                    e.wait_ge(sem("oT_copied"), b)
                for s in range(4):
                    if s in (max(DVE_COPIES), 3):
                        e.wait_ge(sem(copied(4 * g + s)), copies(b, 4 * g + s))
                for t in range(nk // P):
                    for s in range(4):
                        h = 4 * g + s
                        i = e.matmul(p_oT[VW * s:VW * s + VW, g * P:(g + 1) * P], v[:, odd, t, h, :],
                                     probT[:, h % PT_RING, t * P:(t + 1) * P], start=t == 0, stop=t == nk // P - 1)
                i.then_inc(sem("valued"), 1)

            def turn_out(b, projected):
                e.wait_ge(sem("oT_copied"), b + 1)
                e.wait_ge(sem("proj_copied"), projected)
                if not (isinstance(b, int) and b == 0):
                    e.wait_ge(sem("added"), b)
                for g in range(4):
                    i = e.transpose(p_proj[:, g * P:(g + 1) * P], oT[:, g, :], ident[:])
                i.then_inc(sem("o_turned"), 1)

            def body(b, odd):
                first, last = isinstance(b, int) and b == 0, isinstance(b, int) and b == LAST
                for h in range(HX):
                    if h == 0:
                        e.wait_ge(sem("proj_copied"), (b + 1) * 4)
                    scores(b, odd, h)
                    if h % 4 == 3:
                        if h > 3:
                            values(b, odd, h // 4 - 1)
                        elif not first:
                            values(b - 1, 1 - odd, 3)
                        if not last:
                            nb = (b + 1)
                            project(nb, 1 - odd, h // 4)
                    if h == 5 and not first:
                        turn_out(b - 1, 4 * NBLK + 4 if last else 4 * b + 5)
                    if h >= 2:
                        turn(b, odd, h - 2)
                    elif not first:
                        turn(b - 1, 1 - odd, HX - 2 + h)

            e.wait_ge(sem("q_weights"), 32)
            e.wait_ge(sem("xnT_copied"), 1)
            for oc in range(DC):
                for c in range(DC):
                    i = e.matmul(p_t[1][:, oc * P:(oc + 1) * P], wq[:, c, oc * P:(oc + 1) * P], xnT[:, c, :],
                                 start=c == 0, stop=c == DC - 1)
            i.then_inc(sem("q_made"), 1)
            e.wait_ge(sem("kv_weights"), 48)
            for part in range(4):
                project(0, 0, part)
            e.wait_ge(sem("q_split"), 1)
            over_blocks(e, body)
            odd = LAST % 2
            turn(LAST, odd, HX - 2)
            turn(LAST, odd, HX - 1)
            values(LAST, odd, 3)
            turn_out(LAST, 4 * NBLK + 4)
            if has_wo:
                e.wait_ge(sem("o_final"), 1)
                for c in range(DC):
                    i = e.transpose(p_t[0][:, c * P:(c + 1) * P], o[:, c * P:(c + 1) * P], ident[:])
                i.then_inc(sem("o2_turned"), 1)
                e.wait_ge(sem("o2T_copied"), 1)
                e.wait_ge(sem("out_weights"), 48)
                for c in range(DC):
                    i = e.matmul(p_proj[:, 0:D], o2T[:, c, :], wo[:, c, :], start=c == 0, stop=c == DC - 1)
                i.then_inc(sem("out_made"), 1)

        @block.scalar
        def _(e):
            e.wait_ge(sem("stats"), 2)
            e.activation(rstd[:, 0:1], rstd[:, 1:2], ACT.Sqrt).then_inc(sem("root"), 1)

            def copy_proj(b, odd, part):
                nk = keys(b)
                e.wait_ge(sem("projected"), b * 4 + part + 1)
                if part < 2:
                    i = e.activation(kT[:, odd, part, 0:nk], p_proj[:, 0:nk], ACT.Identity, bias=bias_k[:, part:part + 1])
                else:
                    t0 = (part - 2) * 2
                    nt = min(2, max(nk // P - t0, 0))
                    if nt:
                        i = e.activation(v[:, odd, t0:t0 + nt, :, 0:HD],
                                         p_proj[:, 0:nt * D].rearrange("p (t h d) -> p t h d", t=nt, h=HX), ACT.Copy)
                    else:
                        i = e.nop()
                i.then_inc(sem("proj_copied"), 1)

            def body(b, odd):
                first, last = isinstance(b, int) and b == 0, isinstance(b, int) and b == LAST
                nk = keys(b)
                for h in range(HX):
                    e.wait_ge(sem("maxed"), b * HX + h + 1)
                    if not (first and h < P_RING):
                        e.wait_ge(sem("turned"), b * HX + h - P_RING + 1)
                    e.activation(prob[:, h % P_RING, 0:nk], p_s[h % S_RING][:, 0:nk], ACT.Exp,
                                 bias=neg_max[:, odd, h:h + 1]).then_inc(sem("exped"), 1)
                    if h % 4 == 3 and not last:
                        copy_proj(b + 1, 1 - odd, h // 4)
                    if h >= 2:
                        if (h - 2) % 4 not in DVE_COPIES:
                            copy_turned(e, e.copy, b, odd, h - 2)
                    elif not first:
                        if (h - 2) % 4 not in DVE_COPIES:
                            copy_turned(e, e.copy, b - 1, 1 - odd, HX - 2 + h)
                e.wait_ge(sem("stepped"), b + 1)
                if not first:
                    e.wait_ge(sem("scaled"), b)
                e.activation(alpha[:], max_step[:], ACT.Exp).then_inc(sem("alpha"), 1)

            e.wait_ge(sem("v_ones"), 1)
            e.wait_ge(sem("kv_weights"), 48)
            for part in range(4):
                copy_proj(0, 0, part)
            over_blocks(e, body)
            for h in (HX - 2, HX - 1):
                if h % 4 not in DVE_COPIES:
                    copy_turned(e, e.copy, LAST, LAST % 2, h)

        @block.vector
        def _(e):
            e.bn_stats(stats[:], x[:]).then_inc(sem("bn"), 1)
            e.memset(acc[:], 0.0).then_inc(sem("acc_zero"), 1)
            e.memset(neg_max[:], BIG).then_inc(sem("acc_zero"), 1)
            e.wait_ge(sem("bn"), 1)
            e.bn_aggr(mean_var[:], stats[:]).then_inc(sem("stats"), 1)
            e.wait_ge(sem("stats"), 1)
            e.tensor_scalar(rstd[:, 1:2], mean_var[:, 1:2], 1e-5, None, ALU.add).then_inc(sem("stats"), 1)
            e.wait_ge(sem("root"), 1)
            e.reciprocal(rstd[:, 1:2], rstd[:, 0:1]).then_inc(sem("bn"), 1)
            e.wait_ge(sem("bn"), 2)
            e.tensor_scalar(xn[:], x[:], mean_var[:, 0:1], rstd[:, 1:2], ALU.subtract, ALU.mult).then_inc(sem("normed"), 1)
            e.wait_ge(sem("xn_turned"), 1)
            e.tensor_copy(xnT[:].rearrange("p c n -> p (c n)"), p_t[0][:, 0:D]).then_inc(sem("xnT_copied"), 1)
            e.wait_ge(sem("q_made"), 1)
            e.wait_ge(sem("q_weights"), 32)
            for c in range(DC):
                e.tensor_scalar(qT[:, c, :], p_t[1][:, c * P:(c + 1) * P], bias_q[:, c:c + 1], float(HD) ** -0.5,
                                ALU.add, ALU.mult).then_inc(sem("q_copied"), 1)
            e.wait_ge(sem("q_copied"), DC)
            for h in range(HX):
                i = e.tensor_scalar(q_head[:, h, :], qT[:, h // HPC, :], st["head_rows"][:, h % HPC:h % HPC + 1], None, ALU.mult)
            i.then_inc(sem("q_split"), 1)
            e.wait_ge(sem("acc_zero"), 2)

            def body(b, odd):
                first, last = isinstance(b, int) and b == 0, isinstance(b, int) and b == LAST
                nk = keys(b)
                if mask_kind:
                    e.wait_ge(sem("mask_made"), b + 1)
                for h in range(HX):
                    made = in_register(e, b * HX + h + 1)
                    if mask_kind:
                        e.wait_ge(sem("acc_zero"), 2)
                    e.wait_ge(sem("scored"), made)
                    s = p_s[h % S_RING][:, 0:nk]
                    if mask_kind:
                        e.tensor_tensor_reduce(s, s, mask[:, odd, 0:nk], 1.0, -3e38, ALU.add, ALU.max,
                                               block_max[:, h:h + 1]).then_inc(sem("head_maxed"), 1)
                    else:
                        e.tensor_reduce(block_max[:, h:h + 1], s, AX, ALU.max).then_inc(sem("head_maxed"), 1)
                    e.wait_ge(sem("head_maxed"), b * HX + h + 1)
                    e.scalar_tensor_tensor(neg_max[:, odd, h:h + 1], block_max[:, h:h + 1], -1.0,
                                           neg_max[:, 1 - odd, h:h + 1], ALU.mult, ALU.min).then_inc(sem("maxed"), 1)
                    if h >= 2:
                        if (h - 2) % 4 in DVE_COPIES:
                            copy_turned(e, e.tensor_copy, b, odd, h - 2)
                    elif not first:
                        if (h - 2) % 4 in DVE_COPIES:
                            copy_turned(e, e.tensor_copy, b - 1, 1 - odd, HX - 2 + h)
                    if h == 4 and not first:
                        copy_oT(b - 1)
                    if h == 6 and not first:
                        accumulate(b - 1)
                if not first:
                    e.wait_ge(sem("alpha"), b)
                e.wait_ge(sem("maxed"), (b + 1) * HX)
                e.tensor_tensor(max_step[:], neg_max[:, odd, :], neg_max[:, 1 - odd, :], ALU.subtract).then_inc(sem("stepped"), 1)

            def copy_oT(b):
                e.wait_ge(sem("valued"), (b + 1) * 4)
                if not (isinstance(b, int) and b == 0):
                    e.wait_ge(sem("o_turned"), b)
                e.tensor_copy(oT[:].rearrange("p g n -> p (g n)"), p_oT[:]).then_inc(sem("oT_copied"), 1)

            def accumulate(b):
                e.wait_ge(sem("alpha"), b + 1)
                if not (isinstance(b, int) and b == 0):
                    e.wait_ge(sem("added"), b)
                a = acc[:, :, 0:HD + 1]
                e.tensor_tensor(a, a, alpha[:].unsqueeze(2).broadcast_to([P, HX, HD + 1]), ALU.mult).then_inc(sem("scaled"), 1)
                e.wait_ge(sem("scaled"), b + 1)
                e.wait_ge(sem("o_turned"), b + 1)
                e.tensor_tensor(a, a, p_proj[:].rearrange("p (h d) -> p h d", h=HX)[:, :, 0:HD + 1], ALU.add).then_inc(sem("added"), 1)

            over_blocks(e, body)
            for h in (HX - 2, HX - 1):
                if h % 4 in DVE_COPIES:
                    copy_turned(e, e.tensor_copy, LAST, LAST % 2, h)
            copy_oT(LAST)
            accumulate(LAST)
            e.wait_ge(sem("added"), LAST + 1)
            e.reciprocal(rsum[:], acc[:, :, HD]).then_inc(sem("rsum"), 1)
            e.wait_ge(sem("rsum"), 1)
            e.tensor_tensor(o[:].rearrange("p (h d) -> p h d", h=HX), acc[:, :, 0:HD],
                            rsum[:].unsqueeze(2).broadcast_to([P, HX, HD]), ALU.mult).then_inc(sem("rsum"), 1)
            e.wait_ge(sem("rsum"), 2)
            e.wait_ge(sem("out_weights"), 48 if has_wo else 16)
            e.tensor_tensor(o[:], o[:], bias_v[:], ALU.add).then_inc(sem("o_final"), 1)
            e.wait_ge(sem("o_final"), 1)
            if has_wo:
                e.wait_ge(sem("o2_turned"), 1)
                e.tensor_copy(o2T[:].rearrange("p c n -> p (c n)"), p_t[0][:, 0:D]).then_inc(sem("o2T_copied"), 1)
                e.tensor_tensor(x[:], x[:], bias_o[:], ALU.add).then_inc(sem("x_biased"), 1)
                e.wait_ge(sem("x_biased"), 1)
                e.wait_ge(sem("out_made"), 1)
                e.tensor_tensor(x[:], x[:], p_proj[:, 0:D], ALU.add)
            else:
                e.tensor_tensor(x[:], x[:], o[:], ALU.add)

    m.end()


def chain(e, sem):
    count = [0]

    def link(i):
        count[0] += 1
        i.then_inc(sem, 1)
        e.wait_ge(sem, count[0])

    return link


def norm_scratch(m, tag):
    return m.sb(f"{tag}_stats", [P, 6]), m.sb(f"{tag}_mean_var", [P, 2]), m.sb(f"{tag}_rstd", [P, 2])


def norm_vector(e, m, link, tag, scratch, src, out, eps=1e-5):
    stats, mean_var, rstd = scratch
    link(e.bn_stats(stats[:], src))
    link(e.bn_aggr(mean_var[:], stats[:]))
    e.tensor_scalar(rstd[:, 1:2], mean_var[:, 1:2], eps, None, ALU.add).then_inc(m.sem(f"{tag}_var"), 1)
    e.wait_ge(m.sem(f"{tag}_root"), 1)
    link(e.reciprocal(rstd[:, 1:2], rstd[:, 0:1]))
    e.tensor_scalar(out, src, mean_var[:, 0:1], rstd[:, 1:2], ALU.subtract, ALU.mult).then_inc(m.sem(f"{tag}_normed"), 1)


def norm_scalar(e, m, tag, scratch):
    rstd = scratch[2]
    e.wait_ge(m.sem(f"{tag}_var"), 1)
    e.activation(rstd[:, 0:1], rstd[:, 1:2], ACT.Sqrt).then_inc(m.sem(f"{tag}_root"), 1)


def turn_chunks(e, ident, bank, src, chunks=DC):
    for c in range(chunks):
        i = e.transpose(bank[:, c * P:(c + 1) * P], src[:, c * P:(c + 1) * P], ident[:])
    return i


def project_turned(e, bank, w, xT, chunks_out=DC, at=0):
    for oc in range(chunks_out):
        for c in range(DC):
            i = e.matmul(bank[:, at + oc * P:at + (oc + 1) * P], w[:, c, oc * P:(oc + 1) * P], xT[:, c, :],
                         start=c == 0, stop=c == DC - 1)
    return i


def project_rows(e, out, xT, w, chunks=DC):
    for c in range(chunks):
        i = e.matmul(out, xT[:, c, :], w[:, c, :], start=c == 0, stop=c == chunks - 1)
    return i


def chunked(w):
    return w.rearrange("(c p) n -> p c n", p=P)


def one_head_attention(nc, st, name, w, kind):
    m = Module(nc, name)
    sb, ps, sem = m.sb, m.ps, m.sem
    x, ident = st["x"], st["ident"]
    columns = kind == "columns"
    scale = float(D) ** -0.5
    scratch = norm_scratch(m, "ln")
    xn, xnT = sb("xn", [P, D]), sb("xnT", [P, DC, P])
    wq, wk, wv = (sb(n, [P, DC, D]) for n in ("wq", "wk", "wv"))
    bq, bk, bv = (sb("bq", [P, DC]), sb("bk", [P, DC]), sb("bv", [P, D])) if columns else (None, None, None)
    mask = sb("mask", [P, P])
    qT, kT, v = sb("qT", [P, DC, P]), sb("kT", [P, DC, P]), sb("v", [P, D])
    s, zero = sb("s", [P, P]), sb("zero", [P, P])
    top, low, total, inv = (sb(n, [P, 1]) for n in ("top", "low", "total", "inv"))
    prob, probT = sb("prob", [P, P]), sb("probT", [P, P])
    p_x, p_q, p_k, p_v, p_s, p_t, p_o = (ps(n) for n in ("p_x", "p_q", "p_k", "p_v", "p_s", "p_t", "p_o"))
    loads = [(wq, chunked(w["wq"])), (wk, chunked(w["wk"])), (wv, chunked(w["wv"])), (mask, w["mask"])]
    if columns:
        loads += [(bq, w["bq"]), (bk, w["bk"]), (bv, w["bv"])]

    with nc.Block() as block:

        @block.sync
        def _(e):
            for t, src in loads:
                e.dma_start(t[:], src).then_inc(sem("weights"), 16)

        @block.tensor
        def _(e):
            e.wait_ge(sem("ln_normed"), 1)
            turn_chunks(e, ident, p_x, xn).then_inc(sem("xn_turned"), 1)
            e.wait_ge(sem("xnT_copied"), 1)
            e.wait_ge(sem("weights"), 16 * len(loads))
            project_turned(e, p_q, wq, xnT)
            project_turned(e, p_k, wk, xnT).then_inc(sem("qk_made"), 1)
            project_rows(e, p_v[:, 0:D], xnT, wv).then_inc(sem("v_made"), 1)
            e.wait_ge(sem("q_copied"), 1)
            e.wait_ge(sem("k_copied"), 1)
            a, b = (kT, qT) if columns else (qT, kT)
            for c in range(DC):
                i = e.matmul(p_s[:, 0:P], a[:, c, :], b[:, c, :], start=c == 0, stop=c == DC - 1)
            i.then_inc(sem("scored"), 1)
            if columns:
                probs_by_key = prob
                e.wait_ge(sem("prob_scaled"), 1)
            else:
                probs_by_key = probT
                e.wait_ge(sem("exped"), 1)
                e.transpose(p_t[:, 0:P], prob[:], ident[:]).then_inc(sem("prob_turned"), 1)
                e.wait_ge(sem("probT_copied"), 1)
            e.wait_ge(sem("v_copied"), 1)
            e.matmul(p_o[:, 0:D], probs_by_key[:], v[:], start=True, stop=True).then_inc(sem("out_made"), 1)

        @block.scalar
        def _(e):
            norm_scalar(e, m, "ln", scratch)
            e.wait_ge(sem("qk_made"), 1)
            e.wait_ge(sem("weights"), 16 * len(loads))
            for c in range(DC):
                part = p_k[:, c * P:(c + 1) * P]
                i = e.activation(kT[:, c, :], part, ACT.Identity, bias=bk[:, c:c + 1]) if columns else \
                    e.copy(kT[:, c, :], part)
            i.then_inc(sem("k_copied"), 1)
            if not columns:
                e.wait_ge(sem("v_made"), 1)
                e.copy(v[:], p_v[:, 0:D]).then_inc(sem("v_copied"), 1)
            e.wait_ge(sem("low"), 1)
            e.activation(prob[:], s[:], ACT.Exp, bias=low[:, 0:1], accum_out=total[:]).then_inc(sem("exped"), 1)

        @block.vector
        def _(e):
            link = chain(e, sem("vector_chain"))
            norm_vector(e, m, link, "ln", scratch, x[:], xn[:])
            e.wait_ge(sem("xn_turned"), 1)
            e.tensor_copy(xnT[:].rearrange("p c n -> p (c n)"), p_x[:, 0:D]).then_inc(sem("xnT_copied"), 1)
            e.wait_ge(sem("qk_made"), 1)
            e.wait_ge(sem("weights"), 16 * len(loads))
            for c in range(DC):
                part = p_q[:, c * P:(c + 1) * P]
                i = e.tensor_scalar(qT[:, c, :], part, bq[:, c:c + 1], scale, ALU.add, ALU.mult) if columns else \
                    e.tensor_scalar(qT[:, c, :], part, scale, None, ALU.mult)
            i.then_inc(sem("q_copied"), 1)
            if columns:
                e.wait_ge(sem("v_made"), 1)
                e.tensor_tensor(v[:], p_v[:, 0:D], bv[:], ALU.add).then_inc(sem("v_copied"), 1)
            e.wait_ge(sem("scored"), 1)
            if columns:
                link(e.tensor_tensor(s[:], p_s[:, 0:P], mask[:], ALU.add))
            else:
                link(e.tensor_tensor(s[:], p_s[:, 0:P], mask[:], ALU.mult))
                link(e.tensor_scalar(zero[:], s[:], 0.0, -9e15, ALU.is_equal, ALU.mult))
                link(e.tensor_tensor(s[:], s[:], zero[:], ALU.add))
            link(e.tensor_reduce(top[:], s[:], AX, ALU.max))
            e.tensor_scalar(low[:], top[:], -1.0, None, ALU.mult).then_inc(sem("low"), 1)
            e.wait_ge(sem("exped"), 1)
            link(e.reciprocal(inv[:], total[:]))
            if columns:
                e.tensor_scalar(prob[:], prob[:], inv[:, 0:1], None, ALU.mult).then_inc(sem("prob_scaled"), 1)
                e.wait_ge(sem("out_made"), 1)
                e.tensor_tensor(x[:], x[:], p_o[:, 0:D], ALU.add)
            else:
                e.wait_ge(sem("prob_turned"), 1)
                e.tensor_copy(probT[:], p_t[:, 0:P]).then_inc(sem("probT_copied"), 1)
                e.wait_ge(sem("out_made"), 1)
                e.scalar_tensor_tensor(x[:], p_o[:, 0:D], inv[:, 0:1], x[:], ALU.mult, ALU.add)

    m.end()


def token_choice_experts(nc, st, name, w):
    m = Module(nc, name)
    sb, ps, sem = m.sb, m.ps, m.sem
    x, ident = st["x"], st["ident"]
    E, K, RING = 16, 64, 4
    scratch = norm_scratch(m, "ln")
    xn, xnT = sb("xn", [P, D]), sb("xnT", [P, DC, P])
    wg, bg = sb("wg", [P, DC, E]), sb("bg", [E, 1])
    b12, b3 = sb("b12", [P, 2, E]), sb("b3", [E, 1])
    w1, w2, w3 = (sb(n, [P, RING, DC, D]) for n in ("w1", "w2", "w3"))
    logits = sb("logits", [E, P])
    top, low, total, inv = (sb(n, [E, 1]) for n in ("top", "low", "total", "inv"))
    prob, left, taken, best = sb("prob", [E, P]), sb("left", [E, P]), sb("taken", [E, P]), sb("best", [E, 8])
    weight = sb("weight", [P, E])
    h1, h2 = sb("h1", [P, 2, DC, P]), sb("h2", [P, 2, DC, P])
    p_g, p_w = ps("p_g"), ps("p_w")
    p_h1, p_h2, p_y = ([ps(f"{n}{i}") for i in range(2)] for n in ("p_h1", "p_h2", "p_y"))

    with nc.Block() as block:

        @block.sync
        def _(e):
            for t, src in ((wg, chunked(w["wg"])), (bg, w["bg"]), (b12, w["b12"]), (b3, w["b3"])):
                e.dma_start(t[:], src).then_inc(sem("gate_weights"), 16)
            for x_ in range(E):
                if x_ >= RING:
                    e.wait_ge(sem("y_made"), x_ - RING + 1)
                for t, src in ((w1, w["w1"]), (w2, w["w2"]), (w3, w["w3"])):
                    e.dma_start(t[:, x_ % RING, :, :], chunked(src[x_])).then_inc(sem(f"expert_loaded_{x_ % RING}"), 16)

        @block.tensor
        def _(e):
            e.wait_ge(sem("ln_normed"), 1)
            turn_chunks(e, ident, p_w, xn).then_inc(sem("xn_turned"), 1)
            e.wait_ge(sem("xnT_copied"), 1)
            e.wait_ge(sem("gate_weights"), 64)
            for c in range(DC):
                i = e.matmul(p_g[0:E, 0:P], wg[:, c, :], xnT[:, c, :], start=c == 0, stop=c == DC - 1)
            i.then_inc(sem("gated"), 1)

            def layers(x_, k):
                r = x_ % 2
                if k == 1:
                    e.wait_ge(sem(f"expert_loaded_{x_ % RING}"), 48 * (x_ // RING + 1))
                    if x_ >= 2:
                        e.wait_ge(sem("h1_done"), x_ - 1)
                    project_turned(e, p_h1[r], w1[:, x_ % RING], xnT).then_inc(sem("h1_made"), 1)
                if k == 2:
                    e.wait_ge(sem("h1_done"), x_ + 1)
                    if x_ >= 2:
                        e.wait_ge(sem("h2_done"), x_ - 1)
                    project_turned(e, p_h2[r], w2[:, x_ % RING], h1[:, r]).then_inc(sem("h2_made"), 1)
                if k == 3:
                    e.wait_ge(sem("h2_done"), x_ + 1)
                    if x_ >= 2:
                        e.wait_ge(sem("y_added"), x_ - 1)
                    project_rows(e, p_y[r][:, 0:D], h2[:, r], w3[:, x_ % RING]).then_inc(sem("y_made"), 1)

            for n in range(E + 2):
                if n < E:
                    layers(n, 1)
                if 1 <= n <= E:
                    layers(n - 1, 2)
                if n == 2:
                    e.wait_ge(sem("taken"), 1)
                    e.transpose(p_w[:, 0:E], taken[:], ident[0:E, 0:E])
                    e.matmul(p_w[:, 32:33], taken[:], b3[:], start=True, stop=True).then_inc(sem("weight_turned"), 1)
                if n >= 2:
                    layers(n - 2, 3)

        @block.scalar
        def _(e):
            norm_scalar(e, m, "ln", scratch)
            e.wait_ge(sem("low"), 1)
            e.activation(prob[:], logits[:], ACT.Exp, bias=low[:, 0:1], accum_out=total[:]).then_inc(sem("exped"), 1)
            for x_ in range(E):
                e.wait_ge(sem("gate_weights"), 64)
                e.wait_ge(sem("h1_made"), x_ + 1)
                if x_ >= 2:
                    e.wait_ge(sem("h2_made"), x_ - 1)
                e.activation(h1[:, x_ % 2].rearrange("p c n -> p (c n)"), p_h1[x_ % 2][:, 0:D], ACT.Relu,
                             bias=b12[:, 0, x_:x_ + 1]).then_inc(sem("h1_done"), 1)
                e.wait_ge(sem("h2_made"), x_ + 1)
                if x_ >= 2:
                    e.wait_ge(sem("y_made"), x_ - 1)
                e.activation(h2[:, x_ % 2].rearrange("p c n -> p (c n)"), p_h2[x_ % 2][:, 0:D], ACT.Relu,
                             bias=b12[:, 1, x_:x_ + 1]).then_inc(sem("h2_done"), 1)

        @block.vector
        def _(e):
            link = chain(e, sem("vector_chain"))
            norm_vector(e, m, link, "ln", scratch, x[:], xn[:])
            e.wait_ge(sem("xn_turned"), 1)
            e.tensor_copy(xnT[:].rearrange("p c n -> p (c n)"), p_w[:, 0:D]).then_inc(sem("xnT_copied"), 1)
            e.wait_ge(sem("gated"), 1)
            e.wait_ge(sem("gate_weights"), 64)
            link(e.tensor_scalar(logits[:], p_g[0:E, 0:P], bg[:, 0:1], None, ALU.add))
            link(e.tensor_reduce(top[:], logits[:], AX, ALU.max))
            e.tensor_scalar(low[:], top[:], -1.0, None, ALU.mult).then_inc(sem("low"), 1)
            e.wait_ge(sem("exped"), 1)
            link(e.reciprocal(inv[:], total[:]))
            link(e.tensor_scalar(prob[:], prob[:], inv[:, 0:1], None, ALU.mult))
            for k in range(K // 8):
                src = prob if k == 0 else left
                link(e.max(best[:], src[:]))
                link(e.match_replace(left[:], best[:], src[:], -1.0))
            link(e.tensor_scalar(left[:], left[:], 0.0, None, ALU.is_lt))
            e.tensor_tensor(taken[:], prob[:], left[:], ALU.mult).then_inc(sem("taken"), 1)
            e.wait_ge(sem("weight_turned"), 1)
            link(e.tensor_copy(weight[:], p_w[:, 0:E]))
            link(e.tensor_scalar(x[:], x[:], p_w[:, 32:33], None, ALU.add))
            for x_ in range(E):
                e.wait_ge(sem("y_made"), x_ + 1)
                if x_:
                    e.wait_ge(sem("y_added"), x_)
                e.scalar_tensor_tensor(x[:], p_y[x_ % 2][:, 0:D], weight[:, x_:x_ + 1], x[:],
                                       ALU.mult, ALU.add).then_inc(sem("y_added"), 1)

    m.end()


def top_two_experts(nc, st, name, w):
    m = Module(nc, name)
    sb, ps, sem = m.sb, m.ps, m.sem
    x, ident = st["x"], st["ident"]
    E, H = 8, 512
    HC = H // P
    scratch, scratch2 = norm_scratch(m, "ln"), norm_scratch(m, "out")
    xn, xnT = sb("xn", [P, D]), sb("xnT", [P, DC, P])
    gate = sb("gate", [P, DC, E])
    w1 = sb("w1", [P, E, DC, H])
    w2 = sb("w2", [P, E, HC, D])
    b1 = sb("b1", [1, E, H])
    g1, b1n = sb("g1", [P, E, HC]), sb("b1n", [P, E, HC])
    b2 = sb("b2", [E, D])
    out_g, out_b = sb("out_g", [P, D]), sb("out_b", [P, D])
    ones = sb("ones", [1, P])
    logits, total, inv, low = sb("logits", [P, E]), sb("total", [P, 1]), sb("inv", [P, 1]), sb("low", [P, 1])
    gates, best, wanted = sb("gates", [P, 2 * E]), sb("best", [P, 8]), sb("wanted", [P, 8])
    left, chosen, weight = sb("left", [P, 2 * E]), sb("chosen", [P, E]), sb("weight", [P, E])
    weightT = sb("weightT", [E, P])
    h = sb("h", [P, E, H])
    stats, mean_var, rstd = sb("stats", [P, E, 6]), sb("mean_var", [P, E, 2]), sb("rstd", [P, 2, E])
    a = sb("a", [P, 2, HC, P])
    acc, y = sb("acc", [P, D]), sb("y", [P, D])
    p_x, p_g = ps("p_x"), ps("p_g")
    p_h, p_t, p_y = ([ps(f"{n}{i}") for i in range(2)] for n in ("p_h", "p_t", "p_y"))

    with nc.Block() as block:

        @block.sync
        def _(e):
            small = ((gate, chunked(w["gate"])), (b1, w["b1"]), (g1, w["g1"]), (b1n, w["b1n"]), (b2, w["b2"]),
                     (out_g, w["out_g"]), (out_b, w["out_b"]))
            for t, src in small:
                e.dma_start(t[:], src).then_inc(sem("small_weights"), 16)
            for x_ in range(E):
                e.dma_start(w1[:, x_], chunked(w["w1"][x_])).then_inc(sem(f"w1_loaded_{x_}"), 16)
            for x_ in range(E):
                e.dma_start(w2[:, x_], chunked(w["w2"][x_])).then_inc(sem(f"w2_loaded_{x_}"), 16)

        @block.gpsimd
        def _(e):
            e.memset(ones[:], 1.0).then_inc(sem("constants"), 1)
            for k in range(E):
                e.memset(gates[:, E + k:E + k + 1], -1.0 - k).then_inc(sem("constants"), 1)
            for k in range(8):
                e.memset(wanted[:, k:k + 1], -1.0 - k).then_inc(sem("constants"), 1)

        @block.tensor
        def _(e):
            e.wait_ge(sem("ln_normed"), 1)
            turn_chunks(e, ident, p_x, xn).then_inc(sem("xn_turned"), 1)
            e.wait_ge(sem("xnT_copied"), 1)
            e.wait_ge(sem("small_weights"), 112)
            project_rows(e, p_g[:, 0:E], xnT, gate).then_inc(sem("gated"), 1)
            e.wait_ge(sem("constants"), 1 + E + 8)
            for x_ in range(E):
                e.wait_ge(sem(f"w1_loaded_{x_}"), 16)
                if x_ >= 2:
                    e.wait_ge(sem("h_copied"), x_ - 1)
                e.matmul(p_h[x_ % 2][:], ones[:], b1[:, x_, :], start=True, stop=False)
                for c in range(DC):
                    i = e.matmul(p_h[x_ % 2][:], xnT[:, c, :], w1[:, x_, c, :], start=False, stop=c == DC - 1)
                i.then_inc(sem("h_made"), 1)
            e.wait_ge(sem("weighted"), 1)
            e.transpose(p_x[0:E, 0:P], weight[:], ident[:]).then_inc(sem("weight_turned"), 1)
            e.wait_ge(sem("weightT_copied"), 1)
            e.matmul(p_g[:, 0:D], weightT[:], b2[:], start=True, stop=True).then_inc(sem("b2_made"), 1)

            def second(x_):
                e.wait_ge(sem("activated"), x_ + 1)
                e.wait_ge(sem(f"w2_loaded_{x_}"), 16)
                if x_ >= 2:
                    e.wait_ge(sem("y_added"), x_ - 1)
                project_rows(e, p_y[x_ % 2][:, 0:D], a[:, x_ % 2], w2[:, x_], HC).then_inc(sem("y_made"), 1)

            for x_ in range(E):
                e.wait_ge(sem("h_normed"), x_ + 1)
                if x_ >= 2:
                    e.wait_ge(sem("activated"), x_ - 1)
                turn_chunks(e, ident, p_t[x_ % 2], h[:, x_], HC).then_inc(sem("h_turned"), 1)
                if x_ >= 1:
                    second(x_ - 1)
            second(E - 1)

        @block.scalar
        def _(e):
            norm_scalar(e, m, "ln", scratch)
            e.wait_ge(sem("low"), 1)
            e.activation(gates[:, 0:E], logits[:], ACT.Exp, bias=low[:, 0:1], accum_out=total[:]).then_inc(sem("exped"), 1)
            for x_ in range(E):
                e.wait_ge(sem("h_made"), x_ + 1)
                e.copy(h[:, x_], p_h[x_ % 2][:]).then_inc(sem("h_copied"), 1)
            e.wait_ge(sem("h_vars"), 1)
            e.activation(rstd[:, 0, :], rstd[:, 1, :], ACT.Sqrt).then_inc(sem("h_roots"), 1)
            e.wait_ge(sem("small_weights"), 112)
            for x_ in range(E):
                e.wait_ge(sem("h_turned"), x_ + 1)
                if x_ >= 2:
                    e.wait_ge(sem("y_made"), x_ - 1)
                for c in range(HC):
                    i = e.activation(a[:, x_ % 2, c, :], p_t[x_ % 2][:, c * P:(c + 1) * P], ACT.Gelu,
                                     bias=b1n[:, x_, c:c + 1], scale=g1[:, x_, c:c + 1])
                i.then_inc(sem("activated"), 1)
            norm_scalar(e, m, "out", scratch2)

        @block.vector
        def _(e):
            link = chain(e, sem("vector_chain"))
            norm_vector(e, m, link, "ln", scratch, x[:], xn[:])
            e.wait_ge(sem("xn_turned"), 1)
            e.tensor_copy(xnT[:].rearrange("p c n -> p (c n)"), p_x[:, 0:D]).then_inc(sem("xnT_copied"), 1)
            e.wait_ge(sem("gated"), 1)
            link(e.tensor_copy(logits[:], p_g[:, 0:E]))
            link(e.tensor_reduce(low[:], logits[:], AX, ALU.max))
            e.tensor_scalar(low[:], low[:], -1.0, None, ALU.mult).then_inc(sem("low"), 1)
            e.wait_ge(sem("exped"), 1)
            link(e.reciprocal(inv[:], total[:]))
            link(e.tensor_scalar(gates[:, 0:E], gates[:, 0:E], inv[:, 0:1], None, ALU.mult))
            e.wait_ge(sem("constants"), 1 + E + 8)
            link(e.max(best[:], gates[:, 0:E]))
            link(e.tensor_copy(wanted[:, 0:2], best[:, 0:2]))
            link(e.match_replace(left[:], wanted[:], gates[:], -100.0))
            link(e.tensor_scalar(chosen[:], left[:, 0:E], -50.0, None, ALU.is_lt))
            link(e.tensor_tensor(total[:], best[:, 0:1], best[:, 1:2], ALU.add))
            link(e.reciprocal(inv[:], total[:]))
            e.scalar_tensor_tensor(weight[:], gates[:, 0:E], inv[:, 0:1], chosen[:], ALU.mult, ALU.mult).then_inc(sem("weighted"), 1)
            for x_ in range(E):
                e.wait_ge(sem("h_copied"), x_ + 1)
                e.bn_stats(stats[:, x_], h[:, x_]).then_inc(sem("h_stats"), 1)
            e.wait_ge(sem("h_stats"), E)
            for x_ in range(E):
                e.bn_aggr(mean_var[:, x_], stats[:, x_]).then_inc(sem("h_aggr"), 1)
            e.wait_ge(sem("h_aggr"), E)
            e.tensor_scalar(rstd[:, 1, :], mean_var[:, :, 1], 1e-5, None, ALU.add).then_inc(sem("h_vars"), 1)
            e.wait_ge(sem("weight_turned"), 1)
            e.tensor_copy(weightT[:], p_x[0:E, 0:P]).then_inc(sem("weightT_copied"), 1)
            e.wait_ge(sem("b2_made"), 1)
            link(e.tensor_tensor(acc[:], xn[:], p_g[:, 0:D], ALU.add))
            e.wait_ge(sem("h_roots"), 1)
            link(e.reciprocal(rstd[:, 1, :], rstd[:, 0, :]))
            for x_ in range(E):
                e.tensor_scalar(h[:, x_], h[:, x_], mean_var[:, x_, 0:1], rstd[:, 1, x_:x_ + 1],
                                ALU.subtract, ALU.mult).then_inc(sem("h_normed"), 1)
            for x_ in range(E):
                e.wait_ge(sem("y_made"), x_ + 1)
                if x_:
                    e.wait_ge(sem("y_added"), x_)
                e.scalar_tensor_tensor(acc[:], p_y[x_ % 2][:, 0:D], weight[:, x_:x_ + 1], acc[:],
                                       ALU.mult, ALU.add).then_inc(sem("y_added"), 1)
            e.wait_ge(sem("y_added"), E)
            norm_vector(e, m, link, "out", scratch2, acc[:], y[:])
            e.wait_ge(sem("out_normed"), 1)
            e.wait_ge(sem("small_weights"), 112)
            link(e.tensor_tensor(y[:], y[:], out_g[:], ALU.mult))
            link(e.tensor_tensor(y[:], y[:], out_b[:], ALU.add))
            e.tensor_tensor(x[:], x[:], y[:], ALU.add)

    m.end()


TAPS = (3, 15, 31)
LEAD = max(TAPS) - 1


def delta_rule_attention(nc, st, name, w):
    m = Module(nc, name)
    sb, ps, sem = m.sb, m.ps, m.sem
    x, ident = st["x"], st["ident"]
    NH, HW = 4, 64
    LEVELS = 7
    H2 = 2 * D
    HC = H2 // P
    G = 3 * NH
    scratch = norm_scratch(m, "ln")
    xn, xnT = sb("xn", [P, D]), sb("xnT", [P, DC, P])
    wqkv = sb("wqkv", [P, 3, DC, D])
    wb = sb("wb", [P, DC, NH])
    short = sb("short", [P, 3, DC, 4])
    taps = [sb(f"taps{n}", [P, DC, n]) for n in TAPS]
    mix = sb("mix", [P, 2, 3, HW])
    mixer = sb("mixer", [P, DC, D])
    fw1, fw1b = sb("fw1", [P, DC, H2]), sb("fw1b", [G, H2])
    fb1 = sb("fb1", [P, HC])
    fw2, fb2 = sb("fw2", [P, HC, G]), sb("fb2", [P, G])
    onorm, wo = sb("onorm", [P, HW]), sb("wo", [P, DC, D])
    below = sb("below", [P, LEVELS, P])
    causalT = sb("causalT", [P, P])
    pre = sb("pre", [P, 3, DC, 3 + P])
    conv = sb("conv", [P, 3, DC, P])
    act = sb("act", [P, 3, DC, P])
    vpad = sb("vpad", [P, DC, LEAD + P])
    ms = sb("ms", [P, 3, DC, P])
    nat = sb("nat", [P, 3, NH, HW])
    sq, ss, root, scl = sb("sq", [P, 2, NH, HW]), sb("ss", [P, 2 * NH]), sb("root", [P, 2 * NH]), sb("scl", [P, 2 * NH])
    beta = sb("beta", [P, NH])
    kb, vb = sb("kb", [P, NH, HW]), sb("vb", [P, NH, HW])
    qT, kT, kbT = sb("qT", [P, DC, P]), sb("kT", [P, DC, P]), sb("kbT", [P, DC, P])
    AT, BT = sb("AT", [P, NH, P]), sb("BT", [P, NH, P])
    X, XT, Y = sb("X", [P, NH, P]), sb("XT", [P, NH, P]), sb("Y", [P, NH, P])
    locT = sb("locT", [P, NH, P])
    u = sb("u", [P, NH, HW])
    mixedT = sb("mixedT", [P, DC, P])
    branch = sb("branch", [P, 3, NH, HW])
    absmean = sb("absmean", [P, 3, NH])
    absT = sb("absT", [G, P])
    hid = sb("hid", [P, HC, P])
    lg, mx, den, inv = sb("lg", [P, NH, 3]), sb("mx", [P, NH]), sb("den", [P, NH]), sb("inv", [P, NH])
    wts = sb("wts", [P, NH, 3])
    o, part, oss, oinv = sb("o", [P, NH, HW]), sb("part", [P, NH, HW]), sb("oss", [P, NH]), sb("oinv", [P, 2, NH])
    oT = sb("oT", [P, DC, P])
    bank = [ps(f"bank{i}") for i in range(8)]
    flat = lambda t: t[:].rearrange("p a b -> p (a b)")
    loads = [(wqkv[:, i], chunked(w[n])) for i, n in enumerate(("Wq", "Wk", "Wv"))]
    loads += [(wb[:], chunked(w["Wb"])), (short[:], w["short"])]
    loads += [(t[:], w[f"ms{n}"]) for t, n in zip(taps, TAPS)]
    loads += [(mix[:], w["mix"]), (mixer[:], chunked(w["mixer"])), (fw1[:], chunked(w["fw1"][0:D, :])),
              (fw1b[:], w["fw1"][D:D + G, :]), (fb1[:], w["fb1"]), (fw2[:], chunked(w["fw2"])), (fb2[:], w["fb2"]),
              (onorm[:], w["onorm"]), (wo[:], chunked(w["Wo"])), (below[:], w["below"]), (causalT[:], w["causalT"])]
    ALL = 16 * len(loads)

    def half(h):
        return slice(HW * (h % 2), HW * (h % 2) + HW), h // 2

    with nc.Block() as block:

        @block.sync
        def _(e):
            for t, src in loads:
                e.dma_start(t, src).then_inc(sem("weights"), 16)

        @block.gpsimd
        def _(e):
            e.memset(pre[:, :, :, 0:3], 0.0).then_inc(sem("pads"), 1)
            e.memset(vpad[:, :, 0:LEAD], 0.0).then_inc(sem("pads"), 1)

        @block.tensor
        def _(e):
            e.wait_ge(sem("ln_normed"), 1)
            turn_chunks(e, ident, bank[0], xn).then_inc(sem("xn_turned"), 1)
            e.wait_ge(sem("xnT_copied"), 1)
            e.wait_ge(sem("weights"), ALL)
            for i in range(3):
                project_turned(e, bank[1 + i], wqkv[:, i], xnT).then_inc(sem("qkv_made"), 1)
            project_rows(e, bank[0][:, 0:NH], xnT, wb).then_inc(sem("beta_made"), 1)
            for i in range(3):
                e.wait_ge(sem("activated"), i + 1)
                for c in range(DC):
                    t = e.transpose(bank[4 + i // 2][:, (i % 2) * D + c * P:(i % 2) * D + (c + 1) * P],
                                    act[:, i, c, :], ident[:])
                t.then_inc(sem("qkv_turned"), 1)
            for n, (src, b) in enumerate(((nat[:, 1], 1), (kb[:], 2), (nat[:, 0], 3))):
                e.wait_ge(sem("rows_ready"), n + 1)
                turn_chunks(e, ident, bank[b], src.rearrange("p a b -> p (a b)")).then_inc(sem("rows_turned"), 1)
            e.wait_ge(sem("turned_copied"), 3)
            e.wait_ge(sem("branch_copied"), 1)
            for out, a, b in ((2, kT, kbT), (6, kT, qT)):
                for h in range(NH):
                    r, c = half(h)
                    t = e.matmul(bank[out + h % 2][:, (h // 2) * P:(h // 2 + 1) * P], a[r, c, :], b[r, c, :],
                                 start=True, stop=True)
                t.then_inc(sem("products"), 1)
            for level in range(LEVELS):
                e.wait_ge(sem("B_masked"), level + 1)
                for h in range(NH):
                    t = e.matmul(bank[4][:, h * P:(h + 1) * P], BT[:, h, :], X[:, h, :], start=True, stop=True)
                t.then_inc(sem("BX_made"), 1)
                e.wait_ge(sem("BX_copied"), level + 1)
                for h in range(NH):
                    t = e.matmul(bank[1][:, h * P:(h + 1) * P], XT[:, h, :], Y[:, h, :], start=True, stop=True)
                t.then_inc(sem("XBX_made"), 1)
                for h in range(NH):
                    t = e.matmul(bank[0][:, h * P:(h + 1) * P], Y[:, h, :], XT[:, h, :], start=True, stop=True)
                t.then_inc(sem("XBXT_made"), 1)
            e.wait_ge(sem("X_updated"), LEVELS)
            for h in range(NH):
                t = e.matmul(bank[4][:, h * HW:(h + 1) * HW], XT[:, h, :], vb[:, h, :], start=True, stop=True)
            t.then_inc(sem("u_made"), 1)
            e.wait_ge(sem("u_copied"), 1)
            for h in range(NH):
                t = e.matmul(bank[5][:, h * HW:(h + 1) * HW], locT[:, h, :], u[:, h, :], start=True, stop=True)
            t.then_inc(sem("delta_made"), 1)
            e.wait_ge(sem("ms_made"), 1)
            for unit in range(12):
                h, j, scale, chunk, side = unit // 3, unit % 3, unit // 4, unit // 2 % 2, unit % 2
                rows, c = half(h)
                t = e.matmul(bank[2][rows, c * P:(c + 1) * P], mix[:, side, j, :], ms[:, scale, chunk, :],
                             start=j == 0, stop=j == 2)
            t.then_inc(sem("mixed"), 1)
            e.wait_ge(sem("mixed_copied"), 1)
            project_rows(e, bank[3][:, 0:D], mixedT, mixer).then_inc(sem("ms_out"), 1)
            e.wait_ge(sem("means_made"), 1)
            e.transpose(bank[6][0:G, 0:P], absmean[:].rearrange("p a b -> p (a b)"), ident[:]).then_inc(sem("means_turned"), 1)
            e.wait_ge(sem("absT_copied"), 1)
            for oc in range(HC):
                for c in range(DC):
                    e.matmul(bank[7][:, oc * P:(oc + 1) * P], fw1[:, c, oc * P:(oc + 1) * P], xnT[:, c, :],
                             start=c == 0, stop=False)
                t = e.matmul(bank[7][:, oc * P:(oc + 1) * P], fw1b[:, oc * P:(oc + 1) * P], absT[:], start=False, stop=True)
            t.then_inc(sem("hid_made"), 1)
            e.wait_ge(sem("hid_done"), 1)
            project_rows(e, bank[0][:, 0:G], hid, fw2, HC).then_inc(sem("logits_made"), 1)
            e.wait_ge(sem("o_done"), 1)
            turn_chunks(e, ident, bank[1], flat(o)).then_inc(sem("o_turned"), 1)
            e.wait_ge(sem("oT_copied"), 1)
            project_rows(e, bank[2][:, 0:D], oT, wo).then_inc(sem("out_made"), 1)

        @block.scalar
        def _(e):
            norm_scalar(e, m, "ln", scratch)
            e.wait_ge(sem("pads"), 2)
            for i in range(3):
                e.wait_ge(sem("qkv_made"), i + 1)
                e.copy(pre[:, i, :, 3:3 + P], bank[1 + i][:, 0:D].rearrange("p (c n) -> p c n", c=DC)).then_inc(sem("pre_copied"), 1)
            e.wait_ge(sem("beta_made"), 1)
            e.activation(beta[:], bank[0][:, 0:NH], ACT.Sigmoid).then_inc(sem("beta_done"), 1)
            for i in range(3):
                e.wait_ge(sem("convolved"), i + 1)
                e.activation(act[:, i], conv[:, i], ACT.Sigmoid).then_inc(sem("sigmoids"), 1)
            e.wait_ge(sem("squares"), 1)
            e.activation(root[:], ss[:], ACT.Sqrt).then_inc(sem("roots"), 1)
            for n, (dst, b) in enumerate(((kT, 1), (kbT, 2), (qT, 3))):
                e.wait_ge(sem("rows_turned"), n + 1)
                e.copy(flat(dst), bank[b][:, 0:D]).then_inc(sem("turned_copied"), 1)
            e.wait_ge(sem("mixed"), 1)
            e.copy(flat(mixedT), bank[2][:, 0:D]).then_inc(sem("mixed_copied"), 1)
            e.wait_ge(sem("ms_out"), 1)
            e.copy(branch[:, 0].rearrange("p a b -> p (a b)"), bank[3][:, 0:D]).then_inc(sem("ms_copied"), 1)
            e.wait_ge(sem("hid_made"), 1)
            for c in range(HC):
                t = e.activation(hid[:, c, :], bank[7][:, c * P:(c + 1) * P], ACT.Gelu, bias=fb1[:, c:c + 1])
            t.then_inc(sem("hid_done"), 1)
            e.wait_ge(sem("lg_shifted"), 1)
            e.activation(wts[:], lg[:], ACT.Exp).then_inc(sem("wts_exp"), 1)
            e.wait_ge(sem("o_squares"), 1)
            e.activation(oinv[:, 0, :], oinv[:, 1, :], ACT.Sqrt).then_inc(sem("o_roots"), 1)

        @block.vector
        def _(e):
            link = chain(e, sem("vector_chain"))
            norm_vector(e, m, link, "ln", scratch, x[:], xn[:])
            e.wait_ge(sem("xn_turned"), 1)
            e.tensor_copy(flat(xnT), bank[0][:, 0:D]).then_inc(sem("xnT_copied"), 1)
            e.wait_ge(sem("weights"), ALL)
            for i in range(3):
                e.wait_ge(sem("pre_copied"), i + 1)
                for j in range(4):
                    for c in range(DC):
                        src, tap, dst = pre[:, i, c, j:j + P], short[:, i, c, j:j + 1], conv[:, i, c, :]
                        t = e.tensor_scalar(dst, src, tap, None, ALU.mult) if j == 0 else \
                            e.scalar_tensor_tensor(dst, src, tap, dst, ALU.mult, ALU.add)
                        if j < 3:
                            t.then_inc(sem("short_conv"), 1)
                        if j < 3 and c == DC - 1:
                            e.wait_ge(sem("short_conv"), 2 * (3 * i + j + 1))
                        if j == 3:
                            t.then_inc(sem("convolved_part"), 1)
                e.wait_ge(sem("convolved_part"), 2 * (i + 1))
                e.nop().then_inc(sem("convolved"), 1)
            for i in range(3):
                e.wait_ge(sem("sigmoids"), i + 1)
                e.tensor_tensor(act[:, i], act[:, i], conv[:, i], ALU.mult).then_inc(sem("activated"), 1)
            e.wait_ge(sem("activated"), 3)
            e.wait_ge(sem("pads"), 2)
            link(e.tensor_copy(vpad[:, :, LEAD:LEAD + P], act[:, 2]))
            e.wait_ge(sem("qkv_turned"), 2)
            qk = nat[:, 0:2].rearrange("p i h d -> p (i h d)")
            link(e.tensor_copy(qk, bank[4][:]))
            link(e.tensor_tensor(sq[:].rearrange("p i h d -> p (i h d)"), qk, qk, ALU.mult))
            link(e.tensor_reduce(ss[:], sq[:].rearrange("p i h d -> p (i h) d"), AX, ALU.add))
            e.tensor_scalar(ss[:], ss[:], 1e-6, None, ALU.add).then_inc(sem("squares"), 1)
            e.wait_ge(sem("qkv_turned"), 3)
            link(e.tensor_copy(branch[:, 2].rearrange("p a b -> p (a b)"), bank[5][:, 0:D]))
            e.nop().then_inc(sem("branch_copied"), 1)
            e.wait_ge(sem("roots"), 1)
            link(e.reciprocal(scl[:], root[:]))
            n8 = nat[:, 0:2].rearrange("p i h d -> p (i h) d")
            link(e.tensor_tensor(n8, n8, scl[:].unsqueeze(2).broadcast_to([P, 2 * NH, HW]), ALU.mult))
            e.nop().then_inc(sem("rows_ready"), 1)
            e.wait_ge(sem("beta_done"), 1)
            over = beta[:].unsqueeze(2).broadcast_to([P, NH, HW])
            e.tensor_tensor(kb[:], nat[:, 1], over, ALU.mult).then_inc(sem("rows_ready"), 1)
            link(e.tensor_tensor(vb[:], branch[:, 2], over, ALU.mult))
            e.nop().then_inc(sem("rows_ready"), 1)
            for n, (dst, out) in enumerate(((AT, 2), (locT, 6))):
                e.wait_ge(sem("products"), n + 1)
                for odd in range(2):
                    d = dst[:, odd:NH:2, :]
                    s = bank[out + odd][:, 0:D].rearrange("p (c n) -> p c n", c=2)
                    if n == 0:
                        link(e.tensor_copy(d, s))
                    else:
                        link(e.tensor_tensor(d, s, causalT[:].unsqueeze(1).broadcast_to([P, 2, P]), ALU.mult))
            idents = ident[:].unsqueeze(1).broadcast_to([P, NH, P])
            link(e.tensor_copy(X[:], idents))
            link(e.tensor_copy(XT[:], idents))
            for level in range(LEVELS):
                link(e.tensor_tensor(BT[:], AT[:], below[:, level, :].unsqueeze(1).broadcast_to([P, NH, P]), ALU.mult))
                e.nop().then_inc(sem("B_masked"), 1)
                e.wait_ge(sem("BX_made"), level + 1)
                e.tensor_copy(flat(Y), bank[4][:]).then_inc(sem("BX_copied"), 1)
                e.wait_ge(sem("XBX_made"), level + 1)
                e.wait_ge(sem("XBXT_made"), level + 1)
                link(e.tensor_tensor(flat(X), flat(X), bank[1][:], ALU.subtract))
                link(e.tensor_tensor(flat(XT), flat(XT), bank[0][:], ALU.subtract))
                e.nop().then_inc(sem("X_updated"), 1)
            e.wait_ge(sem("u_made"), 1)
            e.tensor_copy(flat(u), bank[4][:, 0:D]).then_inc(sem("u_copied"), 1)
            for s, (n, t) in enumerate(zip(TAPS, taps)):
                for j in range(n):
                    at = LEAD - (n - 1) + j
                    for c in range(DC):
                        src, tap, dst = vpad[:, c, at:at + P], t[:, c, j:j + 1], ms[:, s, c, :]
                        i = e.tensor_scalar(dst, src, tap, None, ALU.mult) if j == 0 else \
                            e.scalar_tensor_tensor(dst, src, tap, dst, ALU.mult, ALU.add)
                        i.then_inc(sem("ms_taps"), 1)
                    e.wait_ge(sem("ms_taps"), 2 * (sum(TAPS[:s]) + j + 1))
            e.nop().then_inc(sem("ms_made"), 1)
            e.wait_ge(sem("delta_made"), 1)
            link(e.tensor_copy(branch[:, 1].rearrange("p a b -> p (a b)"), bank[5][:, 0:D]))
            e.wait_ge(sem("ms_copied"), 1)
            b12 = branch[:].rearrange("p i h d -> p (i h) d")
            link(e.tensor_reduce(absmean[:].rearrange("p i h -> p (i h)"), b12, AX, ALU.add, apply_absolute_value=True))
            link(e.tensor_scalar(absmean[:], absmean[:], 1.0 / HW, None, ALU.mult))
            e.nop().then_inc(sem("means_made"), 1)
            e.wait_ge(sem("means_turned"), 1)
            e.tensor_copy(absT[:], bank[6][0:G, 0:P]).then_inc(sem("absT_copied"), 1)
            e.wait_ge(sem("logits_made"), 1)
            link(e.tensor_tensor(lg[:].rearrange("p h j -> p (h j)"), bank[0][:, 0:G], fb2[:], ALU.add))
            link(e.tensor_reduce(mx[:], lg[:], AX, ALU.max))
            e.tensor_tensor(lg[:], lg[:], mx[:].unsqueeze(2).broadcast_to([P, NH, 3]), ALU.subtract).then_inc(sem("lg_shifted"), 1)
            e.wait_ge(sem("wts_exp"), 1)
            link(e.tensor_reduce(den[:], wts[:], AX, ALU.add))
            link(e.reciprocal(inv[:], den[:]))
            link(e.tensor_tensor(wts[:], wts[:], inv[:].unsqueeze(2).broadcast_to([P, NH, 3]), ALU.mult))
            for j in range(3):
                ww = wts[:, :, j:j + 1].broadcast_to([P, NH, HW])
                if j == 0:
                    link(e.tensor_tensor(o[:], branch[:, j], ww, ALU.mult))
                else:
                    link(e.tensor_tensor(part[:], branch[:, j], ww, ALU.mult))
                    link(e.tensor_tensor(o[:], o[:], part[:], ALU.add))
            link(e.tensor_tensor(part[:], o[:], o[:], ALU.mult))
            link(e.tensor_reduce(oss[:], part[:], AX, ALU.add))
            e.tensor_scalar(oinv[:, 1, :], oss[:], 1.0 / HW, 1e-5, ALU.mult, ALU.add).then_inc(sem("o_squares"), 1)
            e.wait_ge(sem("o_roots"), 1)
            link(e.reciprocal(oinv[:, 1, :], oinv[:, 0, :]))
            link(e.tensor_tensor(o[:], o[:], oinv[:, 1, :].unsqueeze(2).broadcast_to([P, NH, HW]), ALU.mult))
            e.tensor_tensor(o[:], o[:], onorm[:].unsqueeze(1).broadcast_to([P, NH, HW]), ALU.mult).then_inc(sem("o_done"), 1)
            e.wait_ge(sem("o_turned"), 1)
            e.tensor_copy(flat(oT), bank[1][:, 0:D]).then_inc(sem("oT_copied"), 1)
            e.wait_ge(sem("out_made"), 1)
            e.tensor_tensor(x[:], x[:], bank[2][:, 0:D], ALU.add)

    m.end()


STEP = 256.0
MAGIC = 1.5 * 2.0 ** 23


def rounded_ffn(nc, st, name, w):
    m = Module(nc, name)
    sb, ps, sem = m.sb, m.ps, m.sem
    x, ident = st["x"], st["ident"]
    F = 1024
    FC = F // P
    scratch = norm_scratch(m, "ln")
    xn, xnT = sb("xn", [P, D]), sb("xnT", [P, DC, P])
    w1, w2 = sb("w1", [P, DC, F]), sb("w2", [P, FC, D])
    b1, b2 = sb("b1", [1, F]), sb("b2", [1, D])
    ones = sb("ones", [1, P])
    h, c, left, frac = sb("h", [P, F]), sb("c", [P, F]), sb("left", [P, 2, F]), sb("frac", [P, F])
    y, flag = sb("y", [P, 2, F]), sb("flag", [P, F])
    hT = sb("hT", [P, FC, P])
    out = sb("out", [P, D])
    p_x, p_o = ps("p_x"), ps("p_o")
    p_h = ps("p_h", [P, F])
    with nc.Block() as block:

        @block.sync
        def _(e):
            for t, src in ((w1, chunked(w["w1"])), (w2, chunked(w["w2"])), (b1, w["b1"]), (b2, w["b2"])):
                e.dma_start(t[:], src).then_inc(sem("weights"), 16)

        @block.gpsimd
        def _(e):
            e.memset(ones[:], 1.0).then_inc(sem("ones"), 1)

        @block.tensor
        def _(e):
            e.wait_ge(sem("ln_normed"), 1)
            turn_chunks(e, ident, p_x, xn).then_inc(sem("xn_turned"), 1)
            e.wait_ge(sem("xnT_copied"), 1)
            e.wait_ge(sem("weights"), 64)
            e.wait_ge(sem("ones"), 1)
            for fc in range(FC):
                f = slice(fc * P, (fc + 1) * P)
                for k in range(DC):
                    e.matmul(p_h[:, f], w1[:, k, f], xnT[:, k, :], start=k == 0, stop=False)
                i = e.matmul(p_h[:, f], b1[:, f], ones[:], start=False, stop=True)
            i.then_inc(sem("h_made"), 1)
            e.wait_ge(sem("h_done"), 1)
            for fc in range(FC):
                e.matmul(p_o[:, 0:D], hT[:, fc, :], w2[:, fc, :], start=fc == 0, stop=False)
            e.matmul(p_o[:, 0:D], ones[:], b2[:], start=False, stop=True).then_inc(sem("out_made"), 1)

        @block.scalar
        def _(e):
            norm_scalar(e, m, "ln", scratch)
            for k in range(2):
                e.wait_ge(sem("piece_ends"), k + 1)
                e.activation(y[:, k, :], left[:, k, :], ACT.Gelu).then_inc(sem("gelus"), 1)

        @block.vector
        def _(e):
            link = chain(e, sem("vector_chain"))
            norm_vector(e, m, link, "ln", scratch, x[:], xn[:])
            e.wait_ge(sem("xn_turned"), 1)
            e.tensor_copy(xnT[:].rearrange("p c n -> p (c n)"), p_x[:, 0:D]).then_inc(sem("xnT_copied"), 1)

            def rounded(dst, src):
                link(e.tensor_scalar(dst, src, STEP, MAGIC, ALU.mult, ALU.add))
                link(e.tensor_scalar(dst, dst, MAGIC, 1.0 / STEP, ALU.subtract, ALU.mult))

            e.wait_ge(sem("h_made"), 1)
            rounded(h[:], p_h[:])
            link(e.tensor_scalar(c[:], h[:], -4.0, 4.0, ALU.max, ALU.min))
            link(e.tensor_scalar(frac[:], c[:], 4.0, -63.0 / 128, ALU.mult, ALU.add))
            link(e.tensor_scalar(frac[:], frac[:], MAGIC, MAGIC, ALU.add, ALU.subtract))
            e.tensor_scalar(left[:, 0, :], frac[:], 0.25, None, ALU.mult).then_inc(sem("piece_ends"), 1)
            e.wait_ge(sem("piece_ends"), 1)
            e.tensor_scalar(left[:, 1, :], left[:, 0, :], 0.25, None, ALU.add).then_inc(sem("piece_ends"), 1)
            link(e.tensor_tensor(frac[:], c[:], left[:, 0, :], ALU.subtract))
            e.wait_ge(sem("gelus"), 2)
            link(e.tensor_tensor(y[:, 1, :], y[:, 1, :], y[:, 0, :], ALU.subtract))
            link(e.scalar_tensor_tensor(y[:, 1, :], frac[:], 4.0, y[:, 1, :], ALU.mult, ALU.mult))
            link(e.tensor_tensor(y[:, 0, :], y[:, 0, :], y[:, 1, :], ALU.add))
            link(e.scalar_tensor_tensor(flag[:], h[:], -4.0, y[:, 0, :], ALU.is_ge, ALU.mult))
            link(e.scalar_tensor_tensor(flag[:], h[:], 4.0, flag[:], ALU.is_le, ALU.mult))
            link(e.scalar_tensor_tensor(c[:], h[:], 4.0, h[:], ALU.is_gt, ALU.mult))
            link(e.tensor_tensor(c[:], c[:], flag[:], ALU.add))
            rounded(hT[:].rearrange("p c n -> p (c n)"), c[:])
            e.nop().then_inc(sem("h_done"), 1)
            e.wait_ge(sem("out_made"), 1)
            rounded(out[:], p_o[:, 0:D])
            e.tensor_tensor(x[:], x[:], out[:], ALU.add)

    m.end()


def window_attention(nc, st, name, w):
    m = Module(nc, name)
    sb, ps, sem = m.sb, m.ps, m.sem
    x, ident = st["x"], st["ident"]
    NH, HW = 4, 64
    scratch, scratch2 = norm_scratch(m, "ln"), norm_scratch(m, "ln2")
    xn, xa, xaT = sb("xn", [P, D]), sb("xa", [P, D]), sb("xaT", [P, DC, P])
    ln_w, ln_b = sb("ln_w", [P, D]), sb("ln_b", [P, D])
    wqkv, wo = sb("wqkv", [P, DC, 3 * D]), sb("wo", [P, DC, D])
    cos, sin = sb("cos", [P, HW]), sb("sin", [P, HW])
    mask = sb("mask", [P, P])
    qk = sb("qk", [P, 2 * NH, HW])
    turn, rot = sb("turn", [P, 2 * NH, HW]), sb("rot", [P, 2 * NH, HW])
    v = sb("v", [P, D])
    qkT = sb("qkT", [P, 4, P])
    s, top, low = sb("s", [P, NH, P]), sb("top", [P, NH]), sb("low", [P, NH])
    prob, probT = sb("prob", [P, NH, P]), sb("probT", [P, NH, P])
    total, inv = sb("total", [P, NH]), sb("inv", [P, NH])
    o, oT = sb("o", [P, NH, HW]), sb("oT", [P, DC, P])
    p_x, p_qk, p_v, p_t, p_o = (ps(n) for n in ("p_x", "p_qk", "p_v", "p_t", "p_o"))
    p_s = [ps(f"p_s{i}") for i in range(2)]
    loads = ((ln_w, w["ln_w"]), (ln_b, w["ln_b"]), (wqkv, chunked(w["wqkv"])), (wo, chunked(w["wo"])),
             (cos, w["cos"]), (sin, w["sin"]), (mask, w["mask"]))
    with nc.Block() as block:

        @block.sync
        def _(e):
            for t, src in loads:
                e.dma_start(t[:], src).then_inc(sem("weights"), 16)

        @block.tensor
        def _(e):
            e.wait_ge(sem("affine"), 1)
            turn_chunks(e, ident, p_x, xa).then_inc(sem("xa_turned"), 1)
            e.wait_ge(sem("xaT_copied"), 1)
            project_rows(e, p_qk[:], xaT, wqkv[:, :, 0:2 * D]).then_inc(sem("qk_made"), 1)
            project_rows(e, p_v[:, 0:D], xaT, wqkv[:, :, 2 * D:3 * D]).then_inc(sem("v_made"), 1)
            e.wait_ge(sem("rotated"), 1)
            turn_chunks(e, ident, p_t, rot[:].rearrange("p h d -> p (h d)"), 4).then_inc(sem("qk_turned"), 1)
            e.wait_ge(sem("qkT_copied"), 1)
            for h in range(NH):
                r = slice(HW * (h % 2), HW * (h % 2) + HW)
                i = e.matmul(p_s[h % 2][:, (h // 2) * P:(h // 2 + 1) * P], qkT[r, h // 2, :], qkT[r, 2 + h // 2, :],
                             start=True, stop=True)
            i.then_inc(sem("scored"), 1)
            e.wait_ge(sem("exped"), NH)
            for h in range(NH):
                i = e.transpose(p_x[:, h * P:(h + 1) * P], prob[:, h, :], ident[:])
            i.then_inc(sem("prob_turned"), 1)
            e.wait_ge(sem("probT_copied"), 1)
            e.wait_ge(sem("v_copied"), 1)
            for h in range(NH):
                i = e.matmul(p_o[:, h * HW:(h + 1) * HW], probT[:, h, :], v[:, h * HW:(h + 1) * HW], start=True, stop=True)
            i.then_inc(sem("valued"), 1)
            e.wait_ge(sem("o_done"), 1)
            turn_chunks(e, ident, p_t, o[:].rearrange("p h d -> p (h d)")).then_inc(sem("o_turned"), 1)
            e.wait_ge(sem("oT_copied"), 1)
            project_rows(e, p_v[:, 0:D], oT, wo).then_inc(sem("out_made"), 1)

        @block.scalar
        def _(e):
            norm_scalar(e, m, "ln", scratch)
            norm_scalar(e, m, "ln2", scratch2)
            e.wait_ge(sem("v_made"), 1)
            e.copy(v[:], p_v[:, 0:D]).then_inc(sem("v_copied"), 1)
            e.wait_ge(sem("low"), 1)
            for h in range(NH):
                e.activation(prob[:, h, :], s[:, h, :], ACT.Exp, bias=low[:, h:h + 1],
                             accum_out=total[:, h:h + 1]).then_inc(sem("exped"), 1)

        @block.vector
        def _(e):
            link = chain(e, sem("vector_chain"))
            norm_vector(e, m, link, "ln", scratch, x[:], xn[:])
            e.wait_ge(sem("ln_normed"), 1)
            norm_vector(e, m, link, "ln2", scratch2, xn[:], xa[:])
            e.wait_ge(sem("ln2_normed"), 1)
            e.wait_ge(sem("weights"), 16 * len(loads))
            link(e.tensor_tensor(xa[:], xa[:], ln_w[:], ALU.mult))
            e.tensor_tensor(xa[:], xa[:], ln_b[:], ALU.add).then_inc(sem("affine"), 1)
            e.wait_ge(sem("xa_turned"), 1)
            e.tensor_copy(xaT[:].rearrange("p c n -> p (c n)"), p_x[:, 0:D]).then_inc(sem("xaT_copied"), 1)
            e.wait_ge(sem("qk_made"), 1)
            link(e.tensor_copy(qk[:].rearrange("p h d -> p (h d)"), p_qk[:]))
            over = lambda t, a, b: t[:, a:b].unsqueeze(1).broadcast_to([P, 2 * NH, b - a])
            H = HW // 2
            link(e.tensor_tensor(turn[:, :, 0:H], qk[:, :, H:HW], over(sin, 0, H), ALU.mult))
            link(e.tensor_tensor(turn[:, :, H:HW], qk[:, :, 0:H], over(sin, H, HW), ALU.mult))
            link(e.tensor_tensor(rot[:], qk[:], over(cos, 0, HW), ALU.mult))
            e.tensor_tensor(rot[:], rot[:], turn[:], ALU.add).then_inc(sem("rotated"), 1)
            e.wait_ge(sem("qk_turned"), 1)
            e.tensor_copy(qkT[:].rearrange("p c n -> p (c n)"), p_t[:]).then_inc(sem("qkT_copied"), 1)
            e.wait_ge(sem("scored"), 1)
            for odd in range(2):
                link(e.scalar_tensor_tensor(s[:, odd:NH:2, :], p_s[odd][:, 0:D].rearrange("p (c n) -> p c n", c=2), float(HW) ** -0.5,
                                            mask[:].unsqueeze(1).broadcast_to([P, 2, P]), ALU.mult, ALU.add))
            link(e.tensor_reduce(top[:], s[:], AX, ALU.max))
            e.tensor_scalar(low[:], top[:], -1.0, None, ALU.mult).then_inc(sem("low"), 1)
            e.wait_ge(sem("prob_turned"), 1)
            e.tensor_copy(probT[:].rearrange("p h n -> p (h n)"), p_x[:]).then_inc(sem("probT_copied"), 1)
            e.wait_ge(sem("exped"), NH)
            link(e.reciprocal(inv[:], total[:]))
            e.wait_ge(sem("valued"), 1)
            e.tensor_tensor(o[:], p_o[:, 0:D].rearrange("p (h d) -> p h d", h=NH),
                            inv[:].unsqueeze(2).broadcast_to([P, NH, HW]), ALU.mult).then_inc(sem("o_done"), 1)
            e.wait_ge(sem("o_turned"), 1)
            e.tensor_copy(oT[:].rearrange("p c n -> p (c n)"), p_t[:, 0:D]).then_inc(sem("oT_copied"), 1)
            link(e.tensor_tensor(x[:], x[:], xn[:], ALU.add))
            e.wait_ge(sem("out_made"), 1)
            e.tensor_tensor(x[:], x[:], p_v[:, 0:D], ALU.add)

    m.end()


def nearest_expert(nc, st, name, w):
    m = Module(nc, name)
    sb, ps, sem = m.sb, m.ps, m.sem
    x, ident = st["x"], st["ident"]
    E, F, RING = 8, 1024, 4
    FC = F // P
    scratch, scratch2 = norm_scratch(m, "ln"), norm_scratch(m, "ln2")
    xn, xnT, xh, xhT = sb("xn", [P, D]), sb("xnT", [P, DC, P]), sb("xh", [P, D]), sb("xhT", [P, DC, P])
    cent = sb("cent", [P, DC, E])
    g, b = sb("g", [P, E, DC]), sb("b", [P, E, DC])
    b1, b2 = sb("b1", [P, E, FC]), sb("b2", [E, D])
    w1, w2 = sb("w1", [P, RING, DC, F]), sb("w2", [P, RING, FC, D])
    aff, best = sb("aff", [P, 2 * E]), sb("best", [P, 8])
    wanted, left, one = sb("wanted", [P, 8]), sb("left", [P, 2 * E]), sb("one", [P, E])
    alpha, weight, weightT = sb("alpha", [P, E]), sb("weight", [P, E]), sb("weightT", [E, P])
    xe = sb("xe", [P, 2, DC, P])
    h = sb("h", [P, 2, FC, P])
    p_x, p_g = ps("p_x"), ps("p_g")
    p_h = [ps(f"p_h{i}", [P, F]) for i in range(2)]
    p_y = [ps(f"p_y{i}") for i in range(2)]
    small = ((cent, chunked(w["cent"])), (g, w["g"]), (b, w["b"]), (b1, w["b1"]), (b2, w["b2"]))

    with nc.Block() as block:

        @block.sync
        def _(e):
            for t, src in small:
                e.dma_start(t[:], src).then_inc(sem("small_weights"), 16)
            for x_ in range(E):
                if x_ >= RING:
                    e.wait_ge(sem("y_made"), x_ - RING + 1)
                e.dma_start(w1[:, x_ % RING], chunked(w["w1"][x_])).then_inc(sem(f"expert_loaded_{x_ % RING}"), 16)
                e.dma_start(w2[:, x_ % RING], chunked(w["w2"][x_])).then_inc(sem(f"expert_loaded_{x_ % RING}"), 16)

        @block.tensor
        def _(e):
            e.wait_ge(sem("ln_normed"), 1)
            turn_chunks(e, ident, p_x, xn).then_inc(sem("xn_turned"), 1)
            e.wait_ge(sem("xnT_copied"), 1)
            e.wait_ge(sem("small_weights"), 16 * len(small))
            project_rows(e, p_g[:, 0:E], xnT, cent).then_inc(sem("aff_made"), 1)
            e.wait_ge(sem("ln2_normed"), 1)
            turn_chunks(e, ident, p_x, xh).then_inc(sem("xh_turned"), 1)

            def first(x_):
                e.wait_ge(sem(f"expert_loaded_{x_ % RING}"), 32 * (x_ // RING + 1))
                e.wait_ge(sem("xe_made"), x_ + 1)
                if x_ >= 2:
                    e.wait_ge(sem("h_low"), x_ - 1)
                    e.wait_ge(sem("h_high"), x_ - 1)
                project_turned(e, p_h[x_ % 2], w1[:, x_ % RING], xe[:, x_ % 2], FC).then_inc(sem("h_made"), 1)

            def second(x_):
                e.wait_ge(sem("h_low"), x_ + 1)
                e.wait_ge(sem("h_high"), x_ + 1)
                if x_ >= 2:
                    e.wait_ge(sem("y_added"), x_ - 1)
                project_rows(e, p_y[x_ % 2][:, 0:D], h[:, x_ % 2], w2[:, x_ % RING], FC).then_inc(sem("y_made"), 1)

            for n in range(E + 1):
                if n < E:
                    first(n)
                if n == 1:
                    e.wait_ge(sem("weighted"), 1)
                    e.transpose(p_x[0:E, 0:P], weight[:], ident[:]).then_inc(sem("weight_turned"), 1)
                    e.wait_ge(sem("weightT_copied"), 1)
                    e.matmul(p_g[:, 0:D], weightT[:], b2[:], start=True, stop=True).then_inc(sem("b2_made"), 1)
                if n >= 1:
                    second(n - 1)

        @block.gpsimd
        def _(e):
            for k in range(E):
                e.memset(aff[:, E + k:E + k + 1], -3.0e38 - k * 1e36).then_inc(sem("fillers"), 1)
            for k in range(8):
                e.memset(wanted[:, k:k + 1], -3.0e38 - k * 1e36).then_inc(sem("fillers"), 1)

        @block.scalar
        def _(e):
            norm_scalar(e, m, "ln", scratch)
            norm_scalar(e, m, "ln2", scratch2)
            e.wait_ge(sem("aff_copied"), 1)
            e.activation(alpha[:], aff[:, 0:E], ACT.Sigmoid).then_inc(sem("alpha_made"), 1)
            e.wait_ge(sem("small_weights"), 16 * len(small))
            for x_ in range(E):
                e.wait_ge(sem("h_made"), x_ + 1)
                if x_ >= 2:
                    e.wait_ge(sem("y_made"), x_ - 1)
                for fc in range(FC // 2):
                    i = e.activation(h[:, x_ % 2, fc, :], p_h[x_ % 2][:, fc * P:(fc + 1) * P], ACT.Relu, bias=b1[:, x_, fc:fc + 1])
                i.then_inc(sem("h_low"), 1)

        @block.vector
        def _(e):
            link = chain(e, sem("vector_chain"))
            norm_vector(e, m, link, "ln", scratch, x[:], xn[:])
            e.wait_ge(sem("xn_turned"), 1)
            e.tensor_copy(xnT[:].rearrange("p c n -> p (c n)"), p_x[:, 0:D]).then_inc(sem("xnT_copied"), 1)
            e.wait_ge(sem("ln_normed"), 1)
            norm_vector(e, m, link, "ln2", scratch2, xn[:], xh[:])
            e.wait_ge(sem("xh_turned"), 1)
            link(e.tensor_copy(xhT[:].rearrange("p c n -> p (c n)"), p_x[:, 0:D]))

            def affine(x_):
                if x_ >= 2:
                    e.wait_ge(sem("h_made"), x_ - 1)
                for c in range(DC):
                    i = e.tensor_scalar(xe[:, x_ % 2, c, :], xhT[:, c, :], g[:, x_, c:c + 1], b[:, x_, c:c + 1],
                                        ALU.mult, ALU.add)
                i.then_inc(sem("xe_made"), 1)

            def add_y(x_):
                e.wait_ge(sem("y_made"), x_ + 1)
                if x_:
                    e.wait_ge(sem("y_added"), x_)
                e.scalar_tensor_tensor(x[:], p_y[x_ % 2][:, 0:D], weight[:, x_:x_ + 1], x[:],
                                       ALU.mult, ALU.add).then_inc(sem("y_added"), 1)

            e.wait_ge(sem("small_weights"), 16 * len(small))
            affine(0)
            affine(1)
            e.wait_ge(sem("aff_made"), 1)
            e.wait_ge(sem("fillers"), 16)
            e.tensor_copy(aff[:, 0:E], p_g[:, 0:E]).then_inc(sem("aff_copied"), 1)
            e.wait_ge(sem("aff_copied"), 1)
            link(e.max(best[:], aff[:, 0:E]))
            link(e.tensor_copy(wanted[:, 0:1], best[:, 0:1]))
            link(e.match_replace(left[:], wanted[:], aff[:], 3.0e38))
            link(e.tensor_scalar(one[:], left[:, 0:E], 2.9e38, None, ALU.is_gt))
            e.wait_ge(sem("alpha_made"), 1)
            e.tensor_tensor(weight[:], one[:], alpha[:], ALU.mult).then_inc(sem("weighted"), 1)
            e.wait_ge(sem("weight_turned"), 1)
            e.tensor_copy(weightT[:], p_x[0:E, 0:P]).then_inc(sem("weightT_copied"), 1)
            link(e.tensor_tensor(x[:], x[:], xn[:], ALU.add))
            e.wait_ge(sem("b2_made"), 1)
            link(e.tensor_tensor(x[:], x[:], p_g[:, 0:D], ALU.add))
            for x_ in range(E):
                e.wait_ge(sem("h_made"), x_ + 1)
                if x_ >= 2:
                    e.wait_ge(sem("y_made"), x_ - 1)
                for fc in range(FC // 2, FC):
                    i = e.tensor_scalar(h[:, x_ % 2, fc, :], p_h[x_ % 2][:, fc * P:(fc + 1) * P], b1[:, x_, fc:fc + 1], 0.0,
                                        ALU.add, ALU.max)
                i.then_inc(sem("h_high"), 1)
                if x_ + 2 < E:
                    affine(x_ + 2)
                if x_ >= 1:
                    add_y(x_ - 1)
            add_y(E - 1)

    m.end()


def build(nc, a, modules=None):
    m = Module(nc, "net")
    st = {n: m.sb(n, shape) for n, shape in (("x", [P, D]), ("ident", [P, P]), ("head_rows", [P, HPC]))}
    with nc.Block() as block:
        @block.sync
        def _(e):
            e.dma_start(st["x"][:], a["x"]).then_inc(m.sem("loaded"), 16)
            e.dma_start(st["ident"][:], a["c_ident"]).then_inc(m.sem("loaded"), 16)
            e.dma_start(st["head_rows"][:], a["c_head_rows"]).then_inc(m.sem("loaded"), 16)
            e.wait_ge(m.sem("loaded"), 48)

    def L0_xattn():
        cross_attention(nc, st, "L0x", {"ctxT": a["ctxT"], "mask": a["mask_BxS2_ik0"], "wq": a["L0_xattn_q_w"],
                        "bq": a["L0_xattn_q_b"], "wk": a["L0_xattn_k_w"], "bk": a["L0_xattn_k_b"],
                        "wv": a["L0_xattn_v_w"], "bv": a["L0_xattn_v_b"]}, "int")

    def L1_xattn():
        cross_attention(nc, st, "L1x", {"ctxT": a["ctxT"], "mask": a["fside_SxS2_0"], "pad": a["fside_BxS2_0"],
                        "wq": a["L1_xattn_Wq"], "bq": a["L1_xattn_bq"], "wk": a["L1_xattn_Wk"],
                        "bk": a["L1_xattn_bk"], "wv": a["L1_xattn_Wv"], "bv": a["L1_xattn_bv"],
                        "wo": a["L1_xattn_Wo"], "bo": a["L1_xattn_bo"]}, "two")

    def L2_xattn():
        cross_attention(nc, st, "L2x", {"ctxT": a["ctxT"], "wq": a["L2_xattn_wq"], "bq": a["L2_xattn_bq"],
                        "wk": a["L2_xattn_wk"], "bk": a["L2_xattn_bk"], "wv": a["L2_xattn_wv"],
                        "bv": a["L2_xattn_bv"], "wo": a["L2_xattn_wo"], "bo": a["L2_xattn_bo"]}, None)

    def L3_xattn():
        cross_attention(nc, st, "L3x", {"ctxT": a["ctxT"], "mask": a["mask_Bx1x1xS2_fk0"], "wq": a["L3_xattn_Wq"],
                        "bq": a["L3_xattn_bq"], "wk": a["L3_xattn_Wk"], "bk": a["L3_xattn_bk"],
                        "wv": a["L3_xattn_Wv"], "bv": a["L3_xattn_bv"], "wo": a["L3_xattn_Wo"],
                        "bo": a["L3_xattn_bo"]}, "float")

    def L0_attn():
        one_head_attention(nc, st, "L0a", {"wq": a["L0_attn_Wq"], "bq": a["L0_attn_bq"], "wk": a["L0_attn_Wk"],
                           "bk": a["L0_attn_bk"], "wv": a["L0_attn_Wv"], "bv": a["L0_attn_bv"],
                           "mask": a["c_after"]}, "columns")

    def L2_attn():
        qkv = [a["L2_attn_W"][:, i * D:(i + 1) * D] for i in range(3)]
        one_head_attention(nc, st, "L2a", {"wq": qkv[0], "wk": qkv[1], "wv": qkv[2], "mask": a["c_upper"]}, "upper")

    def L0_ffn():
        token_choice_experts(nc, st, "L0f", {"wg": a["L0_ffn_Wg"], "bg": a["L0_ffn_bg"], "b12": a["L0_ffn_b12"],
                             "b3": a["L0_ffn_b3"], "w1": a["L0_ffn_w1"], "w2": a["L0_ffn_w2"], "w3": a["L0_ffn_w3"]})

    def L1_attn():
        w = {n: a[f"L1_attn_{n}"] for n in ("Wq", "Wk", "Wv", "Wb", "Wo", "short", "ms3", "ms15", "ms31", "mix")}
        w.update(mixer=a["L1_attn_channel_mixer_w"], fw1=a["L1_attn_fusion_w1"], fb1=a["L1_attn_fusion_b1"],
                 fw2=a["L1_attn_fusion_w2"], fb2=a["L1_attn_fusion_b2"], onorm=a["L1_attn_o_norm_w"],
                 below=a["c_below"], causalT=a["c_upper"])
        delta_rule_attention(nc, st, "L1a", w)

    def L1_ffn():
        top_two_experts(nc, st, "L1f", {"gate": a["L1_ffn_gate_w"], "w1": a["L1_ffn_w1"], "b1": a["L1_ffn_b1"],
                        "g1": a["L1_ffn_ln1_g"], "b1n": a["L1_ffn_ln1_b"], "w2": a["L1_ffn_w2"],
                        "b2": a["L1_ffn_b2"], "out_g": a["L1_ffn_ln_g"], "out_b": a["L1_ffn_ln_b"]})

    def L2_ffn():
        rounded_ffn(nc, st, "L2f", {n: a[f"L2_ffn_{n}"] for n in ("w1", "b1", "w2", "b2")})

    def L3_attn():
        window_attention(nc, st, "L3a", {"ln_w": a["L3_attn_ln_w"], "ln_b": a["L3_attn_ln_b"],
                         "wqkv": a["L3_attn_w_qkv"], "wo": a["L3_attn_w_out"], "cos": a["c_cos"],
                         "sin": a["c_sin"], "mask": a["c_window"]})

    def L3_ffn():
        nearest_expert(nc, st, "L3f", {"cent": a["L3_ffn_centroids"], "g": a["L3_ffn_ln_g"], "b": a["L3_ffn_ln_b"],
                       "w1": a["L3_ffn_w1"], "b1": a["L3_ffn_b1"], "w2": a["L3_ffn_w2"], "b2": a["L3_ffn_b2"]})

    every = {"L0_xattn": L0_xattn, "L0_attn": L0_attn, "L0_ffn": L0_ffn,
             "L1_xattn": L1_xattn, "L1_attn": L1_attn, "L1_ffn": L1_ffn,
             "L2_xattn": L2_xattn, "L2_attn": L2_attn, "L2_ffn": L2_ffn,
             "L3_xattn": L3_xattn, "L3_attn": L3_attn, "L3_ffn": L3_ffn}
    for n in modules or list(every):
        every[n]()
    with nc.Block() as block:
        @block.sync
        def _(e):
            e.dma_start(a["out"], st["x"][:]).then_inc(m.sem("stored"), 16)
            e.wait_ge(m.sem("stored"), 16)
    m.end()


def lay_out(inputs):
    a = {n: np.asarray(v) for n, v in inputs.items()}
    col = lambda v: np.ascontiguousarray(v.reshape(-1, P).T)
    row = lambda v: np.ascontiguousarray(np.broadcast_to(v.reshape(1, -1), (P, v.size)))
    T = lambda v: np.ascontiguousarray(np.swapaxes(v, -1, -2))
    out = {"x": a["x"][0], "ctxT": T(a["ctx_1024"][0])}
    out["mask_BxS2_ik0"] = a["mask_BxS2_ik0"]
    out["mask_Bx1x1xS2_fk0"] = a["mask_Bx1x1xS2_fk0"].reshape(1, NKEYS)
    out["fside_SxS2_0"], out["fside_BxS2_0"] = a["fside_SxS2_0"], a["fside_BxS2_0"]
    for n in ("L0_xattn_q_w", "L0_xattn_k_w", "L0_xattn_v_w"):
        out[n] = T(a[n])
    for n in ("L1_xattn_Wq", "L1_xattn_Wk", "L1_xattn_Wv", "L1_xattn_Wo", "L2_xattn_wq", "L2_xattn_wk",
              "L2_xattn_wv", "L2_xattn_wo", "L3_xattn_Wq", "L3_xattn_Wk", "L3_xattn_Wv", "L3_xattn_Wo"):
        out[n] = a[n]
    for n in ("L0_xattn_q_b", "L0_xattn_k_b", "L1_xattn_bq", "L1_xattn_bk", "L2_xattn_bq", "L2_xattn_bk",
              "L3_xattn_bq", "L3_xattn_bk"):
        out[n] = col(a[n])
    for n in ("L0_xattn_v_b", "L1_xattn_bv", "L1_xattn_bo", "L2_xattn_bv", "L2_xattn_bo", "L3_xattn_bv",
              "L3_xattn_bo"):
        out[n] = row(a[n])
    for n in ("L0_attn_Wq", "L0_attn_Wk", "L0_attn_Wv", "L3_attn_w_qkv", "L3_attn_w_out", "L3_ffn_centroids",
              "L3_ffn_w1", "L3_ffn_w2"):
        out[n] = T(a[n])
    for n in ("L0_ffn_Wg", "L0_ffn_w1", "L0_ffn_w2", "L0_ffn_w3", "L0_ffn_b3", "L1_attn_Wq", "L1_attn_Wk",
              "L1_attn_Wv", "L1_attn_Wb", "L1_attn_Wo", "L1_attn_channel_mixer_w", "L1_attn_fusion_w1",
              "L1_attn_fusion_w2", "L1_ffn_gate_w", "L1_ffn_w1", "L1_ffn_w2", "L1_ffn_b2", "L2_attn_W",
              "L2_ffn_w1", "L2_ffn_w2", "L3_ffn_b2"):
        out[n] = a[n]
    for n in ("L0_attn_bq", "L0_attn_bk", "L1_attn_fusion_b1"):
        out[n] = col(a[n])
    for n in ("L0_attn_bv", "L1_attn_fusion_b2", "L1_attn_o_norm_w", "L1_ffn_ln_g", "L1_ffn_ln_b",
              "L3_attn_ln_w", "L3_attn_ln_b"):
        out[n] = row(a[n])
    per_expert = lambda v: v.reshape(v.shape[0], -1, P).transpose(2, 0, 1)
    for n in ("L1_ffn_ln1_g", "L1_ffn_ln1_b", "L3_ffn_ln_g", "L3_ffn_ln_b", "L3_ffn_b1"):
        out[n] = per_expert(a[n])
    channels = lambda v: v.reshape(DC, P, -1).transpose(1, 0, 2)
    out["L1_attn_short"] = np.stack([channels(a[f"L1_attn_conv_{n}_w"]) for n in "qkv"], axis=1)
    for n in (3, 15, 31):
        out[f"L1_attn_ms{n}"] = channels(a[f"L1_attn_ms_w{n}"])
    mix = a["L1_attn_kernel_mix_w"].reshape(3, 64, 64).transpose(1, 0, 2)
    out["L1_attn_mix"] = np.zeros((P, 2, 3, 64), np.float32)
    out["L1_attn_mix"][:64, 0], out["L1_attn_mix"][64:, 1] = mix, mix
    out["L0_ffn_bg"] = a["L0_ffn_bg"].reshape(16, 1)
    out["L0_ffn_b12"] = np.broadcast_to(np.stack([a["L0_ffn_b1"][:, 0], a["L0_ffn_b2"][:, 0]])[None], (P, 2, 16))
    out["L1_ffn_b1"] = a["L1_ffn_b1"][None]
    out["L2_ffn_b1"], out["L2_ffn_b2"] = a["L2_ffn_b1"][None], a["L2_ffn_b2"][None]
    i = np.arange(P)
    out["c_after"] = np.where(i[None, :] >= i[:, None], 0.0, -BIG).astype(np.float32)
    out["c_upper"] = (i[None, :] >= i[:, None]).astype(np.float32)
    gap = i[:, None] - i[None, :]
    out["c_window"] = np.where((gap >= 0) & (gap < 32), 0.0, -BIG).astype(np.float32)
    out["c_below"] = np.stack([((i[None, :] // (2 * s) == i[:, None] // (2 * s)) & (i[None, :] % (2 * s) >= s)
                                & (i[:, None] % (2 * s) < s)) for s in (1, 2, 4, 8, 16, 32, 64)],
                              axis=1).astype(np.float32)
    inv = (1.0 / 10000.0 ** (np.arange(0, 64, 2, dtype=np.float32) / 64)).astype(np.float32)
    angle = i.astype(np.float32)[:, None] * np.concatenate([inv, inv])[None, :]
    out["c_cos"] = np.cos(angle).astype(np.float32)
    out["c_sin"] = (np.sin(angle) * np.repeat([-1.0, 1.0], 32)).astype(np.float32)
    out["c_ident"] = np.eye(P, dtype=np.float32)
    out["c_head_rows"] = np.repeat(np.eye(HPC, dtype=np.float32), HD, axis=0)
    return {n: np.ascontiguousarray(v) for n, v in out.items()}


def kernel(**inputs):
    import concourse.bacc as bacc
    from concourse.bass_utils import run_bass_kernel_spmd

    nc = bacc.Bacc("TRN2", target_bir_lowering=False, num_devices=1)
    arrays = lay_out(inputs)
    a = {n: nc.dram_tensor(f"in_{n}", list(v.shape), mybir.dt.from_np(v.dtype), kind="ExternalInput").ap()
         for n, v in arrays.items()}
    a["out"] = nc.dram_tensor("out_x", [P, D], F32, kind="ExternalOutput").ap()
    build(nc, a)
    r = run_bass_kernel_spmd(nc, [{f"in_{n}": v for n, v in arrays.items()}], core_ids=[0])
    return r.results[0]["out_x"].reshape(1, P, D)
```

```python
from contextlib import ExitStack

import numpy as np
import concourse.bass as bass
from concourse import mybir

F32 = mybir.dt.float32
I32 = mybir.dt.int32
F32R = mybir.dt.float32r
ALU = mybir.AluOpType
ACT = mybir.ActivationFunctionType
AX = mybir.AxisListType.X

P = 128
D = 256
DC = D // P
NKEYS = 12544
HX = 16
HD = D // HX
HPC = P // HD
BIG = 1e30


class Module:

    def __init__(self, nc, name):
        self.nc, self.name, self.stack, self.sems = nc, name, ExitStack(), {}

    def sb(self, name, shape, dtype=F32):
        return self.stack.enter_context(self.nc.sbuf_tensor(f"{self.name}_{name}", shape, dtype))

    def ps(self, name, shape=(P, 512), dtype=F32):
        return self.stack.enter_context(self.nc.psum_tensor(f"{self.name}_{name}", list(shape), dtype))

    def sem(self, name):
        if name not in self.sems:
            self.sems[name] = self.nc.alloc_semaphore(f"{self.name}_{name}")
        return self.sems[name]

    def end(self):
        self.nc.clear_and_free_semaphores(list(self.sems.values()))
        self.nc.all_engine_barrier()
        self.stack.close()


KB = 512
NBLK = NKEYS // KB
TAIL = NKEYS - NBLK * KB
S_RING = 4
T_RING = 2
P_RING = 8
PT_RING = 8
TURN_LAG = 4
COPY_LAG = 3
VALUE_LAGS = (9, 10)
PROJECT_STEPS = {1: ((0, 1),), 4: ((1, 1),), 11: ((2, 0), (2, 1)), 14: ((3, 0),), 15: ((3, 1),)}
PROJ_COPY_STEPS = (0, 4, 12, 15)
K_LOW_STEPS = (1, 5)
ALPHA_STEP, OT_COPY_STEP, OUT_STEP, ADD_STEP = 0, 6, 8, 7
DRAIN = 10
VW = 32
DVE_COPIES = (1, 5, 9, 13)


def cross_attention(nc, st, name, w, mask_kind):
    m = Module(nc, name)
    sb, ps, sem = m.sb, m.ps, m.sem
    x, ident = st["x"], st["ident"]
    has_wo = "wo" in w

    xn = sb("xn", [P, D])
    stats = sb("stats", [P, 6])
    mean_var = sb("mean_var", [P, 2])
    rstd = sb("rstd", [P, 2])
    xnT = sb("xnT", [P, DC, P])
    wq, wk, wv = (sb(n, [P, DC, D]) for n in ("wq", "wk", "wv"))
    wo = sb("wo", [P, DC, D]) if has_wo else None
    bias_k = sb("bias_k", [P, DC])
    bias_v = sb("bias_v", [P, D])
    bias_o = sb("bias_o", [P, D]) if has_wo else None
    wk_part, wv_part = sb("wk_part", [P, 2, DC, D], F32R), sb("wv_part", [P, 2, DC, D], F32R)
    SLOT = 2 * HD
    SLOTS = 3
    ROWS = SLOTS * SLOT
    PAIRS = P // SLOT
    bias_q = sb("bias_q", [ROWS, HX // 2])
    q_full = sb("q_full", [ROWS, HX // 2, P])
    q_stack = sb("q_stack", [ROWS, HX, P], F32R)
    k_stack = sb("k_stack", [P, 2, HX // 2, KB], F32R)
    ctx = sb("ctx", [P, 2, DC, KB])
    ctx_part = sb("ctx_part", [P, 2, 2, DC, KB], F32R)
    kT = sb("kT", [P, 2, 2, DC, KB], F32R)
    v = sb("v", [P, 2, KB // P, HX, VW])
    raw = sb("raw", [P, 2, KB], I32 if mask_kind == "int" else F32) if mask_kind else None
    pad = sb("pad", [P, 2, KB]) if mask_kind == "two" else None
    mask = sb("mask", [P, 2, KB]) if mask_kind else None
    block_max = sb("block_max", [P, HX])
    neg_max = sb("neg_max", [P, 2, HX])
    max_step = sb("max_step", [P, HX])
    alpha = sb("alpha", [P, HX])
    prob = sb("prob", [P, P_RING, KB])
    probT = sb("probT", [P, PT_RING, KB])
    oT = sb("oT", [P, 4, P])
    acc = sb("acc", [P, HX, VW])
    rsum = sb("rsum", [P, HX])
    o = sb("o", [P, D])
    o2T = sb("o2T", [P, DC, P])

    p_s = [ps(f"p_s{i}") for i in range(S_RING)]
    p_t = [ps(f"p_t{i}") for i in range(T_RING)]
    p_proj, p_oT = ps("p_proj"), ps("p_oT")

    HIGH, LOW = 0, 1
    PRODUCTS = ((HIGH, HIGH), (HIGH, LOW), (LOW, HIGH))
    STACKED = SLOTS * PAIRS * 16
    LAST = NBLK
    keys = lambda b: TAIL if isinstance(b, int) and b == LAST else KB

    def loads(b, odd):
        return b // 2 + 1 if isinstance(b, int) else (b - odd) // 2 + 1

    def in_register(eng, value):
        return value if isinstance(value, int) else eng.to_reg(value)

    def lagging(b, odd, step, lag):
        h = step - lag
        if h >= 0:
            return (b, odd, h) if h < HX else None
        return None if isinstance(b, int) and b == 0 or h < -HX else (b - 1, 1 - odd, h + HX)

    def over_blocks(eng, body, peeled=0):
        body(0, 0)
        body(1, 1)
        with eng.Fori(1, (NBLK - peeled) // 2) as pair:
            body(pair * 2, 0)
            body(pair * 2 + 1, 1)
        for b in range(NBLK - peeled, LAST + 1):
            body(b, b % 2)

    def copied(h):
        return "probT_copied_dve" if h % HX in DVE_COPIES else "probT_copied_act"

    def copies(b, h):
        mine = [i for i in range(HX) if copied(i) == copied(h)]
        return b * len(mine) + len([i for i in mine if i <= h]) if h >= 0 else \
            b * len(mine) - len([i for i in mine if i - HX > h])

    def copy_turned(e, copy, b, odd, h):
        nk = keys(b)
        e.wait_ge(sem("turned"), b * HX + h + 1)
        if not (isinstance(b, int) and b == 0 and h < PT_RING):
            e.wait_ge(sem("valued"), b * 4 + h // 4 - 1)
        copy(probT[:, h % PT_RING, 0:nk], p_t[h % T_RING][:, 0:nk]).then_inc(sem(copied(h)), 1)

    with nc.Block() as block:

        @block.sync
        def _(e):
            ctx_dram = w["ctxT"].rearrange("(c p) n -> p c n", p=P)

            def load(b, odd):
                nk = keys(b)
                late = not (isinstance(b, int) and b < 2)
                if late:
                    if isinstance(b, int) and b == 2:
                        e.wait_ge(sem("first_ctx_split"), 1)
                    else:
                        e.wait_ge(sem("ctx_split"), b - 2)
                e.dma_start(ctx[:, odd, :, 0:nk], ctx_dram[:, :, bass.ds(b * KB, nk)]).then_inc(sem(f"ctx_loaded_{odd}"), 16)
                if mask_kind:
                    if late:
                        e.wait_ge(sem("mask_made"), b - 1)
                    src = w["mask"]
                    if mask_kind == "two":
                        e.dma_start(raw[:, odd, 0:nk], src[:, bass.ds(b * KB, nk)]).then_inc(sem(f"mask_loaded_{odd}"), 16)
                        e.dma_start(pad[:, odd, 0:nk], w["pad"][:, bass.ds(b * KB, nk)].broadcast_to([P, nk])).then_inc(sem(f"mask_loaded_{odd}"), 16)
                    else:
                        e.dma_start(raw[:, odd, 0:nk], src[:, bass.ds(b * KB, nk)].broadcast_to([P, nk])).then_inc(sem(f"mask_loaded_{odd}"), 16)

            def stack_k(b, odd):
                nk = keys(b)
                split, used = in_register(e, b * 4 + 2), in_register(e, (b - 1) * HX)
                e.wait_ge(sem("proj_copied"), split)
                if not (isinstance(b, int) and b < 2):
                    e.wait_ge(sem("scored"), used)
                first = isinstance(b, int) and b == 0
                for pair in range(PAIRS):
                    for slot, (_, part) in enumerate(PRODUCTS):
                        e.dma_start(k_stack[slot * SLOT:(slot + 1) * SLOT, odd, pair::PAIRS, 0:nk].bitcast(F32),
                                    kT[pair * SLOT:(pair + 1) * SLOT, odd, part, :, 0:nk].bitcast(F32)
                                    ).then_inc(sem(f"first_k_stacked_{pair}" if first else f"k_stacked_{odd}"), 16)

            def body(b, odd):
                if not (isinstance(b, int) and b + 2 > LAST):
                    load(b + 2, odd)
                if not (isinstance(b, int) and b == LAST):
                    stack_k(b + 1, 1 - odd)

            e.dma_start(wk[:], w["wk"].rearrange("(c p) n -> p c n", p=P)).then_inc(sem("k_weights"), 16)
            load(0, 0)
            e.dma_start(wq[:], w["wq"].rearrange("(c p) n -> p c n", p=P)).then_inc(sem("q_weights"), 16)
            e.dma_start(bias_k[:], w["bk"]).then_inc(sem("k_bias"), 16)
            e.dma_start(bias_q[:], w["bq"]).then_inc(sem("q_weights"), 16)
            e.dma_start(wv[:], w["wv"].rearrange("(c p) n -> p c n", p=P)).then_inc(sem("v_weights"), 16)
            load(1, 1)
            stack_k(0, 0)
            e.dma_start(bias_v[:], w["bv"]).then_inc(sem("out_weights"), 16)
            if has_wo:
                e.dma_start(wo[:], w["wo"].rearrange("(c p) n -> p c n", p=P)).then_inc(sem("out_weights"), 16)
                e.dma_start(bias_o[:], w["bo"]).then_inc(sem("out_weights"), 16)
            over_blocks(e, body, peeled=2)

        @block.gpsimd
        def _(e):
            e.memset(v[:], 0.0).then_inc(sem("v_zero"), 1)
            e.wait_ge(sem("v_zero"), 1)
            e.memset(v[:, :, :, :, HD:HD + 1], 1.0).then_inc(sem("v_ones"), 1)

            def split_ctx(b, odd):
                nk = keys(b)
                e.wait_ge(sem(f"ctx_loaded_{odd}"), loads(b, odd) * 16)
                if not (isinstance(b, int) and b < 2):
                    used = in_register(e, (b - 1) * 4)
                    e.wait_ge(sem("v_ones"), 1)
                    e.wait_ge(sem("projected"), used)
                high, low = ctx_part[:, odd, HIGH, :, 0:nk], ctx_part[:, odd, LOW, :, 0:nk]
                e.tensor_copy(high, ctx[:, odd, :, 0:nk]).then_inc(sem("ctx_high"), 1)
                e.wait_ge(sem("ctx_high"), b)
                e.tensor_tensor(low, ctx[:, odd, :, 0:nk], high.bitcast(F32), ALU.subtract).then_inc(sem("ctx_split"), 1)

            def make_mask(b, odd):
                nk = keys(b)
                e.wait_ge(sem(f"mask_loaded_{odd}"), loads(b, odd) * (32 if mask_kind == "two" else 16))
                if not (isinstance(b, int) and b < 2):
                    used = in_register(e, (b - 1) * HX)
                    e.wait_ge(sem("v_ones"), 1)
                    e.wait_ge(sem("maxed"), used)
                r, q = raw[:, odd, 0:nk], mask[:, odd, 0:nk]
                if mask_kind == "int":
                    i = e.tensor_scalar(q, r, 0.0, -BIG, ALU.is_gt, ALU.mult)
                elif mask_kind == "float":
                    i = e.tensor_scalar(q, r, -1e9, None, ALU.mult)
                else:
                    i = e.tensor_tensor(q, r, pad[:, odd, 0:nk], ALU.add)
                i.then_inc(sem("mask_made"), 1)

            def body(b, odd):
                if not (isinstance(b, int) and b == LAST):
                    split_ctx(b + 1, 1 - odd)
                if mask_kind:
                    make_mask(b, odd)

            over_blocks(e, body)

        @block.tensor
        def _(e):
            e.wait_ge(sem("normed"), 1)
            for c in range(DC):
                i = e.transpose(p_t[0][:, c * P:(c + 1) * P], xn[:, c * P:(c + 1) * P], ident[:])
            i.then_inc(sem("xn_turned"), 1)

            def project(b, odd, part, half=None):
                nk = keys(b)
                halves = (0, 1) if half is None or part < 2 else (half,)
                if part == 0 and not (isinstance(b, int) and b == 0):
                    e.wait_ge(sem("ctx_split"), b)
                if 0 in halves and not (isinstance(b, int) and b == 0 and part == 0):
                    e.wait_ge(sem("proj_copied"), b * 4 + part)
                if part == 2 and 0 in halves and not (isinstance(b, int) and b < 2):
                    e.wait_ge(sem("added"), b - 1)
                steps = [(a, c, c == 0 and a == PRODUCTS[0], c == DC - 1 and a == PRODUCTS[-1])
                         for a in PRODUCTS for c in range(DC)]
                if part < 2:
                    for (wp, cp), c, start, stop in steps:
                        i = e.matmul(p_proj[:, 0:nk], wk_part[:, wp, c, part * P:(part + 1) * P],
                                     ctx_part[:, odd, cp, c, 0:nk], start=start, stop=stop)
                if part >= 2:
                    i = None
                    for t in halves:
                        k0 = ((part - 2) * 2 + t) * P
                        if k0 < nk:
                            for (wp, cp), c, start, stop in steps:
                                i = e.matmul(p_proj[:, t * D:(t + 1) * D], ctx_part[:, odd, cp, c, k0:k0 + P],
                                             wv_part[:, wp, c, :], start=start, stop=stop)
                if 1 in halves:
                    if i is None:
                        e.nop().then_inc(sem("projected"), 1)
                    else:
                        i.then_inc(sem("projected"), 1)

            def scores(b, odd, h):
                nk = keys(b)
                if not (isinstance(b, int) and b == 0 and h < S_RING):
                    e.wait_ge(sem("exped"), b * HX + h - S_RING + 1)
                e.matmul(p_s[h % S_RING][:, 0:nk], q_stack[0:ROWS, h, :], k_stack[0:ROWS, odd, h // 2, 0:nk],
                         start=True, stop=True).then_inc(sem("scored"), 1)

            def turn(b, odd, h):
                nk = keys(b)
                e.wait_ge(sem("exped"), b * HX + h + 1)
                if not (isinstance(b, int) and b == 0 and h < T_RING):
                    e.wait_ge(sem(copied(h - T_RING)), copies(b, h - T_RING))
                for t in range(nk // P):
                    i = e.transpose(p_t[h % T_RING][:, t * P:(t + 1) * P], prob[:, h % P_RING, t * P:(t + 1) * P], ident[:])
                i.then_inc(sem("turned"), 1)

            def values(b, odd, g, half):
                nk = keys(b)
                nt = nk // P // 2
                if half == 0 and g == 0:
                    e.wait_ge(sem("proj_copied"), (b + 1) * 4)
                if half == 0 and g == 0 and not (isinstance(b, int) and b == 0):
                    e.wait_ge(sem("oT_copied"), b)
                last_of = {copied(h): h for h in range(4 * g, 4 * g + 4)}
                for h in last_of.values() if half == 0 else ():
                    e.wait_ge(sem(copied(h)), copies(b, h))
                for t in range(half * nt, half * nt + nt):
                    for s in range(4):
                        h = 4 * g + s
                        i = e.matmul(p_oT[VW * s:VW * s + VW, g * P:(g + 1) * P], v[:, odd, t, h, :],
                                     probT[:, h % PT_RING, t * P:(t + 1) * P], start=t == 0, stop=t == nk // P - 1)
                if half == 1:
                    i.then_inc(sem("valued"), 1)

            def turn_out(b, projected):
                e.wait_ge(sem("oT_copied"), b + 1)
                e.wait_ge(sem("proj_copied"), projected)
                if not (isinstance(b, int) and b == 0):
                    e.wait_ge(sem("added"), b)
                for g in range(4):
                    i = e.transpose(p_proj[:, g * P:(g + 1) * P], oT[:, g, :], ident[:])
                i.then_inc(sem("o_turned"), 1)

            def behind(b, odd, step):
                at = lagging(b, odd, step, TURN_LAG)
                if at:
                    turn(*at)
                for half, lag in enumerate(VALUE_LAGS):
                    at = lagging(b, odd, step, lag)
                    if at and at[2] % 4 == 0:
                        values(at[0], at[1], at[2] // 4, half)
                if step % HX == OUT_STEP:
                    at = lagging(b, odd, step, HX + OUT_STEP)
                    if at:
                        turn_out(at[0], 4 * NBLK + 4 if step > HX or isinstance(b, int) and b == LAST else 4 * b + 6)

            def body(b, odd):
                last = isinstance(b, int) and b == LAST
                for h in range(HX):
                    if isinstance(b, int) and b == 0:
                        if h % 2 == 0 and h < HPC:
                            e.wait_ge(sem(f"first_k_stacked_{h // 2}"), SLOTS * 16)
                    elif h == 0:
                        e.wait_ge(sem(f"k_stacked_{odd}"), (loads(b, odd) - (1 - odd)) * STACKED)
                    scores(b, odd, h)
                    behind(b, odd, h)
                    for part, half in PROJECT_STEPS.get(h, ()) if not last else ():
                        project(b + 1, 1 - odd, part, half)

            def project_q(pairs):
                for pair in pairs:
                    for slot in range(SLOTS):
                        for c in range(DC):
                            i = e.matmul(p_t[pair // 4][slot * SLOT:(slot + 1) * SLOT, pair % 4 * P:(pair % 4 + 1) * P],
                                         wq[:, c, pair * SLOT:(pair + 1) * SLOT], xnT[:, c, :], start=c == 0, stop=c == DC - 1)
                i.then_inc(sem("q_made"), 1)

            e.wait_ge(sem("k_weights_split"), 1)
            e.wait_ge(sem("first_ctx_split"), 1)
            project(0, 0, 0)
            e.wait_ge(sem("q_weights"), 32)
            e.wait_ge(sem("xnT_copied"), 1)
            project_q(range(0, 4))
            project(0, 0, 1)
            project_q(range(4, 8))
            e.wait_ge(sem("v_weights_split"), 1)
            project(0, 0, 2)
            project(0, 0, 3)
            e.wait_ge(sem("q_stacked"), 2)
            over_blocks(e, body)
            for step in range(HX, HX + DRAIN):
                behind(LAST, LAST % 2, step)
            if has_wo:
                e.wait_ge(sem("o_final"), 1)
                for c in range(DC):
                    i = e.transpose(p_t[0][:, c * P:(c + 1) * P], o[:, c * P:(c + 1) * P], ident[:])
                i.then_inc(sem("o2_turned"), 1)
                e.wait_ge(sem("o2T_copied"), 1)
                e.wait_ge(sem("out_weights"), 48)
                for c in range(DC):
                    i = e.matmul(p_proj[:, 0:D], o2T[:, c, :], wo[:, c, :], start=c == 0, stop=c == DC - 1)
                i.then_inc(sem("out_made"), 1)

        @block.scalar
        def _(e):
            e.wait_ge(sem("stats"), 2)
            e.activation(rstd[:, 0:1], rstd[:, 1:2], ACT.Sqrt).then_inc(sem("root"), 1)

            def copy_proj(b, odd, part):
                nk = keys(b)
                e.wait_ge(sem("projected"), b * 4 + part + 1)
                if part < 2:
                    e.activation(kT[:, odd, HIGH, part, 0:nk], p_proj[:, 0:nk], ACT.Identity,
                                 bias=bias_k[:, part:part + 1]).then_inc(sem("k_high"), 1)
                    return
                else:
                    t0 = (part - 2) * 2
                    nt = min(2, max(nk // P - t0, 0))
                    if nt:
                        i = e.activation(v[:, odd, t0:t0 + nt, :, 0:HD],
                                         p_proj[:, 0:nt * D].rearrange("p (t h d) -> p t h d", t=nt, h=HX), ACT.Copy)
                    else:
                        i = e.nop()
                i.then_inc(sem("proj_copied"), 1)

            def body(b, odd):
                first, last = isinstance(b, int) and b == 0, isinstance(b, int) and b == LAST
                nk = keys(b)
                for h in range(HX):
                    e.wait_ge(sem("maxed"), b * HX + h + 1)
                    if not (first and h < P_RING):
                        e.wait_ge(sem("turned"), b * HX + h - P_RING + 1)
                    e.activation(prob[:, h % P_RING, 0:nk], p_s[h % S_RING][:, 0:nk], ACT.Exp,
                                 bias=neg_max[:, odd, h:h + 1]).then_inc(sem("exped"), 1)
                    if h in PROJ_COPY_STEPS and not last:
                        copy_proj(b + 1, 1 - odd, PROJ_COPY_STEPS.index(h))
                    behind(b, odd, h)

            def behind(b, odd, step):
                if step % HX == ALPHA_STEP:
                    at = lagging(b, odd, step, HX + ALPHA_STEP)
                    if at:
                        rise(at[0])
                at = lagging(b, odd, step, COPY_LAG)
                if at and at[2] not in DVE_COPIES:
                    copy_turned(e, e.copy, *at)

            def rise(b):
                e.wait_ge(sem("stepped"), b + 1)
                if not (isinstance(b, int) and b == 0):
                    e.wait_ge(sem("scaled"), b)
                e.activation(alpha[:], max_step[:], ACT.Exp).then_inc(sem("alpha"), 1)

            e.wait_ge(sem("k_weights"), 16)
            e.copy(wk_part[:, HIGH], wk[:]).then_inc(sem("k_weights_high"), 1)
            e.wait_ge(sem("ctx_loaded_0"), 16)
            e.copy(ctx_part[:, 0, HIGH], ctx[:, 0]).then_inc(sem("first_ctx_high"), 1)
            e.wait_ge(sem("k_bias"), 16)
            copy_proj(0, 0, 0)
            e.wait_ge(sem("v_weights"), 16)
            e.copy(wv_part[:, HIGH], wv[:]).then_inc(sem("v_weights_high"), 1)
            copy_proj(0, 0, 1)
            e.wait_ge(sem("v_ones"), 1)
            copy_proj(0, 0, 2)
            copy_proj(0, 0, 3)
            over_blocks(e, body)
            for step in range(HX, HX + DRAIN):
                behind(LAST, LAST % 2, step)

        @block.vector
        def _(e):
            e.bn_stats(stats[:], x[:]).then_inc(sem("bn"), 1)
            e.memset(acc[:], 0.0).then_inc(sem("acc_zero"), 1)
            e.memset(neg_max[:], BIG).then_inc(sem("acc_zero"), 1)
            e.wait_ge(sem("bn"), 1)
            e.bn_aggr(mean_var[:], stats[:]).then_inc(sem("stats"), 1)
            e.wait_ge(sem("stats"), 1)
            e.tensor_scalar(rstd[:, 1:2], mean_var[:, 1:2], 1e-5, None, ALU.add).then_inc(sem("stats"), 1)
            e.wait_ge(sem("root"), 1)
            e.reciprocal(rstd[:, 1:2], rstd[:, 0:1]).then_inc(sem("bn"), 1)
            e.wait_ge(sem("bn"), 2)
            e.tensor_scalar(xn[:], x[:], mean_var[:, 0:1], rstd[:, 1:2], ALU.subtract, ALU.mult).then_inc(sem("normed"), 1)
            def low(full, parts, high, signal):
                e.wait_ge(sem(high), 1)
                e.tensor_tensor(parts[:, LOW], full, parts[:, HIGH].bitcast(F32), ALU.subtract).then_inc(sem(signal), 1)

            def k_low(b, odd, part):
                nk = keys(b)
                e.wait_ge(sem("k_high"), b * 2 + part + 1)
                e.scalar_tensor_tensor(kT[:, odd, LOW, part, 0:nk], p_proj[:, 0:nk], bias_k[:, part:part + 1],
                                       kT[:, odd, HIGH, part, 0:nk].bitcast(F32), ALU.add,
                                       ALU.subtract).then_inc(sem("proj_copied"), 1)

            e.wait_ge(sem("xn_turned"), 1)
            e.tensor_copy(xnT[:].rearrange("p c n -> p (c n)"), p_t[0][:, 0:D]).then_inc(sem("xnT_copied"), 1)
            e.wait_ge(sem("k_weights"), 16)
            low(wk[:], wk_part, "k_weights_high", "k_weights_split")
            e.wait_ge(sem("ctx_loaded_0"), 16)
            low(ctx[:, 0], ctx_part[:, 0], "first_ctx_high", "first_ctx_split")
            e.wait_ge(sem("k_bias"), 16)
            k_low(0, 0, 0)
            e.wait_ge(sem("v_weights"), 16)
            low(wv[:], wv_part, "v_weights_high", "v_weights_split")
            k_low(0, 0, 1)
            e.wait_ge(sem("q_weights"), 32)
            for pair in range(HX // 2):
                e.wait_ge(sem("q_made"), pair // 4 + 1)
                e.tensor_scalar(q_full[:, pair, :], p_t[pair // 4][0:ROWS, pair % 4 * P:(pair % 4 + 1) * P],
                                bias_q[:, pair:pair + 1], float(HD) ** -0.5, ALU.add, ALU.mult).then_inc(sem("q_copied"), 1)
            e.wait_ge(sem("q_copied"), HX // 2)
            heads = q_stack[:].rearrange("p (a j) n -> p a j n", j=2)
            for j in range(2):
                row, last_slot = st["stack_rows"][0:ROWS, j:j + 1], slice((SLOTS - 1) * SLOT, ROWS)
                e.tensor_scalar(heads[:, :, j, :], q_full[:], row, None, ALU.mult).then_inc(sem("q_high"), 1)
                e.wait_ge(sem("q_high"), j + 1)
                e.scalar_tensor_tensor(heads[last_slot, :, j, :], q_full[last_slot], st["stack_rows"][last_slot, j:j + 1],
                                       heads[last_slot, :, j, :].bitcast(F32), ALU.mult, ALU.subtract).then_inc(sem("q_stacked"), 1)
            e.wait_ge(sem("acc_zero"), 2)

            def body(b, odd):
                first, last = isinstance(b, int) and b == 0, isinstance(b, int) and b == LAST
                nk = keys(b)
                if mask_kind:
                    e.wait_ge(sem("mask_made"), b + 1)
                for h in range(HX):
                    made = in_register(e, b * HX + h + 1)
                    if mask_kind:
                        e.wait_ge(sem("acc_zero"), 2)
                    e.wait_ge(sem("scored"), made)
                    s = p_s[h % S_RING][:, 0:nk]
                    if mask_kind:
                        e.tensor_tensor_reduce(s, s, mask[:, odd, 0:nk], 1.0, -3e38, ALU.add, ALU.max,
                                               block_max[:, h:h + 1]).then_inc(sem("head_maxed"), 1)
                    else:
                        e.tensor_reduce(block_max[:, h:h + 1], s, AX, ALU.max).then_inc(sem("head_maxed"), 1)
                    e.wait_ge(sem("head_maxed"), b * HX + h + 1)
                    e.scalar_tensor_tensor(neg_max[:, odd, h:h + 1], block_max[:, h:h + 1], -1.0,
                                           neg_max[:, 1 - odd, h:h + 1], ALU.mult, ALU.min).then_inc(sem("maxed"), 1)
                    if h in K_LOW_STEPS and not last:
                        k_low(b + 1, 1 - odd, K_LOW_STEPS.index(h))
                    behind(b, odd, h)
                if not first:
                    e.wait_ge(sem("alpha"), b)
                e.wait_ge(sem("maxed"), (b + 1) * HX)
                e.tensor_tensor(max_step[:], neg_max[:, odd, :], neg_max[:, 1 - odd, :], ALU.subtract).then_inc(sem("stepped"), 1)

            def behind(b, odd, step):
                if step % HX == OT_COPY_STEP:
                    at = lagging(b, odd, step, HX + OT_COPY_STEP)
                    if at:
                        copy_oT(at[0])
                if step % HX == ADD_STEP:
                    at = lagging(b, odd, step, HX + ADD_STEP)
                    if at:
                        accumulate(at[0])
                at = lagging(b, odd, step, COPY_LAG)
                if at and at[2] in DVE_COPIES:
                    copy_turned(e, e.tensor_copy, *at)

            def copy_oT(b):
                e.wait_ge(sem("valued"), (b + 1) * 4)
                if not (isinstance(b, int) and b == 0):
                    e.wait_ge(sem("o_turned"), b)
                e.tensor_copy(oT[:].rearrange("p g n -> p (g n)"), p_oT[:]).then_inc(sem("oT_copied"), 1)

            def accumulate(b):
                e.wait_ge(sem("alpha"), b + 1)
                if not (isinstance(b, int) and b == 0):
                    e.wait_ge(sem("added"), b)
                a = acc[:, :, 0:HD + 1]
                e.tensor_tensor(a, a, alpha[:].unsqueeze(2).broadcast_to([P, HX, HD + 1]), ALU.mult).then_inc(sem("scaled"), 1)
                e.wait_ge(sem("scaled"), b + 1)
                e.wait_ge(sem("o_turned"), b + 1)
                e.tensor_tensor(a, a, p_proj[:].rearrange("p (h d) -> p h d", h=HX)[:, :, 0:HD + 1], ALU.add).then_inc(sem("added"), 1)

            over_blocks(e, body)
            for step in range(HX, HX + DRAIN):
                behind(LAST, LAST % 2, step)
            e.wait_ge(sem("added"), LAST + 1)
            e.reciprocal(rsum[:], acc[:, :, HD]).then_inc(sem("rsum"), 1)
            e.wait_ge(sem("rsum"), 1)
            e.tensor_tensor(o[:].rearrange("p (h d) -> p h d", h=HX), acc[:, :, 0:HD],
                            rsum[:].unsqueeze(2).broadcast_to([P, HX, HD]), ALU.mult).then_inc(sem("rsum"), 1)
            e.wait_ge(sem("rsum"), 2)
            e.wait_ge(sem("out_weights"), 48 if has_wo else 16)
            e.tensor_tensor(o[:], o[:], bias_v[:], ALU.add).then_inc(sem("o_final"), 1)
            e.wait_ge(sem("o_final"), 1)
            if has_wo:
                e.wait_ge(sem("o2_turned"), 1)
                e.tensor_copy(o2T[:].rearrange("p c n -> p (c n)"), p_t[0][:, 0:D]).then_inc(sem("o2T_copied"), 1)
                e.tensor_tensor(x[:], x[:], bias_o[:], ALU.add).then_inc(sem("x_biased"), 1)
                e.wait_ge(sem("x_biased"), 1)
                e.wait_ge(sem("out_made"), 1)
                e.tensor_tensor(x[:], x[:], p_proj[:, 0:D], ALU.add)
            else:
                e.tensor_tensor(x[:], x[:], o[:], ALU.add)

    m.end()


def chain(e, sem):
    count = [0]

    def link(i):
        count[0] += 1
        i.then_inc(sem, 1)
        e.wait_ge(sem, count[0])

    return link


def norm_scratch(m, tag):
    return m.sb(f"{tag}_stats", [P, 6]), m.sb(f"{tag}_mean_var", [P, 2]), m.sb(f"{tag}_rstd", [P, 2])


def norm_vector(e, m, link, tag, scratch, src, out, eps=1e-5):
    stats, mean_var, rstd = scratch
    link(e.bn_stats(stats[:], src))
    link(e.bn_aggr(mean_var[:], stats[:]))
    e.tensor_scalar(rstd[:, 1:2], mean_var[:, 1:2], eps, None, ALU.add).then_inc(m.sem(f"{tag}_var"), 1)
    e.wait_ge(m.sem(f"{tag}_root"), 1)
    link(e.reciprocal(rstd[:, 1:2], rstd[:, 0:1]))
    e.tensor_scalar(out, src, mean_var[:, 0:1], rstd[:, 1:2], ALU.subtract, ALU.mult).then_inc(m.sem(f"{tag}_normed"), 1)


def norm_scalar(e, m, tag, scratch):
    rstd = scratch[2]
    e.wait_ge(m.sem(f"{tag}_var"), 1)
    e.activation(rstd[:, 0:1], rstd[:, 1:2], ACT.Sqrt).then_inc(m.sem(f"{tag}_root"), 1)


def turn_chunks(e, ident, bank, src, chunks=DC):
    for c in range(chunks):
        i = e.transpose(bank[:, c * P:(c + 1) * P], src[:, c * P:(c + 1) * P], ident[:])
    return i


def project_turned(e, bank, w, xT, chunks_out=DC, at=0):
    for oc in range(chunks_out):
        for c in range(DC):
            i = e.matmul(bank[:, at + oc * P:at + (oc + 1) * P], w[:, c, oc * P:(oc + 1) * P], xT[:, c, :],
                         start=c == 0, stop=c == DC - 1)
    return i


def project_rows(e, out, xT, w, chunks=DC):
    for c in range(chunks):
        i = e.matmul(out, xT[:, c, :], w[:, c, :], start=c == 0, stop=c == chunks - 1)
    return i


def chunked(w):
    return w.rearrange("(c p) n -> p c n", p=P)


def one_head_attention(nc, st, name, w, kind):
    m = Module(nc, name)
    sb, ps, sem = m.sb, m.ps, m.sem
    x, ident = st["x"], st["ident"]
    columns = kind == "columns"
    scale = float(D) ** -0.5
    scratch = norm_scratch(m, "ln")
    xn, xnT = sb("xn", [P, D]), sb("xnT", [P, DC, P])
    wq, wk, wv = (sb(n, [P, DC, D]) for n in ("wq", "wk", "wv"))
    bq, bk, bv = (sb("bq", [P, DC]), sb("bk", [P, DC]), sb("bv", [P, D])) if columns else (None, None, None)
    mask = sb("mask", [P, P])
    qT, kT, v = sb("qT", [P, DC, P]), sb("kT", [P, DC, P]), sb("v", [P, D])
    s, zero = sb("s", [P, P]), sb("zero", [P, P])
    top, low, total, inv = (sb(n, [P, 1]) for n in ("top", "low", "total", "inv"))
    prob, probT = sb("prob", [P, P]), sb("probT", [P, P])
    p_x, p_q, p_k, p_v, p_s, p_t, p_o = (ps(n) for n in ("p_x", "p_q", "p_k", "p_v", "p_s", "p_t", "p_o"))
    loads = [(wq, chunked(w["wq"])), (wk, chunked(w["wk"])), (wv, chunked(w["wv"])), (mask, w["mask"])]
    if columns:
        loads += [(bq, w["bq"]), (bk, w["bk"]), (bv, w["bv"])]

    with nc.Block() as block:

        @block.sync
        def _(e):
            for t, src in loads:
                e.dma_start(t[:], src).then_inc(sem("weights"), 16)

        @block.tensor
        def _(e):
            e.wait_ge(sem("ln_normed"), 1)
            turn_chunks(e, ident, p_x, xn).then_inc(sem("xn_turned"), 1)
            e.wait_ge(sem("xnT_copied"), 1)
            e.wait_ge(sem("weights"), 16 * len(loads))
            project_turned(e, p_q, wq, xnT)
            project_turned(e, p_k, wk, xnT).then_inc(sem("qk_made"), 1)
            project_rows(e, p_v[:, 0:D], xnT, wv).then_inc(sem("v_made"), 1)
            e.wait_ge(sem("q_copied"), 1)
            e.wait_ge(sem("k_copied"), 1)
            a, b = (kT, qT) if columns else (qT, kT)
            for c in range(DC):
                i = e.matmul(p_s[:, 0:P], a[:, c, :], b[:, c, :], start=c == 0, stop=c == DC - 1)
            i.then_inc(sem("scored"), 1)
            if columns:
                probs_by_key = prob
                e.wait_ge(sem("prob_scaled"), 1)
            else:
                probs_by_key = probT
                e.wait_ge(sem("exped"), 1)
                e.transpose(p_t[:, 0:P], prob[:], ident[:]).then_inc(sem("prob_turned"), 1)
                e.wait_ge(sem("probT_copied"), 1)
            e.wait_ge(sem("v_copied"), 1)
            e.matmul(p_o[:, 0:D], probs_by_key[:], v[:], start=True, stop=True).then_inc(sem("out_made"), 1)

        @block.scalar
        def _(e):
            norm_scalar(e, m, "ln", scratch)
            e.wait_ge(sem("qk_made"), 1)
            e.wait_ge(sem("weights"), 16 * len(loads))
            for c in range(DC):
                part = p_k[:, c * P:(c + 1) * P]
                i = e.activation(kT[:, c, :], part, ACT.Identity, bias=bk[:, c:c + 1]) if columns else \
                    e.copy(kT[:, c, :], part)
            i.then_inc(sem("k_copied"), 1)
            if not columns:
                e.wait_ge(sem("v_made"), 1)
                e.copy(v[:], p_v[:, 0:D]).then_inc(sem("v_copied"), 1)
            e.wait_ge(sem("low"), 1)
            e.activation(prob[:], s[:], ACT.Exp, bias=low[:, 0:1], accum_out=total[:]).then_inc(sem("exped"), 1)

        @block.vector
        def _(e):
            link = chain(e, sem("vector_chain"))
            norm_vector(e, m, link, "ln", scratch, x[:], xn[:])
            e.wait_ge(sem("xn_turned"), 1)
            e.tensor_copy(xnT[:].rearrange("p c n -> p (c n)"), p_x[:, 0:D]).then_inc(sem("xnT_copied"), 1)
            e.wait_ge(sem("qk_made"), 1)
            e.wait_ge(sem("weights"), 16 * len(loads))
            for c in range(DC):
                part = p_q[:, c * P:(c + 1) * P]
                i = e.tensor_scalar(qT[:, c, :], part, bq[:, c:c + 1], scale, ALU.add, ALU.mult) if columns else \
                    e.tensor_scalar(qT[:, c, :], part, scale, None, ALU.mult)
            i.then_inc(sem("q_copied"), 1)
            if columns:
                e.wait_ge(sem("v_made"), 1)
                e.tensor_tensor(v[:], p_v[:, 0:D], bv[:], ALU.add).then_inc(sem("v_copied"), 1)
            e.wait_ge(sem("scored"), 1)
            if columns:
                link(e.tensor_tensor(s[:], p_s[:, 0:P], mask[:], ALU.add))
            else:
                link(e.tensor_tensor(s[:], p_s[:, 0:P], mask[:], ALU.mult))
                link(e.tensor_scalar(zero[:], s[:], 0.0, -9e15, ALU.is_equal, ALU.mult))
                link(e.tensor_tensor(s[:], s[:], zero[:], ALU.add))
            link(e.tensor_reduce(top[:], s[:], AX, ALU.max))
            e.tensor_scalar(low[:], top[:], -1.0, None, ALU.mult).then_inc(sem("low"), 1)
            e.wait_ge(sem("exped"), 1)
            link(e.reciprocal(inv[:], total[:]))
            if columns:
                e.tensor_scalar(prob[:], prob[:], inv[:, 0:1], None, ALU.mult).then_inc(sem("prob_scaled"), 1)
                e.wait_ge(sem("out_made"), 1)
                e.tensor_tensor(x[:], x[:], p_o[:, 0:D], ALU.add)
            else:
                e.wait_ge(sem("prob_turned"), 1)
                e.tensor_copy(probT[:], p_t[:, 0:P]).then_inc(sem("probT_copied"), 1)
                e.wait_ge(sem("out_made"), 1)
                e.scalar_tensor_tensor(x[:], p_o[:, 0:D], inv[:, 0:1], x[:], ALU.mult, ALU.add)

    m.end()


def token_choice_experts(nc, st, name, w):
    m = Module(nc, name)
    sb, ps, sem = m.sb, m.ps, m.sem
    x, ident = st["x"], st["ident"]
    E, K, RING = 16, 64, 8
    scratch = norm_scratch(m, "ln")
    xn, xnT = sb("xn", [P, D]), sb("xnT", [P, DC, P])
    wg, bg = sb("wg", [P, DC, E]), sb("bg", [E, 1])
    b12, b3 = sb("b12", [P, 2, E]), sb("b3", [E, 1])
    w1, w2, w3 = (sb(n, [P, RING, DC, D]) for n in ("w1", "w2", "w3"))
    logits = sb("logits", [E, P])
    top, low, total, inv = (sb(n, [E, 1]) for n in ("top", "low", "total", "inv"))
    prob, left, taken, best = sb("prob", [E, P]), sb("left", [E, P]), sb("taken", [E, P]), sb("best", [E, 8])
    weight = sb("weight", [P, E])
    h1, h2 = sb("h1", [P, 2, DC, P]), sb("h2", [P, 2, DC, P])
    p_g, p_w = ps("p_g"), ps("p_w")
    p_h1, p_h2, p_y = ([ps(f"{n}{i}") for i in range(2)] for n in ("p_h1", "p_h2", "p_y"))

    with nc.Block() as block:

        @block.sync
        def _(e):
            for t, src in ((wg, chunked(w["wg"])), (bg, w["bg"]), (b12, w["b12"]), (b3, w["b3"])):
                e.dma_start(t[:], src).then_inc(sem("gate_weights"), 16)
            for x_ in range(E):
                if x_ >= RING:
                    e.wait_ge(sem("y_made"), x_ - RING + 1)
                for t, src in ((w1, w["w1"]), (w2, w["w2"]), (w3, w["w3"])):
                    e.dma_start(t[:, x_ % RING, :, :], chunked(src[x_])).then_inc(sem(f"expert_loaded_{x_ % RING}"), 16)

        @block.tensor
        def _(e):
            e.wait_ge(sem("ln_normed"), 1)
            turn_chunks(e, ident, p_w, xn).then_inc(sem("xn_turned"), 1)
            e.wait_ge(sem("xnT_copied"), 1)
            e.wait_ge(sem("gate_weights"), 64)
            for c in range(DC):
                i = e.matmul(p_g[0:E, 0:P], wg[:, c, :], xnT[:, c, :], start=c == 0, stop=c == DC - 1)
            i.then_inc(sem("gated"), 1)

            def layers(x_, k):
                r = x_ % 2
                if k == 1:
                    e.wait_ge(sem(f"expert_loaded_{x_ % RING}"), 48 * (x_ // RING + 1))
                    if x_ >= 2:
                        e.wait_ge(sem("h1_done"), x_ - 1)
                    project_turned(e, p_h1[r], w1[:, x_ % RING], xnT).then_inc(sem("h1_made"), 1)
                if k == 2:
                    e.wait_ge(sem("h1_done"), x_ + 1)
                    if x_ >= 2:
                        e.wait_ge(sem("h2_done"), x_ - 1)
                    project_turned(e, p_h2[r], w2[:, x_ % RING], h1[:, r]).then_inc(sem("h2_made"), 1)
                if k == 3:
                    e.wait_ge(sem("h2_done"), x_ + 1)
                    if x_ >= 2:
                        e.wait_ge(sem("y_added"), x_ - 1)
                    project_rows(e, p_y[r][:, 0:D], h2[:, r], w3[:, x_ % RING]).then_inc(sem("y_made"), 1)

            for n in range(E + 2):
                if n < E:
                    layers(n, 1)
                if 1 <= n <= E:
                    layers(n - 1, 2)
                if n == 2:
                    e.wait_ge(sem("taken"), 1)
                    e.transpose(p_w[:, 0:E], taken[:], ident[0:E, 0:E])
                    e.matmul(p_w[:, 32:33], taken[:], b3[:], start=True, stop=True).then_inc(sem("weight_turned"), 1)
                if n >= 2:
                    layers(n - 2, 3)

        @block.scalar
        def _(e):
            norm_scalar(e, m, "ln", scratch)
            e.wait_ge(sem("low"), 1)
            e.activation(prob[:], logits[:], ACT.Exp, bias=low[:, 0:1], accum_out=total[:]).then_inc(sem("exped"), 1)
            for x_ in range(E):
                e.wait_ge(sem("gate_weights"), 64)
                e.wait_ge(sem("h1_made"), x_ + 1)
                if x_ >= 2:
                    e.wait_ge(sem("h2_made"), x_ - 1)
                e.activation(h1[:, x_ % 2].rearrange("p c n -> p (c n)"), p_h1[x_ % 2][:, 0:D], ACT.Relu,
                             bias=b12[:, 0, x_:x_ + 1]).then_inc(sem("h1_done"), 1)
                e.wait_ge(sem("h2_made"), x_ + 1)
                if x_ >= 2:
                    e.wait_ge(sem("y_made"), x_ - 1)
                e.activation(h2[:, x_ % 2].rearrange("p c n -> p (c n)"), p_h2[x_ % 2][:, 0:D], ACT.Relu,
                             bias=b12[:, 1, x_:x_ + 1]).then_inc(sem("h2_done"), 1)

        @block.vector
        def _(e):
            link = chain(e, sem("vector_chain"))
            norm_vector(e, m, link, "ln", scratch, x[:], xn[:])
            e.wait_ge(sem("xn_turned"), 1)
            e.tensor_copy(xnT[:].rearrange("p c n -> p (c n)"), p_w[:, 0:D]).then_inc(sem("xnT_copied"), 1)
            e.wait_ge(sem("gated"), 1)
            e.wait_ge(sem("gate_weights"), 64)
            link(e.tensor_scalar(logits[:], p_g[0:E, 0:P], bg[:, 0:1], None, ALU.add))
            link(e.tensor_reduce(top[:], logits[:], AX, ALU.max))
            e.tensor_scalar(low[:], top[:], -1.0, None, ALU.mult).then_inc(sem("low"), 1)
            e.wait_ge(sem("exped"), 1)
            link(e.reciprocal(inv[:], total[:]))
            link(e.tensor_scalar(prob[:], prob[:], inv[:, 0:1], None, ALU.mult))
            for k in range(K // 8):
                src = prob if k == 0 else left
                link(e.max(best[:], src[:]))
                link(e.match_replace(left[:], best[:], src[:], -1.0))
            link(e.tensor_scalar(left[:], left[:], 0.0, None, ALU.is_lt))
            e.tensor_tensor(taken[:], prob[:], left[:], ALU.mult).then_inc(sem("taken"), 1)
            e.wait_ge(sem("weight_turned"), 1)
            link(e.tensor_copy(weight[:], p_w[:, 0:E]))
            link(e.tensor_scalar(x[:], x[:], p_w[:, 32:33], None, ALU.add))
            for x_ in range(E):
                e.wait_ge(sem("y_made"), x_ + 1)
                if x_:
                    e.wait_ge(sem("y_added"), x_)
                e.scalar_tensor_tensor(x[:], p_y[x_ % 2][:, 0:D], weight[:, x_:x_ + 1], x[:],
                                       ALU.mult, ALU.add).then_inc(sem("y_added"), 1)

    m.end()


def top_two_experts(nc, st, name, w):
    m = Module(nc, name)
    sb, ps, sem = m.sb, m.ps, m.sem
    x, ident = st["x"], st["ident"]
    E, H = 8, 512
    HC = H // P
    scratch, scratch2 = norm_scratch(m, "ln"), norm_scratch(m, "out")
    xn, xnT = sb("xn", [P, D]), sb("xnT", [P, DC, P])
    gate = sb("gate", [P, DC, E])
    w1 = sb("w1", [P, E, DC, H])
    w2 = sb("w2", [P, E, HC, D])
    b1 = sb("b1", [1, E, H])
    g1, b1n = sb("g1", [P, E, HC]), sb("b1n", [P, E, HC])
    b2 = sb("b2", [E, D])
    out_g, out_b = sb("out_g", [P, D]), sb("out_b", [P, D])
    ones = sb("ones", [1, P])
    logits, total, inv, low = sb("logits", [P, E]), sb("total", [P, 1]), sb("inv", [P, 1]), sb("low", [P, 1])
    gates, best, wanted = sb("gates", [P, 2 * E]), sb("best", [P, 8]), sb("wanted", [P, 8])
    left, chosen, weight = sb("left", [P, 2 * E]), sb("chosen", [P, E]), sb("weight", [P, E])
    weightT = sb("weightT", [E, P])
    h = sb("h", [P, E, H])
    stats, mean_var, rstd = sb("stats", [P, E, 6]), sb("mean_var", [P, E, 2]), sb("rstd", [P, 2, E])
    a = sb("a", [P, 2, HC, P])
    acc, y = sb("acc", [P, D]), sb("y", [P, D])
    p_x, p_g = ps("p_x"), ps("p_g")
    p_h, p_t, p_y = ([ps(f"{n}{i}") for i in range(2)] for n in ("p_h", "p_t", "p_y"))

    with nc.Block() as block:

        @block.sync
        def _(e):
            small = ((gate, chunked(w["gate"])), (b1, w["b1"]), (g1, w["g1"]), (b1n, w["b1n"]), (b2, w["b2"]),
                     (out_g, w["out_g"]), (out_b, w["out_b"]))
            for t, src in small:
                e.dma_start(t[:], src).then_inc(sem("small_weights"), 16)
            for x_ in range(E):
                e.dma_start(w1[:, x_], chunked(w["w1"][x_])).then_inc(sem(f"w1_loaded_{x_}"), 16)
            for x_ in range(E):
                e.dma_start(w2[:, x_], chunked(w["w2"][x_])).then_inc(sem(f"w2_loaded_{x_}"), 16)

        @block.gpsimd
        def _(e):
            e.memset(ones[:], 1.0).then_inc(sem("constants"), 1)
            for k in range(E):
                e.memset(gates[:, E + k:E + k + 1], -1.0 - k).then_inc(sem("constants"), 1)
            for k in range(8):
                e.memset(wanted[:, k:k + 1], -1.0 - k).then_inc(sem("constants"), 1)

        @block.tensor
        def _(e):
            e.wait_ge(sem("ln_normed"), 1)
            turn_chunks(e, ident, p_x, xn).then_inc(sem("xn_turned"), 1)
            e.wait_ge(sem("xnT_copied"), 1)
            e.wait_ge(sem("small_weights"), 112)
            project_rows(e, p_g[:, 0:E], xnT, gate).then_inc(sem("gated"), 1)
            e.wait_ge(sem("constants"), 1 + E + 8)
            for x_ in range(E):
                e.wait_ge(sem(f"w1_loaded_{x_}"), 16)
                if x_ >= 2:
                    e.wait_ge(sem("h_copied"), x_ - 1)
                e.matmul(p_h[x_ % 2][:], ones[:], b1[:, x_, :], start=True, stop=False)
                for c in range(DC):
                    i = e.matmul(p_h[x_ % 2][:], xnT[:, c, :], w1[:, x_, c, :], start=False, stop=c == DC - 1)
                i.then_inc(sem("h_made"), 1)
            e.wait_ge(sem("weighted"), 1)
            e.transpose(p_x[0:E, 0:P], weight[:], ident[:]).then_inc(sem("weight_turned"), 1)
            e.wait_ge(sem("weightT_copied"), 1)
            e.matmul(p_g[:, 0:D], weightT[:], b2[:], start=True, stop=True).then_inc(sem("b2_made"), 1)

            def second(x_):
                e.wait_ge(sem("activated"), x_ + 1)
                e.wait_ge(sem(f"w2_loaded_{x_}"), 16)
                if x_ >= 2:
                    e.wait_ge(sem("y_added"), x_ - 1)
                project_rows(e, p_y[x_ % 2][:, 0:D], a[:, x_ % 2], w2[:, x_], HC).then_inc(sem("y_made"), 1)

            for x_ in range(E):
                e.wait_ge(sem("h_normed"), x_ + 1)
                if x_ >= 2:
                    e.wait_ge(sem("activated"), x_ - 1)
                turn_chunks(e, ident, p_t[x_ % 2], h[:, x_], HC).then_inc(sem("h_turned"), 1)
                if x_ >= 1:
                    second(x_ - 1)
            second(E - 1)

        @block.scalar
        def _(e):
            norm_scalar(e, m, "ln", scratch)
            e.wait_ge(sem("low"), 1)
            e.activation(gates[:, 0:E], logits[:], ACT.Exp, bias=low[:, 0:1], accum_out=total[:]).then_inc(sem("exped"), 1)
            for x_ in range(E):
                e.wait_ge(sem("h_made"), x_ + 1)
                e.copy(h[:, x_], p_h[x_ % 2][:]).then_inc(sem("h_copied"), 1)
            e.wait_ge(sem("h_vars"), 1)
            e.activation(rstd[:, 0, :], rstd[:, 1, :], ACT.Sqrt).then_inc(sem("h_roots"), 1)
            e.wait_ge(sem("small_weights"), 112)
            for x_ in range(E):
                e.wait_ge(sem("h_turned"), x_ + 1)
                if x_ >= 2:
                    e.wait_ge(sem("y_made"), x_ - 1)
                for c in range(HC):
                    i = e.activation(a[:, x_ % 2, c, :], p_t[x_ % 2][:, c * P:(c + 1) * P], ACT.Gelu,
                                     bias=b1n[:, x_, c:c + 1], scale=g1[:, x_, c:c + 1])
                i.then_inc(sem("activated"), 1)
            norm_scalar(e, m, "out", scratch2)

        @block.vector
        def _(e):
            link = chain(e, sem("vector_chain"))
            norm_vector(e, m, link, "ln", scratch, x[:], xn[:])
            e.wait_ge(sem("xn_turned"), 1)
            e.tensor_copy(xnT[:].rearrange("p c n -> p (c n)"), p_x[:, 0:D]).then_inc(sem("xnT_copied"), 1)
            e.wait_ge(sem("gated"), 1)
            link(e.tensor_copy(logits[:], p_g[:, 0:E]))
            link(e.tensor_reduce(low[:], logits[:], AX, ALU.max))
            e.tensor_scalar(low[:], low[:], -1.0, None, ALU.mult).then_inc(sem("low"), 1)
            e.wait_ge(sem("exped"), 1)
            link(e.reciprocal(inv[:], total[:]))
            link(e.tensor_scalar(gates[:, 0:E], gates[:, 0:E], inv[:, 0:1], None, ALU.mult))
            e.wait_ge(sem("constants"), 1 + E + 8)
            link(e.max(best[:], gates[:, 0:E]))
            link(e.tensor_copy(wanted[:, 0:2], best[:, 0:2]))
            link(e.match_replace(left[:], wanted[:], gates[:], -100.0))
            link(e.tensor_scalar(chosen[:], left[:, 0:E], -50.0, None, ALU.is_lt))
            link(e.tensor_tensor(total[:], best[:, 0:1], best[:, 1:2], ALU.add))
            link(e.reciprocal(inv[:], total[:]))
            e.scalar_tensor_tensor(weight[:], gates[:, 0:E], inv[:, 0:1], chosen[:], ALU.mult, ALU.mult).then_inc(sem("weighted"), 1)
            for x_ in range(E):
                e.wait_ge(sem("h_copied"), x_ + 1)
                e.bn_stats(stats[:, x_], h[:, x_]).then_inc(sem("h_stats"), 1)
            e.wait_ge(sem("h_stats"), E)
            for x_ in range(E):
                e.bn_aggr(mean_var[:, x_], stats[:, x_]).then_inc(sem("h_aggr"), 1)
            e.wait_ge(sem("h_aggr"), E)
            e.tensor_scalar(rstd[:, 1, :], mean_var[:, :, 1], 1e-5, None, ALU.add).then_inc(sem("h_vars"), 1)
            e.wait_ge(sem("weight_turned"), 1)
            e.tensor_copy(weightT[:], p_x[0:E, 0:P]).then_inc(sem("weightT_copied"), 1)
            e.wait_ge(sem("b2_made"), 1)
            link(e.tensor_tensor(acc[:], xn[:], p_g[:, 0:D], ALU.add))
            e.wait_ge(sem("h_roots"), 1)
            link(e.reciprocal(rstd[:, 1, :], rstd[:, 0, :]))
            for x_ in range(E):
                e.tensor_scalar(h[:, x_], h[:, x_], mean_var[:, x_, 0:1], rstd[:, 1, x_:x_ + 1],
                                ALU.subtract, ALU.mult).then_inc(sem("h_normed"), 1)
            for x_ in range(E):
                e.wait_ge(sem("y_made"), x_ + 1)
                if x_:
                    e.wait_ge(sem("y_added"), x_)
                e.scalar_tensor_tensor(acc[:], p_y[x_ % 2][:, 0:D], weight[:, x_:x_ + 1], acc[:],
                                       ALU.mult, ALU.add).then_inc(sem("y_added"), 1)
            e.wait_ge(sem("y_added"), E)
            norm_vector(e, m, link, "out", scratch2, acc[:], y[:])
            e.wait_ge(sem("out_normed"), 1)
            e.wait_ge(sem("small_weights"), 112)
            link(e.tensor_tensor(y[:], y[:], out_g[:], ALU.mult))
            link(e.tensor_tensor(y[:], y[:], out_b[:], ALU.add))
            e.tensor_tensor(x[:], x[:], y[:], ALU.add)

    m.end()


TAPS = (3, 15, 31)
LEAD = max(TAPS) - 1


def delta_rule_attention(nc, st, name, w):
    m = Module(nc, name)
    sb, ps, sem = m.sb, m.ps, m.sem
    x, ident = st["x"], st["ident"]
    NH, HW = 4, 64
    LEVELS = 7
    H2 = 2 * D
    HC = H2 // P
    G = 3 * NH
    scratch = norm_scratch(m, "ln")
    xn, xnT = sb("xn", [P, D]), sb("xnT", [P, DC, P])
    wqkv = sb("wqkv", [P, 3, DC, D])
    wb = sb("wb", [P, DC, NH])
    short = sb("short", [P, 3, DC, 4])
    taps = [sb(f"taps{n}", [P, DC, n]) for n in TAPS]
    mix = sb("mix", [P, 2, 3, HW])
    mixer = sb("mixer", [P, DC, D])
    fw1, fw1b = sb("fw1", [P, DC, H2]), sb("fw1b", [G, H2])
    fb1 = sb("fb1", [P, HC])
    fw2, fb2 = sb("fw2", [P, HC, G]), sb("fb2", [P, G])
    onorm, wo = sb("onorm", [P, HW]), sb("wo", [P, DC, D])
    below = sb("below", [P, LEVELS, P])
    causalT = sb("causalT", [P, P])
    pre = sb("pre", [P, 3, DC, 3 + P])
    conv = sb("conv", [P, 3, DC, P])
    act = sb("act", [P, 3, DC, P])
    vpad = sb("vpad", [P, DC, LEAD + P])
    ms = sb("ms", [P, 3, DC, P])
    nat = sb("nat", [P, 3, NH, HW])
    sq, ss, root, scl = sb("sq", [P, 2, NH, HW]), sb("ss", [P, 2 * NH]), sb("root", [P, 2 * NH]), sb("scl", [P, 2 * NH])
    beta = sb("beta", [P, NH])
    kb, vb = sb("kb", [P, NH, HW]), sb("vb", [P, NH, HW])
    qT, kT, kbT = sb("qT", [P, DC, P]), sb("kT", [P, DC, P]), sb("kbT", [P, DC, P])
    AT, BT = sb("AT", [P, NH, P]), sb("BT", [P, 2, NH, P])
    X, XT, Y = sb("X", [P, NH, P]), sb("XT", [P, NH, P]), sb("Y", [P, NH, P])
    locT = sb("locT", [P, NH, P])
    u = sb("u", [P, NH, HW])
    mixedT = sb("mixedT", [P, DC, P])
    branch = sb("branch", [P, 3, NH, HW])
    absmean = sb("absmean", [P, 3, NH])
    absT = sb("absT", [G, P])
    hid = sb("hid", [P, HC, P])
    lg, mx, den, inv = sb("lg", [P, NH, 3]), sb("mx", [P, NH]), sb("den", [P, NH]), sb("inv", [P, NH])
    wts = sb("wts", [P, NH, 3])
    o, part, oss, oinv = sb("o", [P, NH, HW]), sb("part", [P, NH, HW]), sb("oss", [P, NH]), sb("oinv", [P, 2, NH])
    oT = sb("oT", [P, DC, P])
    bank = [ps(f"bank{i}") for i in range(8)]
    flat = lambda t: t[:].rearrange("p a b -> p (a b)")
    loads = [(wqkv[:, i], chunked(w[n])) for i, n in enumerate(("Wq", "Wk", "Wv"))]
    loads += [(wb[:], chunked(w["Wb"])), (short[:], w["short"])]
    first_loads = len(loads)
    loads += [(t[:], w[f"ms{n}"]) for t, n in zip(taps, TAPS)]
    loads += [(mix[:], w["mix"]), (mixer[:], chunked(w["mixer"])), (fw1[:], chunked(w["fw1"][0:D, :])),
              (fw1b[:], w["fw1"][D:D + G, :]), (fb1[:], w["fb1"]), (fw2[:], chunked(w["fw2"])), (fb2[:], w["fb2"]),
              (onorm[:], w["onorm"]), (wo[:], chunked(w["Wo"])), (below[:], w["below"]), (causalT[:], w["causalT"])]
    FIRST, ALL = 16 * first_loads, 16 * (len(loads) - first_loads)

    def half(h):
        return slice(HW * (h % 2), HW * (h % 2) + HW), h // 2

    with nc.Block() as block:

        @block.sync
        def _(e):
            for n, (t, src) in enumerate(loads):
                e.dma_start(t, src).then_inc(sem("first_weights" if n < first_loads else "weights"), 16)

        @block.gpsimd
        def _(e):
            e.memset(pre[:, :, :, 0:3], 0.0).then_inc(sem("pads"), 1)
            e.memset(vpad[:, :, 0:LEAD], 0.0).then_inc(sem("pads"), 1)

        @block.tensor
        def _(e):
            e.wait_ge(sem("ln_normed"), 1)
            turn_chunks(e, ident, bank[0], xn).then_inc(sem("xn_turned"), 1)
            e.wait_ge(sem("xnT_copied"), 1)
            e.wait_ge(sem("first_weights"), FIRST)
            for i in range(3):
                project_turned(e, bank[1 + i], wqkv[:, i], xnT).then_inc(sem("qkv_made"), 1)
            project_rows(e, bank[0][:, 0:NH], xnT, wb).then_inc(sem("beta_made"), 1)
            for i in range(3):
                e.wait_ge(sem("activated"), i + 1)
                for c in range(DC):
                    t = e.transpose(bank[4 + i // 2][:, (i % 2) * D + c * P:(i % 2) * D + (c + 1) * P],
                                    act[:, i, c, :], ident[:])
                t.then_inc(sem("qkv_turned"), 1)
            for n, (src, b) in enumerate(((nat[:, 1], 1), (kb[:], 2), (nat[:, 0], 3))):
                e.wait_ge(sem("rows_ready"), n + 1)
                turn_chunks(e, ident, bank[b], src.rearrange("p a b -> p (a b)")).then_inc(sem("rows_turned"), 1)
            e.wait_ge(sem("turned_copied"), 3)
            e.wait_ge(sem("branch_copied"), 1)
            for out, a, b in ((2, kT, kbT), (6, kT, qT)):
                for h in range(NH):
                    r, c = half(h)
                    t = e.matmul(bank[out + h % 2][:, (h // 2) * P:(h // 2 + 1) * P], a[r, c, :], b[r, c, :],
                                 start=True, stop=True)
                t.then_inc(sem("products"), 1)
            for level in range(LEVELS):
                e.wait_ge(sem("B_masked"), level + 1)
                for h in range(NH):
                    t = e.matmul(bank[4][:, h * P:(h + 1) * P], BT[:, level % 2, h, :], X[:, h, :], start=True, stop=True)
                t.then_inc(sem("BX_made"), 1)
                e.wait_ge(sem("BX_copied"), level + 1)
                for h in range(NH):
                    t = e.matmul(bank[1][:, h * P:(h + 1) * P], XT[:, h, :], Y[:, h, :], start=True, stop=True)
                t.then_inc(sem("XBX_made"), 1)
                for h in range(NH):
                    t = e.matmul(bank[0][:, h * P:(h + 1) * P], Y[:, h, :], XT[:, h, :], start=True, stop=True)
                t.then_inc(sem("XBXT_made"), 1)
            e.wait_ge(sem("X_updated"), LEVELS)
            for h in range(NH):
                t = e.matmul(bank[4][:, h * HW:(h + 1) * HW], XT[:, h, :], vb[:, h, :], start=True, stop=True)
            t.then_inc(sem("u_made"), 1)
            e.wait_ge(sem("weights"), ALL)
            e.wait_ge(sem("ms_made"), 1)
            for unit in range(12):
                h, j, scale, chunk, side = unit // 3, unit % 3, unit // 4, unit // 2 % 2, unit % 2
                rows, c = half(h)
                t = e.matmul(bank[2][rows, c * P:(c + 1) * P], mix[:, side, j, :], ms[:, scale, chunk, :],
                             start=j == 0, stop=j == 2)
            t.then_inc(sem("mixed"), 1)
            e.wait_ge(sem("u_copied"), 1)
            for h in range(NH):
                t = e.matmul(bank[5][:, h * HW:(h + 1) * HW], locT[:, h, :], u[:, h, :], start=True, stop=True)
            t.then_inc(sem("delta_made"), 1)
            e.wait_ge(sem("mixed_copied"), 1)
            project_rows(e, bank[3][:, 0:D], mixedT, mixer).then_inc(sem("ms_out"), 1)
            e.wait_ge(sem("means_made"), 1)
            e.transpose(bank[6][0:G, 0:P], absmean[:].rearrange("p a b -> p (a b)"), ident[:]).then_inc(sem("means_turned"), 1)
            e.wait_ge(sem("absT_copied"), 1)
            for oc in range(HC):
                for c in range(DC):
                    e.matmul(bank[7][:, oc * P:(oc + 1) * P], fw1[:, c, oc * P:(oc + 1) * P], xnT[:, c, :],
                             start=c == 0, stop=False)
                t = e.matmul(bank[7][:, oc * P:(oc + 1) * P], fw1b[:, oc * P:(oc + 1) * P], absT[:], start=False, stop=True)
            t.then_inc(sem("hid_made"), 1)
            e.wait_ge(sem("hid_done"), 1)
            project_rows(e, bank[0][:, 0:G], hid, fw2, HC).then_inc(sem("logits_made"), 1)
            e.wait_ge(sem("o_done"), 1)
            turn_chunks(e, ident, bank[1], flat(o)).then_inc(sem("o_turned"), 1)
            e.wait_ge(sem("oT_copied"), 1)
            project_rows(e, bank[2][:, 0:D], oT, wo).then_inc(sem("out_made"), 1)

        @block.scalar
        def _(e):
            norm_scalar(e, m, "ln", scratch)
            e.wait_ge(sem("pads"), 2)
            for i in range(3):
                e.wait_ge(sem("qkv_made"), i + 1)
                e.copy(pre[:, i, :, 3:3 + P], bank[1 + i][:, 0:D].rearrange("p (c n) -> p c n", c=DC)).then_inc(sem("pre_copied"), 1)
            e.wait_ge(sem("beta_made"), 1)
            e.activation(beta[:], bank[0][:, 0:NH], ACT.Sigmoid).then_inc(sem("beta_done"), 1)
            for i in range(3):
                e.wait_ge(sem("convolved"), i + 1)
                e.activation(act[:, i], conv[:, i], ACT.Sigmoid).then_inc(sem("sigmoids"), 1)
            e.wait_ge(sem("squares"), 1)
            e.activation(root[:], ss[:], ACT.Sqrt).then_inc(sem("roots"), 1)
            for n, (dst, b) in enumerate(((kT, 1), (kbT, 2), (qT, 3))):
                e.wait_ge(sem("rows_turned"), n + 1)
                e.copy(flat(dst), bank[b][:, 0:D]).then_inc(sem("turned_copied"), 1)
            e.wait_ge(sem("mixed"), 1)
            e.copy(flat(mixedT), bank[2][:, 0:D]).then_inc(sem("mixed_copied"), 1)
            e.wait_ge(sem("ms_out"), 1)
            e.copy(branch[:, 0].rearrange("p a b -> p (a b)"), bank[3][:, 0:D]).then_inc(sem("ms_copied"), 1)
            e.wait_ge(sem("hid_made"), 1)
            e.wait_ge(sem("weights"), ALL)
            for c in range(HC):
                t = e.activation(hid[:, c, :], bank[7][:, c * P:(c + 1) * P], ACT.Gelu, bias=fb1[:, c:c + 1])
            t.then_inc(sem("hid_done"), 1)
            e.wait_ge(sem("lg_shifted"), 1)
            e.activation(wts[:], lg[:], ACT.Exp).then_inc(sem("wts_exp"), 1)
            e.wait_ge(sem("o_squares"), 1)
            e.activation(oinv[:, 0, :], oinv[:, 1, :], ACT.Sqrt).then_inc(sem("o_roots"), 1)

        @block.vector
        def _(e):
            link = chain(e, sem("vector_chain"))
            norm_vector(e, m, link, "ln", scratch, x[:], xn[:])
            e.wait_ge(sem("xn_turned"), 1)
            e.tensor_copy(flat(xnT), bank[0][:, 0:D]).then_inc(sem("xnT_copied"), 1)
            e.wait_ge(sem("first_weights"), FIRST)
            for i in range(3):
                e.wait_ge(sem("pre_copied"), i + 1)
                for j in range(4):
                    for c in range(DC):
                        src, tap, dst = pre[:, i, c, j:j + P], short[:, i, c, j:j + 1], conv[:, i, c, :]
                        t = e.tensor_scalar(dst, src, tap, None, ALU.mult) if j == 0 else \
                            e.scalar_tensor_tensor(dst, src, tap, dst, ALU.mult, ALU.add)
                        if j < 3:
                            t.then_inc(sem("short_conv"), 1)
                        if j < 3 and c == DC - 1:
                            e.wait_ge(sem("short_conv"), 2 * (3 * i + j + 1))
                        if j == 3:
                            t.then_inc(sem("convolved_part"), 1)
                e.wait_ge(sem("convolved_part"), 2 * (i + 1))
                e.nop().then_inc(sem("convolved"), 1)
            for i in range(3):
                e.wait_ge(sem("sigmoids"), i + 1)
                e.tensor_tensor(act[:, i], act[:, i], conv[:, i], ALU.mult).then_inc(sem("activated"), 1)
            e.wait_ge(sem("activated"), 3)
            e.wait_ge(sem("pads"), 2)
            link(e.tensor_copy(vpad[:, :, LEAD:LEAD + P], act[:, 2]))
            e.wait_ge(sem("qkv_turned"), 2)
            qk = nat[:, 0:2].rearrange("p i h d -> p (i h d)")
            link(e.tensor_copy(qk, bank[4][:]))
            link(e.tensor_tensor(sq[:].rearrange("p i h d -> p (i h d)"), qk, qk, ALU.mult))
            link(e.tensor_reduce(ss[:], sq[:].rearrange("p i h d -> p (i h) d"), AX, ALU.add))
            e.tensor_scalar(ss[:], ss[:], 1e-6, None, ALU.add).then_inc(sem("squares"), 1)
            e.wait_ge(sem("qkv_turned"), 3)
            link(e.tensor_copy(branch[:, 2].rearrange("p a b -> p (a b)"), bank[5][:, 0:D]))
            e.nop().then_inc(sem("branch_copied"), 1)
            e.wait_ge(sem("roots"), 1)
            link(e.reciprocal(scl[:], root[:]))
            n8 = nat[:, 0:2].rearrange("p i h d -> p (i h) d")
            link(e.tensor_tensor(n8, n8, scl[:].unsqueeze(2).broadcast_to([P, 2 * NH, HW]), ALU.mult))
            e.nop().then_inc(sem("rows_ready"), 1)
            e.wait_ge(sem("beta_done"), 1)
            over = beta[:].unsqueeze(2).broadcast_to([P, NH, HW])
            e.tensor_tensor(kb[:], nat[:, 1], over, ALU.mult).then_inc(sem("rows_ready"), 1)
            link(e.tensor_tensor(vb[:], branch[:, 2], over, ALU.mult))
            e.nop().then_inc(sem("rows_ready"), 1)
            e.wait_ge(sem("weights"), ALL)
            for n, (dst, out) in enumerate(((AT, 2), (locT, 6))):
                e.wait_ge(sem("products"), n + 1)
                for odd in range(2):
                    d = dst[:, odd:NH:2, :]
                    s = bank[out + odd][:, 0:D].rearrange("p (c n) -> p c n", c=2)
                    if n == 0:
                        link(e.tensor_copy(d, s))
                    else:
                        link(e.tensor_tensor(d, s, causalT[:].unsqueeze(1).broadcast_to([P, 2, P]), ALU.mult))
            idents = ident[:].unsqueeze(1).broadcast_to([P, NH, P])
            link(e.tensor_copy(X[:], idents))
            link(e.tensor_copy(XT[:], idents))
            every_tap = [(s, j) for s, n in enumerate(TAPS) for j in range(n)]
            per_level = -(-len(every_tap) // LEVELS)

            def convolve(first, last):
                for k in range(first, min(last, len(every_tap))):
                    s, j = every_tap[k]
                    at = LEAD - (TAPS[s] - 1) + j
                    for c in range(DC):
                        src, tap, dst = vpad[:, c, at:at + P], taps[s][:, c, j:j + 1], ms[:, s, c, :]
                        i = e.tensor_scalar(dst, src, tap, None, ALU.mult) if j == 0 else \
                            e.scalar_tensor_tensor(dst, src, tap, dst, ALU.mult, ALU.add)
                        i.then_inc(sem("ms_taps"), 1)
                    e.wait_ge(sem("ms_taps"), 2 * (k + 1))

            def quarter(level):
                link(e.tensor_tensor(BT[:, level % 2], AT[:], below[:, level, :].unsqueeze(1).broadcast_to([P, NH, P]), ALU.mult))

            quarter(0)
            for level in range(LEVELS):
                e.nop().then_inc(sem("B_masked"), 1)
                start = level * per_level
                convolve(start, start + 3)
                e.wait_ge(sem("BX_made"), level + 1)
                e.tensor_copy(flat(Y), bank[4][:]).then_inc(sem("BX_copied"), 1)
                if level + 1 < LEVELS:
                    quarter(level + 1)
                convolve(start + 3, start + per_level)
                e.wait_ge(sem("XBX_made"), level + 1)
                e.wait_ge(sem("XBXT_made"), level + 1)
                link(e.tensor_tensor(flat(X), flat(X), bank[1][:], ALU.subtract))
                link(e.tensor_tensor(flat(XT), flat(XT), bank[0][:], ALU.subtract))
                e.nop().then_inc(sem("X_updated"), 1)
            e.nop().then_inc(sem("ms_made"), 1)
            e.wait_ge(sem("u_made"), 1)
            e.tensor_copy(flat(u), bank[4][:, 0:D]).then_inc(sem("u_copied"), 1)
            e.wait_ge(sem("delta_made"), 1)
            link(e.tensor_copy(branch[:, 1].rearrange("p a b -> p (a b)"), bank[5][:, 0:D]))
            e.wait_ge(sem("ms_copied"), 1)
            b12 = branch[:].rearrange("p i h d -> p (i h) d")
            link(e.tensor_reduce(absmean[:].rearrange("p i h -> p (i h)"), b12, AX, ALU.add, apply_absolute_value=True))
            link(e.tensor_scalar(absmean[:], absmean[:], 1.0 / HW, None, ALU.mult))
            e.nop().then_inc(sem("means_made"), 1)
            e.wait_ge(sem("means_turned"), 1)
            e.tensor_copy(absT[:], bank[6][0:G, 0:P]).then_inc(sem("absT_copied"), 1)
            e.wait_ge(sem("logits_made"), 1)
            link(e.tensor_tensor(lg[:].rearrange("p h j -> p (h j)"), bank[0][:, 0:G], fb2[:], ALU.add))
            link(e.tensor_reduce(mx[:], lg[:], AX, ALU.max))
            e.tensor_tensor(lg[:], lg[:], mx[:].unsqueeze(2).broadcast_to([P, NH, 3]), ALU.subtract).then_inc(sem("lg_shifted"), 1)
            e.wait_ge(sem("wts_exp"), 1)
            link(e.tensor_reduce(den[:], wts[:], AX, ALU.add))
            link(e.reciprocal(inv[:], den[:]))
            link(e.tensor_tensor(wts[:], wts[:], inv[:].unsqueeze(2).broadcast_to([P, NH, 3]), ALU.mult))
            for j in range(3):
                ww = wts[:, :, j:j + 1].broadcast_to([P, NH, HW])
                if j == 0:
                    link(e.tensor_tensor(o[:], branch[:, j], ww, ALU.mult))
                else:
                    link(e.tensor_tensor(part[:], branch[:, j], ww, ALU.mult))
                    link(e.tensor_tensor(o[:], o[:], part[:], ALU.add))
            link(e.tensor_tensor(part[:], o[:], o[:], ALU.mult))
            link(e.tensor_reduce(oss[:], part[:], AX, ALU.add))
            e.tensor_scalar(oinv[:, 1, :], oss[:], 1.0 / HW, 1e-5, ALU.mult, ALU.add).then_inc(sem("o_squares"), 1)
            e.wait_ge(sem("o_roots"), 1)
            link(e.reciprocal(oinv[:, 1, :], oinv[:, 0, :]))
            link(e.tensor_tensor(o[:], o[:], oinv[:, 1, :].unsqueeze(2).broadcast_to([P, NH, HW]), ALU.mult))
            e.tensor_tensor(o[:], o[:], onorm[:].unsqueeze(1).broadcast_to([P, NH, HW]), ALU.mult).then_inc(sem("o_done"), 1)
            e.wait_ge(sem("o_turned"), 1)
            e.tensor_copy(flat(oT), bank[1][:, 0:D]).then_inc(sem("oT_copied"), 1)
            e.wait_ge(sem("out_made"), 1)
            e.tensor_tensor(x[:], x[:], bank[2][:, 0:D], ALU.add)

    m.end()


STEP = 256.0
MAGIC = 1.5 * 2.0 ** 23


def rounded_ffn(nc, st, name, w):
    m = Module(nc, name)
    sb, ps, sem = m.sb, m.ps, m.sem
    x, ident = st["x"], st["ident"]
    F = 1024
    FC = F // P
    scratch = norm_scratch(m, "ln")
    xn, xnT = sb("xn", [P, D]), sb("xnT", [P, DC, P])
    w1, w2 = sb("w1", [P, DC, F]), sb("w2", [P, FC, D])
    b1, b2 = sb("b1", [1, F]), sb("b2", [1, D])
    ones = sb("ones", [1, P])
    h, c, left, frac = sb("h", [P, F]), sb("c", [P, F]), sb("left", [P, 2, F]), sb("frac", [P, F])
    y, flag = sb("y", [P, 2, F]), sb("flag", [P, F])
    hT = sb("hT", [P, FC, P])
    out = sb("out", [P, D])
    p_x, p_o = ps("p_x"), ps("p_o")
    p_h = ps("p_h", [P, F])
    with nc.Block() as block:

        @block.sync
        def _(e):
            for t, src in ((w1, chunked(w["w1"])), (w2, chunked(w["w2"])), (b1, w["b1"]), (b2, w["b2"])):
                e.dma_start(t[:], src).then_inc(sem("weights"), 16)

        @block.gpsimd
        def _(e):
            e.memset(ones[:], 1.0).then_inc(sem("ones"), 1)

        @block.tensor
        def _(e):
            e.wait_ge(sem("ln_normed"), 1)
            turn_chunks(e, ident, p_x, xn).then_inc(sem("xn_turned"), 1)
            e.wait_ge(sem("xnT_copied"), 1)
            e.wait_ge(sem("weights"), 64)
            e.wait_ge(sem("ones"), 1)
            for fc in range(FC):
                f = slice(fc * P, (fc + 1) * P)
                for k in range(DC):
                    e.matmul(p_h[:, f], w1[:, k, f], xnT[:, k, :], start=k == 0, stop=False)
                i = e.matmul(p_h[:, f], b1[:, f], ones[:], start=False, stop=True)
            i.then_inc(sem("h_made"), 1)
            e.wait_ge(sem("h_done"), 1)
            for fc in range(FC):
                e.matmul(p_o[:, 0:D], hT[:, fc, :], w2[:, fc, :], start=fc == 0, stop=False)
            e.matmul(p_o[:, 0:D], ones[:], b2[:], start=False, stop=True).then_inc(sem("out_made"), 1)

        @block.scalar
        def _(e):
            norm_scalar(e, m, "ln", scratch)
            for k in range(2):
                e.wait_ge(sem("piece_ends"), k + 1)
                e.activation(y[:, k, :], left[:, k, :], ACT.Gelu).then_inc(sem("gelus"), 1)

        @block.vector
        def _(e):
            link = chain(e, sem("vector_chain"))
            norm_vector(e, m, link, "ln", scratch, x[:], xn[:])
            e.wait_ge(sem("xn_turned"), 1)
            e.tensor_copy(xnT[:].rearrange("p c n -> p (c n)"), p_x[:, 0:D]).then_inc(sem("xnT_copied"), 1)

            def rounded(dst, src):
                link(e.tensor_scalar(dst, src, STEP, MAGIC, ALU.mult, ALU.add))
                link(e.tensor_scalar(dst, dst, MAGIC, 1.0 / STEP, ALU.subtract, ALU.mult))

            e.wait_ge(sem("h_made"), 1)
            rounded(h[:], p_h[:])
            link(e.tensor_scalar(c[:], h[:], -4.0, 4.0, ALU.max, ALU.min))
            link(e.tensor_scalar(frac[:], c[:], 4.0, -63.0 / 128, ALU.mult, ALU.add))
            link(e.tensor_scalar(frac[:], frac[:], MAGIC, MAGIC, ALU.add, ALU.subtract))
            e.tensor_scalar(left[:, 0, :], frac[:], 0.25, None, ALU.mult).then_inc(sem("piece_ends"), 1)
            e.wait_ge(sem("piece_ends"), 1)
            e.tensor_scalar(left[:, 1, :], left[:, 0, :], 0.25, None, ALU.add).then_inc(sem("piece_ends"), 1)
            link(e.tensor_tensor(frac[:], c[:], left[:, 0, :], ALU.subtract))
            e.wait_ge(sem("gelus"), 2)
            link(e.tensor_tensor(y[:, 1, :], y[:, 1, :], y[:, 0, :], ALU.subtract))
            link(e.scalar_tensor_tensor(y[:, 1, :], frac[:], 4.0, y[:, 1, :], ALU.mult, ALU.mult))
            link(e.tensor_tensor(y[:, 0, :], y[:, 0, :], y[:, 1, :], ALU.add))
            link(e.scalar_tensor_tensor(flag[:], h[:], -4.0, y[:, 0, :], ALU.is_ge, ALU.mult))
            link(e.scalar_tensor_tensor(flag[:], h[:], 4.0, flag[:], ALU.is_le, ALU.mult))
            link(e.scalar_tensor_tensor(c[:], h[:], 4.0, h[:], ALU.is_gt, ALU.mult))
            link(e.tensor_tensor(c[:], c[:], flag[:], ALU.add))
            rounded(hT[:].rearrange("p c n -> p (c n)"), c[:])
            e.nop().then_inc(sem("h_done"), 1)
            e.wait_ge(sem("out_made"), 1)
            rounded(out[:], p_o[:, 0:D])
            e.tensor_tensor(x[:], x[:], out[:], ALU.add)

    m.end()


def window_attention(nc, st, name, w):
    m = Module(nc, name)
    sb, ps, sem = m.sb, m.ps, m.sem
    x, ident = st["x"], st["ident"]
    NH, HW = 4, 64
    scratch, scratch2 = norm_scratch(m, "ln"), norm_scratch(m, "ln2")
    xn, xa, xaT = sb("xn", [P, D]), sb("xa", [P, D]), sb("xaT", [P, DC, P])
    ln_w, ln_b = sb("ln_w", [P, D]), sb("ln_b", [P, D])
    wqkv, wo = sb("wqkv", [P, DC, 3 * D]), sb("wo", [P, DC, D])
    cos, sin = sb("cos", [P, HW]), sb("sin", [P, HW])
    mask = sb("mask", [P, P])
    qk = sb("qk", [P, 2 * NH, HW])
    turn, rot = sb("turn", [P, 2 * NH, HW]), sb("rot", [P, 2 * NH, HW])
    v = sb("v", [P, D])
    qkT = sb("qkT", [P, 4, P])
    s, top, low = sb("s", [P, NH, P]), sb("top", [P, NH]), sb("low", [P, NH])
    prob, probT = sb("prob", [P, NH, P]), sb("probT", [P, NH, P])
    total, inv = sb("total", [P, NH]), sb("inv", [P, NH])
    o, oT = sb("o", [P, NH, HW]), sb("oT", [P, DC, P])
    p_x, p_qk, p_v, p_t, p_o = (ps(n) for n in ("p_x", "p_qk", "p_v", "p_t", "p_o"))
    p_s = [ps(f"p_s{i}") for i in range(2)]
    loads = ((ln_w, w["ln_w"]), (ln_b, w["ln_b"]), (wqkv, chunked(w["wqkv"])), (wo, chunked(w["wo"])),
             (cos, w["cos"]), (sin, w["sin"]), (mask, w["mask"]))
    with nc.Block() as block:

        @block.sync
        def _(e):
            for t, src in loads:
                e.dma_start(t[:], src).then_inc(sem("weights"), 16)

        @block.tensor
        def _(e):
            e.wait_ge(sem("affine"), 1)
            turn_chunks(e, ident, p_x, xa).then_inc(sem("xa_turned"), 1)
            e.wait_ge(sem("xaT_copied"), 1)
            project_rows(e, p_qk[:], xaT, wqkv[:, :, 0:2 * D]).then_inc(sem("qk_made"), 1)
            project_rows(e, p_v[:, 0:D], xaT, wqkv[:, :, 2 * D:3 * D]).then_inc(sem("v_made"), 1)
            e.wait_ge(sem("rotated"), 1)
            turn_chunks(e, ident, p_t, rot[:].rearrange("p h d -> p (h d)"), 4).then_inc(sem("qk_turned"), 1)
            e.wait_ge(sem("qkT_copied"), 1)
            for h in range(NH):
                r = slice(HW * (h % 2), HW * (h % 2) + HW)
                i = e.matmul(p_s[h % 2][:, (h // 2) * P:(h // 2 + 1) * P], qkT[r, h // 2, :], qkT[r, 2 + h // 2, :],
                             start=True, stop=True)
            i.then_inc(sem("scored"), 1)
            e.wait_ge(sem("exped"), NH)
            for h in range(NH):
                i = e.transpose(p_x[:, h * P:(h + 1) * P], prob[:, h, :], ident[:])
            i.then_inc(sem("prob_turned"), 1)
            e.wait_ge(sem("probT_copied"), 1)
            e.wait_ge(sem("v_copied"), 1)
            for h in range(NH):
                i = e.matmul(p_o[:, h * HW:(h + 1) * HW], probT[:, h, :], v[:, h * HW:(h + 1) * HW], start=True, stop=True)
            i.then_inc(sem("valued"), 1)
            e.wait_ge(sem("o_done"), 1)
            turn_chunks(e, ident, p_t, o[:].rearrange("p h d -> p (h d)")).then_inc(sem("o_turned"), 1)
            e.wait_ge(sem("oT_copied"), 1)
            project_rows(e, p_v[:, 0:D], oT, wo).then_inc(sem("out_made"), 1)

        @block.scalar
        def _(e):
            norm_scalar(e, m, "ln", scratch)
            norm_scalar(e, m, "ln2", scratch2)
            e.wait_ge(sem("v_made"), 1)
            e.copy(v[:], p_v[:, 0:D]).then_inc(sem("v_copied"), 1)
            e.wait_ge(sem("low"), 1)
            for h in range(NH):
                e.activation(prob[:, h, :], s[:, h, :], ACT.Exp, bias=low[:, h:h + 1],
                             accum_out=total[:, h:h + 1]).then_inc(sem("exped"), 1)

        @block.vector
        def _(e):
            link = chain(e, sem("vector_chain"))
            norm_vector(e, m, link, "ln", scratch, x[:], xn[:])
            e.wait_ge(sem("ln_normed"), 1)
            norm_vector(e, m, link, "ln2", scratch2, xn[:], xa[:])
            e.wait_ge(sem("ln2_normed"), 1)
            e.wait_ge(sem("weights"), 16 * len(loads))
            link(e.tensor_tensor(xa[:], xa[:], ln_w[:], ALU.mult))
            e.tensor_tensor(xa[:], xa[:], ln_b[:], ALU.add).then_inc(sem("affine"), 1)
            e.wait_ge(sem("xa_turned"), 1)
            e.tensor_copy(xaT[:].rearrange("p c n -> p (c n)"), p_x[:, 0:D]).then_inc(sem("xaT_copied"), 1)
            e.wait_ge(sem("qk_made"), 1)
            link(e.tensor_copy(qk[:].rearrange("p h d -> p (h d)"), p_qk[:]))
            over = lambda t, a, b: t[:, a:b].unsqueeze(1).broadcast_to([P, 2 * NH, b - a])
            H = HW // 2
            link(e.tensor_tensor(turn[:, :, 0:H], qk[:, :, H:HW], over(sin, 0, H), ALU.mult))
            link(e.tensor_tensor(turn[:, :, H:HW], qk[:, :, 0:H], over(sin, H, HW), ALU.mult))
            link(e.tensor_tensor(rot[:], qk[:], over(cos, 0, HW), ALU.mult))
            e.tensor_tensor(rot[:], rot[:], turn[:], ALU.add).then_inc(sem("rotated"), 1)
            e.wait_ge(sem("qk_turned"), 1)
            e.tensor_copy(qkT[:].rearrange("p c n -> p (c n)"), p_t[:]).then_inc(sem("qkT_copied"), 1)
            e.wait_ge(sem("scored"), 1)
            for odd in range(2):
                link(e.scalar_tensor_tensor(s[:, odd:NH:2, :], p_s[odd][:, 0:D].rearrange("p (c n) -> p c n", c=2), float(HW) ** -0.5,
                                            mask[:].unsqueeze(1).broadcast_to([P, 2, P]), ALU.mult, ALU.add))
            link(e.tensor_reduce(top[:], s[:], AX, ALU.max))
            e.tensor_scalar(low[:], top[:], -1.0, None, ALU.mult).then_inc(sem("low"), 1)
            e.wait_ge(sem("prob_turned"), 1)
            e.tensor_copy(probT[:].rearrange("p h n -> p (h n)"), p_x[:]).then_inc(sem("probT_copied"), 1)
            e.wait_ge(sem("exped"), NH)
            link(e.reciprocal(inv[:], total[:]))
            e.wait_ge(sem("valued"), 1)
            e.tensor_tensor(o[:], p_o[:, 0:D].rearrange("p (h d) -> p h d", h=NH),
                            inv[:].unsqueeze(2).broadcast_to([P, NH, HW]), ALU.mult).then_inc(sem("o_done"), 1)
            e.wait_ge(sem("o_turned"), 1)
            e.tensor_copy(oT[:].rearrange("p c n -> p (c n)"), p_t[:, 0:D]).then_inc(sem("oT_copied"), 1)
            link(e.tensor_tensor(x[:], x[:], xn[:], ALU.add))
            e.wait_ge(sem("out_made"), 1)
            e.tensor_tensor(x[:], x[:], p_v[:, 0:D], ALU.add)

    m.end()


def nearest_expert(nc, st, name, w):
    m = Module(nc, name)
    sb, ps, sem = m.sb, m.ps, m.sem
    x, ident = st["x"], st["ident"]
    E, F, RING = 8, 1024, 4
    FC = F // P
    scratch, scratch2 = norm_scratch(m, "ln"), norm_scratch(m, "ln2")
    xn, xnT, xh, xhT = sb("xn", [P, D]), sb("xnT", [P, DC, P]), sb("xh", [P, D]), sb("xhT", [P, DC, P])
    cent = sb("cent", [P, DC, E])
    g, b = sb("g", [P, E, DC]), sb("b", [P, E, DC])
    b1, b2 = sb("b1", [P, E, FC]), sb("b2", [E, D])
    w1, w2 = sb("w1", [P, RING, DC, F]), sb("w2", [P, RING, FC, D])
    aff, best = sb("aff", [P, 2 * E]), sb("best", [P, 8])
    wanted, left, one = sb("wanted", [P, 8]), sb("left", [P, 2 * E]), sb("one", [P, E])
    alpha, weight, weightT = sb("alpha", [P, E]), sb("weight", [P, E]), sb("weightT", [E, P])
    xe = sb("xe", [P, 2, DC, P])
    h = sb("h", [P, 2, FC, P])
    p_x, p_g = ps("p_x"), ps("p_g")
    p_h = [ps(f"p_h{i}", [P, F]) for i in range(2)]
    p_y = [ps(f"p_y{i}") for i in range(2)]
    small = ((cent, chunked(w["cent"])), (g, w["g"]), (b, w["b"]), (b1, w["b1"]), (b2, w["b2"]))

    with nc.Block() as block:

        @block.sync
        def _(e):
            for t, src in small:
                e.dma_start(t[:], src).then_inc(sem("small_weights"), 16)
            for x_ in range(E):
                if x_ >= RING:
                    e.wait_ge(sem("y_made"), x_ - RING + 1)
                e.dma_start(w1[:, x_ % RING], chunked(w["w1"][x_])).then_inc(sem(f"expert_loaded_{x_ % RING}"), 16)
                e.dma_start(w2[:, x_ % RING], chunked(w["w2"][x_])).then_inc(sem(f"expert_loaded_{x_ % RING}"), 16)

        @block.tensor
        def _(e):
            e.wait_ge(sem("ln_normed"), 1)
            turn_chunks(e, ident, p_x, xn).then_inc(sem("xn_turned"), 1)
            e.wait_ge(sem("xnT_copied"), 1)
            e.wait_ge(sem("small_weights"), 16 * len(small))
            project_rows(e, p_g[:, 0:E], xnT, cent).then_inc(sem("aff_made"), 1)
            e.wait_ge(sem("ln2_normed"), 1)
            turn_chunks(e, ident, p_x, xh).then_inc(sem("xh_turned"), 1)

            def first(x_):
                e.wait_ge(sem(f"expert_loaded_{x_ % RING}"), 32 * (x_ // RING + 1))
                e.wait_ge(sem("xe_made"), x_ + 1)
                if x_ >= 2:
                    e.wait_ge(sem("h_low"), x_ - 1)
                    e.wait_ge(sem("h_high"), x_ - 1)
                project_turned(e, p_h[x_ % 2], w1[:, x_ % RING], xe[:, x_ % 2], FC).then_inc(sem("h_made"), 1)

            def second(x_):
                e.wait_ge(sem("h_low"), x_ + 1)
                e.wait_ge(sem("h_high"), x_ + 1)
                if x_ >= 2:
                    e.wait_ge(sem("y_added"), x_ - 1)
                project_rows(e, p_y[x_ % 2][:, 0:D], h[:, x_ % 2], w2[:, x_ % RING], FC).then_inc(sem("y_made"), 1)

            for n in range(E + 1):
                if n < E:
                    first(n)
                if n == 1:
                    e.wait_ge(sem("weighted"), 1)
                    e.transpose(p_x[0:E, 0:P], weight[:], ident[:]).then_inc(sem("weight_turned"), 1)
                    e.wait_ge(sem("weightT_copied"), 1)
                    e.matmul(p_g[:, 0:D], weightT[:], b2[:], start=True, stop=True).then_inc(sem("b2_made"), 1)
                if n >= 1:
                    second(n - 1)

        @block.gpsimd
        def _(e):
            for k in range(E):
                e.memset(aff[:, E + k:E + k + 1], -3.0e38 - k * 1e36).then_inc(sem("fillers"), 1)
            for k in range(8):
                e.memset(wanted[:, k:k + 1], -3.0e38 - k * 1e36).then_inc(sem("fillers"), 1)

        @block.scalar
        def _(e):
            norm_scalar(e, m, "ln", scratch)
            norm_scalar(e, m, "ln2", scratch2)
            e.wait_ge(sem("aff_copied"), 1)
            e.activation(alpha[:], aff[:, 0:E], ACT.Sigmoid).then_inc(sem("alpha_made"), 1)
            e.wait_ge(sem("small_weights"), 16 * len(small))
            for x_ in range(E):
                e.wait_ge(sem("h_made"), x_ + 1)
                if x_ >= 2:
                    e.wait_ge(sem("y_made"), x_ - 1)
                for fc in range(FC // 2):
                    i = e.activation(h[:, x_ % 2, fc, :], p_h[x_ % 2][:, fc * P:(fc + 1) * P], ACT.Relu, bias=b1[:, x_, fc:fc + 1])
                i.then_inc(sem("h_low"), 1)

        @block.vector
        def _(e):
            link = chain(e, sem("vector_chain"))
            norm_vector(e, m, link, "ln", scratch, x[:], xn[:])
            e.wait_ge(sem("xn_turned"), 1)
            e.tensor_copy(xnT[:].rearrange("p c n -> p (c n)"), p_x[:, 0:D]).then_inc(sem("xnT_copied"), 1)
            e.wait_ge(sem("ln_normed"), 1)
            norm_vector(e, m, link, "ln2", scratch2, xn[:], xh[:])
            e.wait_ge(sem("xh_turned"), 1)
            link(e.tensor_copy(xhT[:].rearrange("p c n -> p (c n)"), p_x[:, 0:D]))

            def affine(x_):
                if x_ >= 2:
                    e.wait_ge(sem("h_made"), x_ - 1)
                for c in range(DC):
                    i = e.tensor_scalar(xe[:, x_ % 2, c, :], xhT[:, c, :], g[:, x_, c:c + 1], b[:, x_, c:c + 1],
                                        ALU.mult, ALU.add)
                i.then_inc(sem("xe_made"), 1)

            def add_y(x_):
                e.wait_ge(sem("y_made"), x_ + 1)
                if x_:
                    e.wait_ge(sem("y_added"), x_)
                e.scalar_tensor_tensor(x[:], p_y[x_ % 2][:, 0:D], weight[:, x_:x_ + 1], x[:],
                                       ALU.mult, ALU.add).then_inc(sem("y_added"), 1)

            e.wait_ge(sem("small_weights"), 16 * len(small))
            affine(0)
            affine(1)
            e.wait_ge(sem("aff_made"), 1)
            e.wait_ge(sem("fillers"), 16)
            e.tensor_copy(aff[:, 0:E], p_g[:, 0:E]).then_inc(sem("aff_copied"), 1)
            e.wait_ge(sem("aff_copied"), 1)
            link(e.max(best[:], aff[:, 0:E]))
            link(e.tensor_copy(wanted[:, 0:1], best[:, 0:1]))
            link(e.match_replace(left[:], wanted[:], aff[:], 3.0e38))
            link(e.tensor_scalar(one[:], left[:, 0:E], 2.9e38, None, ALU.is_gt))
            e.wait_ge(sem("alpha_made"), 1)
            e.tensor_tensor(weight[:], one[:], alpha[:], ALU.mult).then_inc(sem("weighted"), 1)
            e.wait_ge(sem("weight_turned"), 1)
            e.tensor_copy(weightT[:], p_x[0:E, 0:P]).then_inc(sem("weightT_copied"), 1)
            link(e.tensor_tensor(x[:], x[:], xn[:], ALU.add))
            e.wait_ge(sem("b2_made"), 1)
            link(e.tensor_tensor(x[:], x[:], p_g[:, 0:D], ALU.add))
            for x_ in range(E):
                e.wait_ge(sem("h_made"), x_ + 1)
                if x_ >= 2:
                    e.wait_ge(sem("y_made"), x_ - 1)
                for fc in range(FC // 2, FC):
                    i = e.tensor_scalar(h[:, x_ % 2, fc, :], p_h[x_ % 2][:, fc * P:(fc + 1) * P], b1[:, x_, fc:fc + 1], 0.0,
                                        ALU.add, ALU.max)
                i.then_inc(sem("h_high"), 1)
                if x_ + 2 < E:
                    affine(x_ + 2)
                if x_ >= 1:
                    add_y(x_ - 1)
            add_y(E - 1)

    m.end()


def build(nc, a, modules=None):
    m = Module(nc, "net")
    st = {n: m.sb(n, shape) for n, shape in (("x", [P, D]), ("ident", [P, P]), ("stack_rows", [P, 2]))}
    with nc.Block() as block:
        @block.sync
        def _(e):
            e.dma_start(st["x"][:], a["x"]).then_inc(m.sem("loaded"), 16)
            e.dma_start(st["ident"][:], a["c_ident"]).then_inc(m.sem("loaded"), 16)
            e.dma_start(st["stack_rows"][:], a["c_stack_rows"]).then_inc(m.sem("loaded"), 16)
            e.wait_ge(m.sem("loaded"), 48)

    def L0_xattn():
        cross_attention(nc, st, "L0x", {"ctxT": a["ctxT"], "mask": a["mask_BxS2_ik0"], "wq": a["L0_xattn_q_w"],
                        "bq": a["L0_xattn_q_b"], "wk": a["L0_xattn_k_w"], "bk": a["L0_xattn_k_b"],
                        "wv": a["L0_xattn_v_w"], "bv": a["L0_xattn_v_b"]}, "int")

    def L1_xattn():
        cross_attention(nc, st, "L1x", {"ctxT": a["ctxT"], "mask": a["fside_SxS2_0"], "pad": a["fside_BxS2_0"],
                        "wq": a["L1_xattn_Wq"], "bq": a["L1_xattn_bq"], "wk": a["L1_xattn_Wk"],
                        "bk": a["L1_xattn_bk"], "wv": a["L1_xattn_Wv"], "bv": a["L1_xattn_bv"],
                        "wo": a["L1_xattn_Wo"], "bo": a["L1_xattn_bo"]}, "two")

    def L2_xattn():
        cross_attention(nc, st, "L2x", {"ctxT": a["ctxT"], "wq": a["L2_xattn_wq"], "bq": a["L2_xattn_bq"],
                        "wk": a["L2_xattn_wk"], "bk": a["L2_xattn_bk"], "wv": a["L2_xattn_wv"],
                        "bv": a["L2_xattn_bv"], "wo": a["L2_xattn_wo"], "bo": a["L2_xattn_bo"]}, None)

    def L3_xattn():
        cross_attention(nc, st, "L3x", {"ctxT": a["ctxT"], "mask": a["mask_Bx1x1xS2_fk0"], "wq": a["L3_xattn_Wq"],
                        "bq": a["L3_xattn_bq"], "wk": a["L3_xattn_Wk"], "bk": a["L3_xattn_bk"],
                        "wv": a["L3_xattn_Wv"], "bv": a["L3_xattn_bv"], "wo": a["L3_xattn_Wo"],
                        "bo": a["L3_xattn_bo"]}, "float")

    def L0_attn():
        one_head_attention(nc, st, "L0a", {"wq": a["L0_attn_Wq"], "bq": a["L0_attn_bq"], "wk": a["L0_attn_Wk"],
                           "bk": a["L0_attn_bk"], "wv": a["L0_attn_Wv"], "bv": a["L0_attn_bv"],
                           "mask": a["c_after"]}, "columns")

    def L2_attn():
        qkv = [a["L2_attn_W"][:, i * D:(i + 1) * D] for i in range(3)]
        one_head_attention(nc, st, "L2a", {"wq": qkv[0], "wk": qkv[1], "wv": qkv[2], "mask": a["c_upper"]}, "upper")

    def L0_ffn():
        token_choice_experts(nc, st, "L0f", {"wg": a["L0_ffn_Wg"], "bg": a["L0_ffn_bg"], "b12": a["L0_ffn_b12"],
                             "b3": a["L0_ffn_b3"], "w1": a["L0_ffn_w1"], "w2": a["L0_ffn_w2"], "w3": a["L0_ffn_w3"]})

    def L1_attn():
        w = {n: a[f"L1_attn_{n}"] for n in ("Wq", "Wk", "Wv", "Wb", "Wo", "short", "ms3", "ms15", "ms31", "mix")}
        w.update(mixer=a["L1_attn_channel_mixer_w"], fw1=a["L1_attn_fusion_w1"], fb1=a["L1_attn_fusion_b1"],
                 fw2=a["L1_attn_fusion_w2"], fb2=a["L1_attn_fusion_b2"], onorm=a["L1_attn_o_norm_w"],
                 below=a["c_below"], causalT=a["c_upper"])
        delta_rule_attention(nc, st, "L1a", w)

    def L1_ffn():
        top_two_experts(nc, st, "L1f", {"gate": a["L1_ffn_gate_w"], "w1": a["L1_ffn_w1"], "b1": a["L1_ffn_b1"],
                        "g1": a["L1_ffn_ln1_g"], "b1n": a["L1_ffn_ln1_b"], "w2": a["L1_ffn_w2"],
                        "b2": a["L1_ffn_b2"], "out_g": a["L1_ffn_ln_g"], "out_b": a["L1_ffn_ln_b"]})

    def L2_ffn():
        rounded_ffn(nc, st, "L2f", {n: a[f"L2_ffn_{n}"] for n in ("w1", "b1", "w2", "b2")})

    def L3_attn():
        window_attention(nc, st, "L3a", {"ln_w": a["L3_attn_ln_w"], "ln_b": a["L3_attn_ln_b"],
                         "wqkv": a["L3_attn_w_qkv"], "wo": a["L3_attn_w_out"], "cos": a["c_cos"],
                         "sin": a["c_sin"], "mask": a["c_window"]})

    def L3_ffn():
        nearest_expert(nc, st, "L3f", {"cent": a["L3_ffn_centroids"], "g": a["L3_ffn_ln_g"], "b": a["L3_ffn_ln_b"],
                       "w1": a["L3_ffn_w1"], "b1": a["L3_ffn_b1"], "w2": a["L3_ffn_w2"], "b2": a["L3_ffn_b2"]})

    every = {"L0_xattn": L0_xattn, "L0_attn": L0_attn, "L0_ffn": L0_ffn,
             "L1_xattn": L1_xattn, "L1_attn": L1_attn, "L1_ffn": L1_ffn,
             "L2_xattn": L2_xattn, "L2_attn": L2_attn, "L2_ffn": L2_ffn,
             "L3_xattn": L3_xattn, "L3_attn": L3_attn, "L3_ffn": L3_ffn}
    for n in modules or list(every):
        every[n]()
    with nc.Block() as block:
        @block.sync
        def _(e):
            e.dma_start(a["out"], st["x"][:]).then_inc(m.sem("stored"), 16)
            e.wait_ge(m.sem("stored"), 16)
    m.end()


def lay_out(inputs):
    a = {n: np.asarray(v) for n, v in inputs.items()}
    col = lambda v: np.ascontiguousarray(v.reshape(-1, P).T)
    row = lambda v: np.ascontiguousarray(np.broadcast_to(v.reshape(1, -1), (P, v.size)))
    T = lambda v: np.ascontiguousarray(np.swapaxes(v, -1, -2))
    out = {"x": a["x"][0], "ctxT": T(a["ctx_1024"][0])}
    out["mask_BxS2_ik0"] = a["mask_BxS2_ik0"]
    out["mask_Bx1x1xS2_fk0"] = a["mask_Bx1x1xS2_fk0"].reshape(1, NKEYS)
    out["fside_SxS2_0"], out["fside_BxS2_0"] = a["fside_SxS2_0"], a["fside_BxS2_0"]
    for n in ("L0_xattn_q_w", "L0_xattn_k_w", "L0_xattn_v_w"):
        out[n] = T(a[n])
    for n in ("L1_xattn_Wq", "L1_xattn_Wk", "L1_xattn_Wv", "L1_xattn_Wo", "L2_xattn_wq", "L2_xattn_wk",
              "L2_xattn_wv", "L2_xattn_wo", "L3_xattn_Wq", "L3_xattn_Wk", "L3_xattn_Wv", "L3_xattn_Wo"):
        out[n] = a[n]
    for n in ("L0_xattn_k_b", "L1_xattn_bk", "L2_xattn_bk", "L3_xattn_bk"):
        out[n] = col(a[n])
    for n in ("L0_xattn_q_b", "L1_xattn_bq", "L2_xattn_bq", "L3_xattn_bq"):
        out[n] = np.tile(a[n].reshape(HX // 2, 2 * HD).T, (3, 1))
    for n in ("L0_xattn_v_b", "L1_xattn_bv", "L1_xattn_bo", "L2_xattn_bv", "L2_xattn_bo", "L3_xattn_bv",
              "L3_xattn_bo"):
        out[n] = row(a[n])
    for n in ("L0_attn_Wq", "L0_attn_Wk", "L0_attn_Wv", "L3_attn_w_qkv", "L3_attn_w_out", "L3_ffn_centroids",
              "L3_ffn_w1", "L3_ffn_w2"):
        out[n] = T(a[n])
    for n in ("L0_ffn_Wg", "L0_ffn_w1", "L0_ffn_w2", "L0_ffn_w3", "L0_ffn_b3", "L1_attn_Wq", "L1_attn_Wk",
              "L1_attn_Wv", "L1_attn_Wb", "L1_attn_Wo", "L1_attn_channel_mixer_w", "L1_attn_fusion_w1",
              "L1_attn_fusion_w2", "L1_ffn_gate_w", "L1_ffn_w1", "L1_ffn_w2", "L1_ffn_b2", "L2_attn_W",
              "L2_ffn_w1", "L2_ffn_w2", "L3_ffn_b2"):
        out[n] = a[n]
    for n in ("L0_attn_bq", "L0_attn_bk", "L1_attn_fusion_b1"):
        out[n] = col(a[n])
    for n in ("L0_attn_bv", "L1_attn_fusion_b2", "L1_attn_o_norm_w", "L1_ffn_ln_g", "L1_ffn_ln_b",
              "L3_attn_ln_w", "L3_attn_ln_b"):
        out[n] = row(a[n])
    per_expert = lambda v: v.reshape(v.shape[0], -1, P).transpose(2, 0, 1)
    for n in ("L1_ffn_ln1_g", "L1_ffn_ln1_b", "L3_ffn_ln_g", "L3_ffn_ln_b", "L3_ffn_b1"):
        out[n] = per_expert(a[n])
    channels = lambda v: v.reshape(DC, P, -1).transpose(1, 0, 2)
    out["L1_attn_short"] = np.stack([channels(a[f"L1_attn_conv_{n}_w"]) for n in "qkv"], axis=1)
    for n in (3, 15, 31):
        out[f"L1_attn_ms{n}"] = channels(a[f"L1_attn_ms_w{n}"])
    mix = a["L1_attn_kernel_mix_w"].reshape(3, 64, 64).transpose(1, 0, 2)
    out["L1_attn_mix"] = np.zeros((P, 2, 3, 64), np.float32)
    out["L1_attn_mix"][:64, 0], out["L1_attn_mix"][64:, 1] = mix, mix
    out["L0_ffn_bg"] = a["L0_ffn_bg"].reshape(16, 1)
    out["L0_ffn_b12"] = np.broadcast_to(np.stack([a["L0_ffn_b1"][:, 0], a["L0_ffn_b2"][:, 0]])[None], (P, 2, 16))
    out["L1_ffn_b1"] = a["L1_ffn_b1"][None]
    out["L2_ffn_b1"], out["L2_ffn_b2"] = a["L2_ffn_b1"][None], a["L2_ffn_b2"][None]
    i = np.arange(P)
    out["c_after"] = np.where(i[None, :] >= i[:, None], 0.0, -BIG).astype(np.float32)
    out["c_upper"] = (i[None, :] >= i[:, None]).astype(np.float32)
    gap = i[:, None] - i[None, :]
    out["c_window"] = np.where((gap >= 0) & (gap < 32), 0.0, -BIG).astype(np.float32)
    out["c_below"] = np.stack([((i[None, :] // (2 * s) == i[:, None] // (2 * s)) & (i[None, :] % (2 * s) >= s)
                                & (i[:, None] % (2 * s) < s)) for s in (1, 2, 4, 8, 16, 32, 64)],
                              axis=1).astype(np.float32)
    inv = (1.0 / 10000.0 ** (np.arange(0, 64, 2, dtype=np.float32) / 64)).astype(np.float32)
    angle = i.astype(np.float32)[:, None] * np.concatenate([inv, inv])[None, :]
    out["c_cos"] = np.cos(angle).astype(np.float32)
    out["c_sin"] = (np.sin(angle) * np.repeat([-1.0, 1.0], 32)).astype(np.float32)
    out["c_ident"] = np.eye(P, dtype=np.float32)
    out["c_stack_rows"] = np.tile(np.repeat(np.eye(2, dtype=np.float32), HD, axis=0), (P // (2 * HD), 1))
    return {n: np.ascontiguousarray(v) for n, v in out.items()}


def kernel(**inputs):
    import concourse.bacc as bacc
    from concourse.bass_utils import run_bass_kernel_spmd

    nc = bacc.Bacc("TRN2", target_bir_lowering=False, num_devices=1)
    arrays = lay_out(inputs)
    a = {n: nc.dram_tensor(f"in_{n}", list(v.shape), mybir.dt.from_np(v.dtype), kind="ExternalInput").ap()
         for n, v in arrays.items()}
    a["out"] = nc.dram_tensor("out_x", [P, D], F32, kind="ExternalOutput").ap()
    build(nc, a)
    r = run_bass_kernel_spmd(nc, [{f"in_{n}": v for n, v in arrays.items()}], core_ids=[0])
    return r.results[0]["out_x"].reshape(1, P, D)
```
